# Optimizing a Trainium2 kernel written in Bass

```python
import numpy as np
import jax
import jax.numpy as jnp

def _softmax(x, axis=-1):
    return jax.nn.softmax(x, axis=axis)

def _gelu(x):
    return jax.nn.gelu(x, approximate=True)

def _silu(x):
    return jax.nn.silu(x)

def _sigmoid(x):
    return jax.nn.sigmoid(x)

def _layernorm(x, axis=-1, eps=1e-05):
    m = jnp.mean(x, axis=axis, keepdims=True)
    v = jnp.var(x, axis=axis, keepdims=True)
    return (x - m) / jnp.sqrt(v + eps)

def _scatter_add(tgt, idx, src, axis=0):
    return tgt.at[idx].add(src)

def _segment_sum(src, seg, n):
    return jax.ops.segment_sum(src, seg, n)
kernel_name = 'mk_gnn_ffn_d1_gnn_r8_9b589e'

def setup_inputs(seed: int=0):
    np.random.seed(seed)
    _w = jnp.asarray

    def _rec_inputs():
        import jax
        import jax.numpy as jnp
        _gk = jax.random.key(seed)
        x = -0.000202 + 1 * jax.random.normal(jax.random.fold_in(_gk, 1), (6250, 256), jnp.float32)
        src = jax.random.randint(jax.random.fold_in(_gk, 2), (200000,), 0, 6250, jnp.int32)
        dst = jax.random.randint(jax.random.fold_in(_gk, 3), (200000,), 0, 6250, jnp.int32)
        _o = jnp.argsort(dst, stable=True)
        src = src[_o]
        dst = dst[_o]
        edge_attr_4 = 0.00121237 + 1.00026 * jax.random.normal(jax.random.fold_in(_gk, 12), (200000, 4), jnp.float32)
        edge_attr_8 = jax.random.uniform(jax.random.fold_in(_gk, 13), (200000, 8), jnp.float32, 0.0, 1)
        node_vec1 = jax.random.uniform(jax.random.fold_in(_gk, 14), (6250, 1), jnp.float32, 0.0, 1)
        return (x, src, dst, edge_attr_4, edge_attr_8, node_vec1)
    x, src, dst, edge_attr_4, edge_attr_8, node_vec1 = _rec_inputs()

    def _L0_gnn_setup():
        import jax, jax.numpy as jnp
        import numpy as np
        N = 3125
        E = 50000
        MUL = 64
        NB = 8
        RN = 64
        NUM_NEIGH = 16.0
        INV_SQRT3 = 1.0 / np.sqrt(3.0)

        def _forward(node_input, node_attr, edge_attr, edge_length_embedded, W_sc0, W_sc1, W_lin1_0, W_lin1_1, fc_w0, fc_w1, W_lin2_0, W_lin2_1, edge_src, edge_dst):
            Nn = node_input.shape[0]
            z = node_attr
            x0 = node_input[:, :MUL]
            x1 = node_input[:, MUL:].reshape(Nn, MUL, 3)
            inv_m = 1.0 / np.sqrt(MUL)
            s0 = x0 @ W_sc0 * z * inv_m
            s1 = jnp.einsum('nuc,uv->nvc', x1, W_sc1) * z[:, :, None] * inv_m
            h0 = x0 @ W_lin1_0 * z * inv_m
            h1 = jnp.einsum('nuc,uv->nvc', x1, W_lin1_1) * z[:, :, None] * inv_m
            hid = jax.nn.silu(edge_length_embedded @ fc_w0 / np.sqrt(NB))
            w = hid @ fc_w1 / np.sqrt(RN)
            wA, wB, wC, wD = (w[:, :MUL], w[:, MUL:2 * MUL], w[:, 2 * MUL:3 * MUL], w[:, 3 * MUL:])
            xs0 = h0[edge_src]
            xs1 = h1[edge_src]
            sh0 = edge_attr[:, :1]
            sh1 = edge_attr[:, 1:4]
            midA = wA * xs0 * sh0
            midD = wD * jnp.einsum('euc,ec->eu', xs1, sh1) * INV_SQRT3
            midB = (wB * xs0)[:, :, None] * sh1[:, None, :]
            midC = wC[:, :, None] * xs1 * sh0[:, None, :]
            mid0 = jnp.concatenate([midA, midD], axis=1)
            mid1 = jnp.concatenate([midB, midC], axis=1)
            inv_nb = 1.0 / np.sqrt(NUM_NEIGH)
            y0 = jax.ops.segment_sum(mid0, edge_dst, num_segments=Nn) * inv_nb
            y1 = jax.ops.segment_sum(mid1.reshape(mid1.shape[0], -1), edge_dst, num_segments=Nn).reshape(Nn, 2 * MUL, 3) * inv_nb
            inv_2m = 1.0 / np.sqrt(2 * MUL)
            o0 = y0 @ W_lin2_0 * z * inv_2m
            o1 = jnp.einsum('nuc,uv->nvc', y1, W_lin2_1) * z[:, :, None] * inv_2m
            c_s = np.float32(np.sin(np.pi / 8.0))
            c_x = np.float32(np.cos(np.pi / 8.0))
            out0 = c_s * s0 + c_x * o0
            out1 = c_s * s1 + c_x * o1
            return jnp.concatenate([out0, out1.reshape(Nn, 3 * MUL)], axis=1)
        key = jax.random.key(seed)
        ks = jax.random.split(key, 14)
        f32 = jnp.float32
        return {'node_input': jax.random.normal(ks[0], (N, 4 * MUL), f32), 'node_attr': jnp.ones((N, 1), f32), 'edge_src': jax.random.randint(ks[1], (E,), 0, N, dtype=jnp.int32), 'edge_dst': jax.random.randint(ks[2], (E,), 0, N, dtype=jnp.int32), 'edge_attr': jax.random.normal(ks[3], (E, 4), f32), 'edge_length_embedded': jax.random.uniform(ks[4], (E, NB), f32), 'W_sc0': jax.random.normal(ks[5], (MUL, MUL), f32), 'W_sc1': jax.random.normal(ks[6], (MUL, MUL), f32), 'W_lin1_0': jax.random.normal(ks[7], (MUL, MUL), f32), 'W_lin1_1': jax.random.normal(ks[8], (MUL, MUL), f32), 'fc_w0': jax.random.normal(ks[9], (NB, RN), f32), 'fc_w1': jax.random.normal(ks[10], (RN, 4 * MUL), f32), 'W_lin2_0': jax.random.normal(ks[11], (2 * MUL, MUL), f32), 'W_lin2_1': jax.random.normal(ks[12], (2 * MUL, MUL), f32)}
    _L0_gnn_all = _L0_gnn_setup()
    _L0_gnn_in = {k: v for k, v in _L0_gnn_all.items() if k in ('W_sc0', 'W_sc1', 'W_lin1_0', 'W_lin1_1', 'fc_w0', 'fc_w1', 'W_lin2_0', 'W_lin2_1')}
    del _L0_gnn_all

    def _L0_ffn_setup():
        import jax, jax.numpy as jnp
        import numpy as np
        NUM_EXPERTS = 8
        TOP_K = 2
        B, S, D = (8, 1024, 256)

        def _moe(tokens, router_w, w1, b1, w2, b2):
            N = tokens.shape[0]
            E = router_w.shape[0]
            logits = tokens.astype(jnp.float32) @ router_w.astype(jnp.float32).T
            probs = jax.nn.softmax(logits, axis=-1)
            rw, re = jax.lax.top_k(probs, TOP_K)
            if TOP_K > 1:
                rw = rw / jnp.maximum(rw.sum(-1, keepdims=True), 1e-12)
            rw = rw.astype(tokens.dtype)
            combine = jnp.zeros((N, E), tokens.dtype).at[jnp.arange(N)[:, None], re].set(rw)
            out = tokens
            for e in range(E):
                h = jax.nn.gelu(tokens @ w1[e] + b1[e], approximate=False)
                y = h @ w2[e] + b2[e]
                out = out + combine[:, e:e + 1] * y
            return out
        key = jax.random.key(seed)
        ks = jax.random.split(key, 4)
        scale = 1.0 / np.sqrt(D).astype(np.float32)
        return {'input_embeddings': jax.random.normal(ks[0], (B, S, D), jnp.float32), 'router_w': jax.random.normal(ks[1], (NUM_EXPERTS, D), jnp.float32) * scale, 'w1': jax.random.normal(ks[2], (NUM_EXPERTS, D, D), jnp.float32) * scale, 'b1': jnp.zeros((NUM_EXPERTS, D), jnp.float32), 'w2': jax.random.normal(ks[3], (NUM_EXPERTS, D, D), jnp.float32) * scale, 'b2': jnp.zeros((NUM_EXPERTS, D), jnp.float32)}
    _L0_ffn_all = _L0_ffn_setup()
    _L0_ffn_in = {k: v for k, v in _L0_ffn_all.items() if k in ('router_w', 'w1', 'b1', 'w2', 'b2')}
    del _L0_ffn_all
    return {'x': x, 'src': src, 'dst': dst, 'edge_attr_4': edge_attr_4, 'edge_attr_8': edge_attr_8, 'node_vec1': node_vec1, 'L0_gnn_W_sc0': _L0_gnn_in['W_sc0'], 'L0_gnn_W_sc1': _L0_gnn_in['W_sc1'], 'L0_gnn_W_lin1_0': _L0_gnn_in['W_lin1_0'], 'L0_gnn_W_lin1_1': _L0_gnn_in['W_lin1_1'], 'L0_gnn_fc_w0': _L0_gnn_in['fc_w0'], 'L0_gnn_fc_w1': _L0_gnn_in['fc_w1'], 'L0_gnn_W_lin2_0': _L0_gnn_in['W_lin2_0'], 'L0_gnn_W_lin2_1': _L0_gnn_in['W_lin2_1'], 'L0_ffn_router_w': _L0_ffn_in['router_w'], 'L0_ffn_w1': _L0_ffn_in['w1'], 'L0_ffn_b1': _L0_ffn_in['b1'], 'L0_ffn_w2': _L0_ffn_in['w2'], 'L0_ffn_b2': _L0_ffn_in['b2']}

def reference(x, src, dst, edge_attr_4, edge_attr_8, node_vec1, L0_gnn_W_sc0, L0_gnn_W_sc1, L0_gnn_W_lin1_0, L0_gnn_W_lin1_1, L0_gnn_fc_w0, L0_gnn_fc_w1, L0_gnn_W_lin2_0, L0_gnn_W_lin2_1, L0_ffn_router_w, L0_ffn_w1, L0_ffn_b1, L0_ffn_w2, L0_ffn_b2):
    import jax
    import jax.numpy as jnp

    def _L0_gnn_ref(node_input, node_attr, edge_src, edge_dst, edge_attr, edge_length_embedded, W_sc0, W_sc1, W_lin1_0, W_lin1_1, fc_w0, fc_w1, W_lin2_0, W_lin2_1):
        import jax, jax.numpy as jnp
        import numpy as np
        N = 3125
        E = 50000
        MUL = 64
        NB = 8
        RN = 64
        NUM_NEIGH = 16.0
        INV_SQRT3 = 1.0 / np.sqrt(3.0)

        def _forward(node_input, node_attr, edge_attr, edge_length_embedded, W_sc0, W_sc1, W_lin1_0, W_lin1_1, fc_w0, fc_w1, W_lin2_0, W_lin2_1, edge_src, edge_dst):
            Nn = node_input.shape[0]
            z = node_attr
            x0 = node_input[:, :MUL]
            x1 = node_input[:, MUL:].reshape(Nn, MUL, 3)
            inv_m = 1.0 / np.sqrt(MUL)
            s0 = x0 @ W_sc0 * z * inv_m
            s1 = jnp.einsum('nuc,uv->nvc', x1, W_sc1) * z[:, :, None] * inv_m
            h0 = x0 @ W_lin1_0 * z * inv_m
            h1 = jnp.einsum('nuc,uv->nvc', x1, W_lin1_1) * z[:, :, None] * inv_m
            hid = jax.nn.silu(edge_length_embedded @ fc_w0 / np.sqrt(NB))
            w = hid @ fc_w1 / np.sqrt(RN)
            wA, wB, wC, wD = (w[:, :MUL], w[:, MUL:2 * MUL], w[:, 2 * MUL:3 * MUL], w[:, 3 * MUL:])
            xs0 = h0[edge_src]
            xs1 = h1[edge_src]
            sh0 = edge_attr[:, :1]
            sh1 = edge_attr[:, 1:4]
            midA = wA * xs0 * sh0
            midD = wD * jnp.einsum('euc,ec->eu', xs1, sh1) * INV_SQRT3
            midB = (wB * xs0)[:, :, None] * sh1[:, None, :]
            midC = wC[:, :, None] * xs1 * sh0[:, None, :]
            mid0 = jnp.concatenate([midA, midD], axis=1)
            mid1 = jnp.concatenate([midB, midC], axis=1)
            inv_nb = 1.0 / np.sqrt(NUM_NEIGH)
            y0 = jax.ops.segment_sum(mid0, edge_dst, num_segments=Nn) * inv_nb
            y1 = jax.ops.segment_sum(mid1.reshape(mid1.shape[0], -1), edge_dst, num_segments=Nn).reshape(Nn, 2 * MUL, 3) * inv_nb
            inv_2m = 1.0 / np.sqrt(2 * MUL)
            o0 = y0 @ W_lin2_0 * z * inv_2m
            o1 = jnp.einsum('nuc,uv->nvc', y1, W_lin2_1) * z[:, :, None] * inv_2m
            c_s = np.float32(np.sin(np.pi / 8.0))
            c_x = np.float32(np.cos(np.pi / 8.0))
            out0 = c_s * s0 + c_x * o0
            out1 = c_s * s1 + c_x * o1
            return jnp.concatenate([out0, out1.reshape(Nn, 3 * MUL)], axis=1)
        return _forward(node_input, node_attr, edge_attr, edge_length_embedded, W_sc0, W_sc1, W_lin1_0, W_lin1_1, fc_w0, fc_w1, W_lin2_0, W_lin2_1, edge_src, edge_dst)

    def _L0_ffn_ref(input_embeddings, router_w, w1, b1, w2, b2):
        import jax, jax.numpy as jnp
        import numpy as np
        NUM_EXPERTS = 8
        TOP_K = 2
        B, S, D = (8, 1024, 256)

        def _moe(tokens, router_w, w1, b1, w2, b2):
            N = tokens.shape[0]
            E = router_w.shape[0]
            logits = tokens.astype(jnp.float32) @ router_w.astype(jnp.float32).T
            probs = jax.nn.softmax(logits, axis=-1)
            rw, re = jax.lax.top_k(probs, TOP_K)
            if TOP_K > 1:
                rw = rw / jnp.maximum(rw.sum(-1, keepdims=True), 1e-12)
            rw = rw.astype(tokens.dtype)
            combine = jnp.zeros((N, E), tokens.dtype).at[jnp.arange(N)[:, None], re].set(rw)
            out = tokens
            for e in range(E):
                h = jax.nn.gelu(tokens @ w1[e] + b1[e], approximate=False)
                y = h @ w2[e] + b2[e]
                out = out + combine[:, e:e + 1] * y
            return out
        b, s, d = input_embeddings.shape
        tokens = input_embeddings.reshape(b * s, d)
        return _moe(tokens, router_w, w1, b1, w2, b2).reshape(b, s, d)
    x = x + _L0_gnn_ref(_layernorm(x, axis=-1), node_vec1, src, dst, edge_attr_4, edge_attr_8, L0_gnn_W_sc0, L0_gnn_W_sc1, L0_gnn_W_lin1_0, L0_gnn_W_lin1_1, L0_gnn_fc_w0, L0_gnn_fc_w1, L0_gnn_W_lin2_0, L0_gnn_W_lin2_1)
    x = x + _L0_ffn_ref(_layernorm(x, axis=-1)[None], L0_ffn_router_w, L0_ffn_w1, L0_ffn_b1, L0_ffn_w2, L0_ffn_b2)[0]
    return x

_drawn_inputs = setup_inputs


def setup_inputs(seed=0):
    import zlib

    import numpy as np

    out = dict(_drawn_inputs(seed))
    spreads = {'L0_ffn_b1': (0.0, 0.329), 'L0_ffn_b2': (0.0, 0.1)}
    factors = {}
    for name, (base, spread) in spreads.items():
        noise = np.random.default_rng([zlib.crc32(name.encode()), seed]).standard_normal(out[name].shape)
        drawn = base * np.exp(spread * noise) if base else spread * noise
        out[name] = jnp.asarray(drawn.astype(out[name].dtype))
    for name, factor in factors.items():
        out[name] = (out[name] * factor).astype(out[name].dtype)
    return out
```

```python
from contextlib import ExitStack

import numpy as np

import concourse.bass as bass
from concourse import mybir

F32 = mybir.dt.float32
I32 = mybir.dt.int32
U32 = mybir.dt.uint32
ALU = mybir.AluOpType
ACT = mybir.ActivationFunctionType
AX = mybir.AxisListType

P = 128
N, E = 6250, 200000
MUL, NB, RN = 64, 8, 64
D = 4 * MUL
Y = 2 * D
NT = -(-N // P)
NPAD = NT * P
SUBS, QS = 4, 4
WIN = QS * P
GROUP = SUBS * WIN
GT = SUBS * QS
NG = -(-E // GROUP)
EPAD = NG * GROUP
RANKS = P // SUBS
NE, TOPK = 8, 2
CH = 512
EPS = 1e-5
SKIP = 1.0e6

C_S = float(np.float32(np.sin(np.pi / 8.0)))
C_X = float(np.float32(np.cos(np.pi / 8.0)))
INV_M = 1.0 / np.sqrt(MUL)
OUT_SCALE = float(C_X / np.sqrt(2 * MUL) / np.sqrt(16.0) / np.sqrt(RN))
INV_SQRT3 = float(1.0 / np.sqrt(3.0))


def since(eng, sem, value):
    if not isinstance(value, int) or value > 0:
        eng.wait_ge(sem, value)


def in_pairs(eng, count, body):
    body(0, 0, 0)
    body(1, 1, 0)
    with eng.Fori(1, count // 2) as i:
        body(2 * i, 0, i)
        body(2 * i + 1, 1, i)
    if count % 2:
        body(count - 1, 0, count // 2)


class Chain:

    def __init__(self, eng, sem):
        self.eng, self.sem, self.count = eng, sem, 0

    def then(self, ins):
        self.count += 1
        ins.then_inc(self.sem, 1)
        self.eng.wait_ge(self.sem, self.count)


def gnn_moe(nc, x, z, src, dst, dst_nat, firsts, sh, e8, w_sc0, w_sc1, w_l10, w_l11, fc0, fc1, w_l20, w_l21,
            router_t, w1, b1, w2, b2, out):
    h_table = nc.dram_tensor("h_table", (NPAD, D), F32, kind="Internal").ap()
    y_sums = nc.dram_tensor("y_sums", (NPAD, Y), F32, kind="Internal").ap()
    comb_rows = nc.dram_tensor("comb_rows", (NE, NPAD), F32, kind="Internal").ap()

    with ExitStack() as whole:
        def sb(name, shape, dt=F32, ctx=whole):
            return ctx.enter_context(nc.sbuf_tensor(name, shape, dt))

        windows = ExitStack()
        X = sb("X", [P, NT, D])
        zcol = sb("zcol", [P, NT])
        ident = sb("ident", [P, P])
        ones = sb("ones", [P, P])
        mean = sb("mean", [P, NT])
        rstd = sb("rstd", [P, NT])
        eps_col = sb("eps_col", [P, 1])
        riota = sb("riota", [P, SUBS, RANKS], ctx=windows)
        neg_base = sb("neg_base", [P, NG, SUBS], ctx=windows)
        ncol = sb("ncol", [P, NG], ctx=windows)
        neg_ncol = sb("neg_ncol", [P, NG], ctx=windows)
        row_index = sb("row_index", [P, NG], ctx=windows)
        rank = sb("rank", [P, NG * GT], ctx=windows)
        dst_i = sb("dst_i", [P, NG * GT], I32, ctx=windows)
        flag = sb("flag", [1, 1], I32, windows)

        def stats_to_rstd(dve, st, tmp, chain, sqrt_in, sqrt_out):
            m1, q1, m2, q2 = st[:, :, 1], st[:, :, 2], st[:, :, 4], st[:, :, 5]
            chain.then(dve.tensor_tensor(mean[:, :], m1, m2, ALU.add))
            chain.then(dve.tensor_tensor(tmp[:, :], m1, m2, ALU.subtract))
            chain.then(dve.tensor_scalar(mean[:, :], mean[:, :], 0.5, None, ALU.mult))
            chain.then(dve.scalar_tensor_tensor(tmp[:, :], tmp[:, :], D / 4.0, tmp[:, :], ALU.mult, ALU.mult))
            chain.then(dve.tensor_tensor(tmp[:, :], tmp[:, :], q1, ALU.add))
            dve.tensor_tensor(tmp[:, :], tmp[:, :], q2, ALU.add).then_inc(sqrt_in, 1)
            dve.wait_ge(sqrt_out, 1)
            chain.then(dve.reciprocal(rstd[:, :], rstd[:, :]))

        with ExitStack() as c1:
            def s1(name, shape, dt=F32):
                return sb(name, shape, dt, c1)

            def sem(name):
                return c1.enter_context(nc.semaphore(name))

            CHUNKS, PER = 7, NT // 7
            st = s1("st", [P, NT, 6])
            tmp = s1("tmp", [P, NT])
            wlin = s1("wlin", [P, 2, 2 * P])
            xn = [s1(f"xn{u}", [P, 4, MUL]) for u in range(2)]
            xnT = [s1(f"xnT{u}", [P, 2 * P]) for u in range(2)]
            hrow = [s1(f"hrow{u}", [P, 2, P]) for u in range(2)]
            z_h = s1("z_h", [P, NT])
            z_s = s1("z_s", [P, NT])
            dst_a = s1("dst_a", [NG, GROUP + 1], I32)
            diff = s1("diff", [NG, GROUP])
            base_i = s1("base_i", [P, 2, SUBS], I32)
            base_f = s1("base_f", [P, 2, SUBS])
            bad = s1("bad", [P, 4])
            diag = s1("diag", [P, NG, SUBS])
            spread = s1("spread", [P, 2, SUBS, RANKS])
            rcol = s1("rcol", [P, 1])
            next_col = s1("next_col", [P, NG])
            bad_f = s1("bad_f", [1, 1])

            tps = [c1.enter_context(nc.psum_tensor(f"tps{u}", [P, 512], F32)) for u in range(2)]
            lin_ps, sc_ps = ([c1.enter_context(nc.psum_tensor(f"{name}{u}", [P, 512], F32)) for u in range(2)] for name in ("lin_ps", "sc_ps"))
            base_ps = c1.enter_context(nc.psum_tensor("base_ps", [P, 512], F32))
            col_ps = c1.enter_context(nc.psum_tensor("col_ps", [P, 512], F32))

            x_in = [sem(f"x_in{c}") for c in range(CHUNKS)]
            w_in, z_in, dst_in = sem("w_in"), sem("z_in"), sem("dst_in")
            w_zero, pool_const = sem("w_zero"), sem("pool_const")
            pool_step = sem("pool_step")
            dve_step, var_ready, std_ready = sem("dve_step"), sem("var_ready"), sem("std_ready")
            const_ready, z_ready = sem("const_ready"), sem("z_ready")
            xn_ready, tr_ready, xnT_ready, lin_ready = sem("xn_ready"), sem("tr_ready"), sem("xnT_ready"), sem("lin_ready")
            h_ready, x_done = sem("h_ready"), sem("x_done")
            h_out = [sem(f"h_out{u}") for u in range(2)]
            spread_ready, spread_ps, bad_ready = sem("spread_ready"), sem("spread_ps"), sem("bad_ready")

            with nc.Block() as block:
                @block.sync
                def _(sp):
                    xt = x.rearrange("(t p) d -> p t d", p=P)
                    for c in range(CHUNKS):
                        sp.dma_start(X[:, c * PER:(c + 1) * PER, :], xt[:, c * PER:(c + 1) * PER, :]).then_inc(x_in[c], 16)
                    def store(t, u, _k):
                        sp.wait_ge(h_ready, t + 1)
                        sp.dma_start(h_table[bass.ds(t * P, P), :], hrow[u][:, :, :].rearrange("p a b -> p (a b)")).then_inc(h_out[u], 16)
                    in_pairs(sp, NT, store)
                    sp.wait_ge(h_out[0], 16 * (NT - NT // 2))
                    sp.wait_ge(h_out[1], 16 * (NT // 2))

                @block.gpsimd
                def _(pool):
                    chain = Chain(pool, pool_step)
                    pool.memset(wlin[:, :, :], 0.0).then_inc(w_zero, 1)
                    chain.then(pool.memset(ident[:, :], 0.0))
                    pool.memset(ones[:, :], 1.0)
                    chain.then(pool.affine_select(out=ident[:, :], in_=ident[:, :], compare_op=ALU.not_equal, fill=1.0,
                                                  base=0, pattern=[[-1, P]], channel_multiplier=1))
                    chain.then(pool.iota(riota[:, :, :], [[0, SUBS], [1, RANKS]], base=0, channel_multiplier=0,
                                         allow_small_or_imprecise_dtypes=True))
                    for j in range(SUBS):
                        chain.then(pool.iota(rcol[j * RANKS:(j + 1) * RANKS, :], [[1, 1]], base=0, channel_multiplier=1,
                                             allow_small_or_imprecise_dtypes=True))
                    pool.sem_inc(pool_const, 1)

                @block.scalar
                def _(act):
                    act.dma_start(zcol[:, :], z).then_inc(z_in, 16)
                    act.wait_ge(w_zero, 1)
                    for b, (top, bottom) in enumerate((((w_l10, w_sc0), (w_l11, w_sc1)), ((w_l11, w_sc1), (w_l11, w_sc1)))):
                        for half, ws in enumerate((top, bottom)):
                            for k, w in enumerate(ws):
                                lo = k * P + half * MUL
                                act.dma_start(wlin[half * MUL:(half + 1) * MUL, b, lo:lo + MUL], w).then_inc(w_in, 16)
                    act.dma_start(dst_a[:, :], bass.AP(dst_nat.tensor, 0, [[GROUP, NG], [1, GROUP + 1]])).then_inc(dst_in, 16)
                    act.dma_start(dst_i[:, :], dst).then_inc(dst_in, 16)
                    act.dma_start(base_i[0:NG, :, :], firsts).then_inc(dst_in, 16)

                    act.wait_ge(const_ready, 1)
                    act.wait_ge(var_ready, 1)
                    act.activation(rstd[:, :], tmp[:, :], ACT.Sqrt, bias=eps_col[:, 0:1], scale=1.0 / D).then_inc(std_ready, 1)

                    def h_of(t, u, k):
                        act.wait_ge(lin_ready, t + 1)
                        since(act, h_out[u], 16 * k)
                        act.activation(hrow[u][:, :, :], lin_ps[u][:, 0:2 * P].rearrange("p (a b) -> p a b", a=2), ACT.Copy,
                                       scale=z_h[:, bass.ds(t, 1)]).then_inc(h_ready, 1)

                    def body(t, u, k):
                        act.wait_ge(tr_ready, t + 1)
                        since(act, lin_ready, t - 1)
                        act.copy(xnT[u][:, :], tps[u][:, 0:2 * P]).then_inc(xnT_ready, 1)
                        if not isinstance(t, int) or t > 0:
                            h_of(t - 1, 1 - u, k - 1 + u)
                    act.wait_ge(z_ready, 2)
                    in_pairs(act, NT, body)
                    h_of(NT - 1, 0, NT // 2)

                @block.tensor
                def _(pe):
                    pe.wait_ge(pool_const, 1)
                    pe.wait_ge(w_in, 16 * 8)

                    def lin(t, u):
                        pe.wait_ge(xnT_ready, t + 1)
                        since(pe, h_ready, t - 1)
                        since(pe, x_done, t - 1)
                        for k, to in enumerate((lin_ps, sc_ps)):
                            for b in range(2):
                                last = pe.matmul(to[u][:, b * P:(b + 1) * P], xnT[u][:, b * P:(b + 1) * P], wlin[:, b, k * P:(k + 1) * P],
                                                 start=True, stop=True)
                        last.then_inc(lin_ready, 1)

                    def body(t, u, k):
                        pe.wait_ge(xn_ready, t + 1)
                        since(pe, xnT_ready, t - 1)
                        for b in range(2):
                            last = pe.transpose(tps[u][:, b * P:(b + 1) * P], xn[u][:, 2 * b:2 * b + 2, :], ident[:, :])
                        last.then_inc(tr_ready, 1)
                        if not isinstance(t, int) or t > 0:
                            lin(t - 1, 1 - u)
                    in_pairs(pe, NT, body)
                    lin(NT - 1, 0)

                    pe.wait_ge(spread_ready, 1)
                    pe.matmul(base_ps[:, 0:NG * SUBS], ones[:, :], diag[:, :, :], start=True, stop=True)
                    for k in range(2):
                        pe.matmul(col_ps[:, k * P:k * P + NG], spread[:, k, :, :], ident[:, 0:NG],
                                  start=True, stop=True)
                    pe.wait_ge(bad_ready, 1)
                    pe.matmul(base_ps[0:1, 511:512], bad[:, 2:3], ones[:, 0:1], start=True, stop=True).then_inc(spread_ps, 1)

                @block.vector
                def _(dve):
                    chain = Chain(dve, dve_step)
                    dve.memset(eps_col[:, :], EPS).then_inc(const_ready, 1)
                    dve.wait_ge(z_in, 16)
                    dve.tensor_scalar(z_h[:, :], zcol[:, :], INV_M, None, ALU.mult).then_inc(z_ready, 1)
                    dve.tensor_scalar(z_s[:, :], zcol[:, :], INV_M * C_S, None, ALU.mult).then_inc(z_ready, 1)
                    for c in range(CHUNKS):
                        dve.wait_ge(x_in[c], 16)
                        with dve.Fori(c * PER, (c + 1) * PER) as t:
                            dve.bn_stats(st[:, bass.ds(t, 1), :].rearrange("p a b -> p (a b)"),
                                         X[:, bass.ds(t, 1), :].rearrange("p a b -> p (a b)"))
                    chain.then(dve.memset(bad[:, :], 0.0))
                    stats_to_rstd(dve, st, tmp, chain, var_ready, std_ready)

                    def residual(t, u):
                        dve.wait_ge(lin_ready, t + 1)
                        xt = X[:, bass.ds(t, 1), :].rearrange("p a b -> p (a b)")
                        x0, x1 = xt[:, 0:MUL], xt[:, MUL:D].rearrange("p (v c) -> p c v", c=3)
                        s = sc_ps[u][:, 0:D].rearrange("p (c v) -> p c v", c=4)
                        dve.scalar_tensor_tensor(x0, s[:, 0, :], z_s[:, bass.ds(t, 1)], x0, ALU.mult, ALU.add)
                        dve.scalar_tensor_tensor(x1, s[:, 1:4, :], z_s[:, bass.ds(t, 1)], x1,
                                                 ALU.mult, ALU.add).then_inc(x_done, 1)

                    def body(t, u, k):
                        since(dve, tr_ready, t - 1)
                        xt = X[:, bass.ds(t, 1), :].rearrange("p a b -> p (a b)")
                        m, r = mean[:, bass.ds(t, 1)], rstd[:, bass.ds(t, 1)]
                        dve.tensor_scalar(xn[u][:, 0, :], xt[:, 0:MUL], m, r, ALU.subtract, ALU.mult)
                        dve.tensor_scalar(xn[u][:, 1:4, :], xt[:, MUL:D].rearrange("p (v c) -> p c v", c=3), m, r,
                                          ALU.subtract, ALU.mult).then_inc(xn_ready, 1)
                        if not isinstance(t, int) or t > 0:
                            residual(t - 1, 1 - u)
                    in_pairs(dve, NT, body)
                    residual(NT - 1, 0)

                    dve.wait_ge(dst_in, 16 * 3)
                    chain.then(dve.memset(base_f[:, :, :], 0.0))
                    chain.then(dve.tensor_copy(base_f[0:NG, :, :], base_i[0:NG, :, :]))
                    chain.then(dve.memset(base_f[0:1, 0, 0:1], 0.0))
                    chain.then(dve.tensor_tensor(diff[:, :], dst_a[:, 1:GROUP + 1], dst_a[:, 0:GROUP], ALU.subtract))
                    chain.then(dve.tensor_reduce(bad[0:NG, 0:1], diff[:, :], AX.X, ALU.min))
                    chain.then(dve.tensor_tensor(diff[:, 0:SUBS], base_f[0:NG, 1, :], base_f[0:NG, 0, :], ALU.subtract))
                    chain.then(dve.tensor_reduce(bad[0:NG, 1:2], diff[:, 0:SUBS], AX.X, ALU.max))
                    chain.then(dve.tensor_scalar(bad[:, 0:1], bad[:, 0:1], 0.0, None, ALU.is_lt))
                    chain.then(dve.tensor_scalar(bad[:, 1:2], bad[:, 1:2], float(RANKS - 1), None, ALU.is_gt))
                    dve.tensor_tensor(bad[:, 2:3], bad[:, 0:1], bad[:, 1:2], ALU.add).then_inc(bad_ready, 1)
                    dve.wait_ge(pool_const, 1)
                    dve.tensor_tensor(diag[:, :, :], ident[:, 0:NG, None].to_broadcast((P, NG, SUBS)),
                                      base_f[:, 0:1, :].to_broadcast((P, NG, SUBS)), ALU.mult)
                    for k in range(2):
                        last = dve.tensor_copy(spread[:, k, :, :], base_f[:, k, :, None].to_broadcast((P, SUBS, RANKS)))
                    last.then_inc(spread_ready, 1)
                    dve.wait_ge(spread_ps, 1)
                    chain.then(dve.tensor_scalar(neg_base[:, :, :].rearrange("p g j -> p (g j)"), base_ps[:, 0:NG * SUBS], -1.0, None, ALU.mult))
                    chain.then(dve.tensor_scalar(ncol[:, :], col_ps[:, 0:NG], rcol[:, 0:1], None, ALU.add))
                    chain.then(dve.tensor_scalar(neg_ncol[:, :], ncol[:, :], -1.0, None, ALU.mult))
                    chain.then(dve.tensor_tensor(next_col[:, :], ncol[:, :], col_ps[:, P:P + NG], ALU.is_ge))
                    chain.then(dve.scalar_tensor_tensor(row_index[:, :], next_col[:, :], SKIP, ncol[:, :], ALU.mult, ALU.add))
                    chain.then(dve.tensor_tensor(rank[:, :].rearrange("p (w q) -> p w q", q=QS), dst_i[:, :].rearrange("p (w q) -> p w q", q=QS),
                                                 neg_base[:, :, :].rearrange("p g j -> p (g j)")[:, :, None].to_broadcast((P, NG * SUBS, QS)), ALU.add))
                    chain.then(dve.tensor_scalar(flag[:, :], base_ps[0:1, 511:512], 0.0, None, ALU.is_gt))

        with ExitStack() as c2:
            def s2(name, shape, dt=F32):
                return sb(name, shape, dt, c2)

            def sem(name):
                return c2.enter_context(nc.semaphore(name))

            fc0_s = s2("fc0_s", [P, P])
            fc1_s = s2("fc1_s", [P, 2, D])
            e8_s = [s2(f"e8_s{v}", [P, 2, WIN]) for v in range(2)]
            src_s = [s2(f"src_s{v}", [P, GT], I32) for v in range(2)]
            sh_s = [s2(f"sh_s{v}", [P, GT, 4]) for v in range(2)]
            hid = [[s2(f"hid{v}{h}", [P, WIN]) for h in range(2)] for v in range(2)]
            xs = [s2(f"xs{v}", [P, QS, SUBS, D]) for v in range(2)]
            mid = [s2(f"mid{k}", [P, SUBS, Y]) for k in range(4)]
            eq = s2("eq", [P, GT, RANKS])
            sel = [s2(f"sel{v}", [P, GT, 4, RANKS]) for v in range(2)]
            same = [s2(f"same{v}", [P, SUBS, RANKS]) for v in range(2)]
            carry = [s2(f"carry{v}", [P, RANKS]) for v in range(2)]
            part = [s2(f"part{v}", [P, Y]) for v in range(2)]
            total = [s2(f"total{v}", [P, Y]) for v in range(2)]
            row_s = [s2(f"row_s{v}", [P, 1], U32) for v in range(2)]
            before = s2("before", [P, P])
            first = s2("first", [P, 2])

            w_ps = [[c2.enter_context(nc.psum_tensor(f"w_ps{k}{h}", [P, 2, D], F32)) for h in range(2)] for k in range(2)]
            y_ps = [c2.enter_context(nc.psum_tensor(f"y_ps{v}", [P, Y], F32)) for v in range(2)]
            hid_ps = c2.enter_context(nc.psum_tensor("hid_ps", [P, WIN], F32))
            t_ps = c2.enter_context(nc.psum_tensor("t_ps", [P, Y], F32))

            pool_went_on, g_went_on = sem("pool_went_on"), sem("g_went_on")
            zero_done, fc_in, fc_zero, before_done = sem("zero_done"), sem("fc_in"), sem("fc_zero"), sem("before_done")
            e8_in = [sem(f"e8_in{v}") for v in range(2)]
            src_in = [sem(f"src_in{v}") for v in range(2)]
            sh_in = [sem(f"sh_in{v}") for v in range(2)]
            xs_in = [[sem(f"xs_in{v}{q}") for q in range(QS)] for v in range(2)]
            hid_done, hid_ready, w_done = sem("hid_done"), sem("hid_ready"), sem("w_done")
            eq_done, sel_done, mid_done, seg_done = sem("eq_done"), sem("sel_done"), sem("mid_done"), sem("seg_done")
            same_done, y_done, part_done, t_done, total_done = sem("same_done"), sem("y_done"), sem("part_done"), sem("t_done"), sem("total_done")
            y_out = [sem(f"y_out{v}") for v in range(2)]
            g_cleared, g_in, g_src, g_gather, g_old, g_put = sem("g_cleared"), sem("g_in"), sem("g_src"), sem("g_gather"), sem("g_old"), sem("g_put")
            g_hid, g_silu, g_w, g_sel, g_row, g_sum, g_new, g_dve, g_zero = (
                sem("g_hid"), sem("g_silu"), sem("g_w"), sem("g_sel"), sem("g_row"), sem("g_sum"), sem("g_new"), sem("g_dve"), sem("g_zero"))

            def products(dve, w, x_row, m):
                wk = w.rearrange("p (f k u) -> p f k u", f=2, k=2)
                mk = m.rearrange("p (b u) -> p b u", u=MUL)
                dve.tensor_tensor(mk[:, 0:8:7, :], wk[:, 0, :, :], x_row[:, None, 0:MUL].to_broadcast((P, 2, MUL)), ALU.mult)
                return dve.tensor_tensor(mk[:, 1:7, :].rearrange("p (k c) u -> p k c u", k=2), wk[:, 1, :, None, :].to_broadcast((P, 2, 3, MUL)),
                                         x_row[:, MUL:D].rearrange("p (c u) -> p c u", c=3)[:, None, :, :].to_broadcast((P, 2, 3, MUL)), ALU.mult)

            def segment(pe, acc, lhs, m, first):
                to = acc.rearrange("p (b u) -> p b u", u=MUL)
                yield lambda: pe.matmul(to[:, 0:8:2, :], lhs(0), m[:, 0:D], start=first, stop=False, skip_group_check=True)
                for c in range(1, 4):
                    moving = m[:, D:Y].rearrange("p (b u) -> p b u", u=MUL)[:, c - 1:4:4 - c, :]
                    yield lambda c=c, moving=moving: pe.matmul(to[:, 1:2 * c + 2:2 * c, :], lhs(c), moving, start=False, stop=False, skip_group_check=True)

            with nc.Block() as block:
                @block.sync
                def _(sp):
                    sp.wait_ge(fc_zero, 4)
                    for h in range(2):
                        sp.dma_start(fc0_s[h * NB:(h + 1) * NB, h * RN:(h + 1) * RN], fc0).then_inc(fc_in, 16)
                        sp.dma_start(fc1_s[h * RN:(h + 1) * RN, h, :], fc1).then_inc(fc_in, 16)
                    bad = sp.value_load(flag[0:1, 0:1], min_val=0, max_val=1)
                    with sp.If(bad == 0):
                        def load(g, v, k):
                            if k is not None:
                                sp.wait_ge(hid_done, 2 * (g - 1))
                            sp.dma_start(e8_s[v][0:2 * NB, :, :], e8[bass.ds(g, 1), :, :, :].rearrange("g h f e -> f (g h) e")).then_inc(e8_in[v], 16)
                            if k is not None:
                                for q in range(QS):
                                    sp.wait_ge(xs_in[v][q], 16 * SUBS * k)
                            sp.dma_start(src_s[v][:, :], src[bass.ds(g, 1), :, :].rearrange("g p t -> (g p) t")).then_inc(src_in[v], 16)
                            if k is not None:
                                sp.wait_ge(sel_done, g - 1)
                            sp.dma_start(sh_s[v][:, :, :].rearrange("p t c -> p (t c)"), sh[bass.ds(g, 1), :, :].rearrange("g p t -> (g p) t")).then_inc(sh_in[v], 16)
                        load(0, 0, None)
                        load(1, 1, None)
                        with sp.Fori(1, NG // 2) as i:
                            load(2 * i, 0, i)
                            load(2 * i + 1, 1, i)
                    with sp.Else():
                        sp.wait_ge(g_zero, 1)
                        with sp.Fori(0, NT) as t:
                            sp.dma_start(y_sums[bass.ds(t * P, P), :], total[0][:, :]).then_inc(g_cleared, 16)
                        sp.wait_ge(g_cleared, 16 * NT)
                        with sp.Fori(0, NG) as g:
                            for j in range(SUBS):
                                for q in range(QS):
                                    s = g * GT + j * QS + q
                                    sp.dma_start(e8_s[0][0:NB, 0, 0:P], e8[bass.ds(g, 1), j // 2, (j % 2) * NB:(j % 2 + 1) * NB, q * P:(q + 1) * P].rearrange("g f e -> (g f) e")).then_inc(g_in, 16)
                                    with nc.allow_non_contiguous_dma(reason="one index a partition"):
                                        sp.dma_start(src_s[0][:, 0:1], src[bass.ds(g, 1), :, j * QS + q:j * QS + q + 1].rearrange("g p t -> (g p) t")).then_inc(g_src, 16)
                                    sp.dma_start(sh_s[0][:, 0, :], sh[bass.ds(g, 1), :, (j * QS + q) * 4:(j * QS + q) * 4 + 4].rearrange("g p t -> (g p) t")).then_inc(g_src, 16)
                                    sp.wait_ge(g_put, 16 * (s + 1))
                                    sp.sem_inc(g_went_on, 1)

                @block.gpsimd
                def _(pool):
                    pool.affine_select(out=before[:, :], in_=ones[:, :], compare_op=ALU.is_gt, fill=0.0,
                                       base=0, pattern=[[-1, P]], channel_multiplier=1).then_inc(before_done, 1)
                    def hold(sem, value):
                        pool.wait_ge(sem, value)
                        pool.sem_inc(pool_went_on, 1)

                    bad = pool.value_load(flag[0:1, 0:1], min_val=0, max_val=1)
                    with pool.If(bad == 0):
                        def scatter(g, v):
                            hold(total_done, 2 * (g + 1))
                            pool.indirect_dma_start(y_sums, bass.IndirectOffsetOnAxis(ap=row_s[v][:, 0:1], axis=0), total[v][:, :], None,
                                                    bounds_check=NPAD - 1, oob_is_err=False).then_inc(y_out[v], 16)

                        def gather(g, v, k, lag):
                            if lag:
                                scatter(g - 3, 1 - v)
                            hold(src_in[v], 16 * (k + 1))
                            for q in range(QS):
                                if not isinstance(g, int) or g >= 2:
                                    hold(mid_done, 4 * (g - 2) + q + 1)
                                for j in range(SUBS):
                                    t = j * QS + q
                                    pool.indirect_dma_start(xs[v][:, q, j, :], None, h_table,
                                                            bass.IndirectOffsetOnAxis(ap=src_s[v][:, t:t + 1], axis=0)).then_inc(xs_in[v][q], 16)
                        for g in range(4):
                            gather(g, g % 2, g // 2, g >= 3)
                        with pool.Fori(2, NG // 2) as i:
                            gather(2 * i, 0, i, True)
                            gather(2 * i + 1, 1, i, True)
                        for g in range(NG - 3, NG):
                            scatter(g, g % 2)
                        for v in range(2):
                            pool.wait_ge(y_out[v], 16 * (NG // 2))
                    with pool.Else():
                        with pool.Fori(0, NG * GT) as s:
                            hold(g_src, 32 * (s + 1))
                            pool.indirect_dma_start(xs[0][:, 0, 0, :], None, h_table,
                                                    bass.IndirectOffsetOnAxis(ap=src_s[0][:, 0:1], axis=0)).then_inc(g_gather, 16)
                            hold(g_row, 2 * (s + 1))
                            hold(g_gather, 16 * (s + 1))
                            pool.indirect_dma_start(total[1][:, :], None, y_sums,
                                                    bass.IndirectOffsetOnAxis(ap=row_s[0][:, 0:1], axis=0)).then_inc(g_old, 16)
                            hold(g_new, s + 1)
                            pool.indirect_dma_start(y_sums, bass.IndirectOffsetOnAxis(ap=row_s[1][:, 0:1], axis=0), total[0][:, :], None,
                                                    bounds_check=NPAD - 1, oob_is_err=False).then_inc(g_put, 16)
                        pool.wait_ge(g_put, 16 * NG * GT)

                @block.scalar
                def _(act):
                    bad = act.value_load(flag[0:1, 0:1], min_val=0, max_val=1)
                    with act.If(bad == 0):
                        def silu(g, v, h):
                            act.wait_ge(hid_done, 2 * g + h + 1)
                            since(act, w_done, 4 * (g - 1))
                            act.activation(hid[v][h][:, :], hid_ps[:, :], ACT.Silu, scale=float(1.0 / np.sqrt(NB))).then_inc(hid_ready, 1)

                        def take_part(g, v):
                            act.wait_ge(y_done, g + 1)
                            since(act, t_done, g - 1)
                            act.copy(part[v][:, :], y_ps[v][:, :]).then_inc(part_done, 1)

                        def take_total(g, v, k):
                            act.wait_ge(t_done, g + 1)
                            since(act, y_out[v], 16 * k)
                            act.copy(row_s[v][:, :], row_index[:, bass.ds(g, 1)]).then_inc(total_done, 1)
                            act.copy(total[v][:, :], t_ps[:, :]).then_inc(total_done, 1)

                        def body(g, v, k, last=False):
                            started = not isinstance(g, int) or g > 0
                            if started:
                                take_part(g - 1, 1 - v)
                            if not last:
                                silu(g + 1, 1 - v, 0)
                            if started:
                                take_total(g - 1, 1 - v, k - 1 + v)
                            if not last:
                                silu(g + 1, 1 - v, 1)
                        silu(0, 0, 0)
                        silu(0, 0, 1)
                        body(0, 0, 0)
                        body(1, 1, 0)
                        with act.Fori(1, NG // 2 - 1) as i:
                            body(2 * i, 0, i)
                            body(2 * i + 1, 1, i)
                        body(NG - 2, 0, NG // 2 - 1)
                        body(NG - 1, 1, NG // 2 - 1, last=True)
                        take_part(NG - 1, 1)
                        take_total(NG - 1, 1, NG // 2 - 1)
                    with act.Else():
                        with act.Fori(0, NG * GT) as s:
                            act.wait_ge(g_hid, s + 1)
                            act.activation(hid[0][0][:, 0:P], hid_ps[:, 0:P], ACT.Silu, scale=float(1.0 / np.sqrt(NB))).then_inc(g_silu, 1)

                @block.tensor
                def _(pe):
                    pe.wait_ge(fc_in, 16 * 4)
                    bad = pe.value_load(flag[0:1, 0:1], min_val=0, max_val=1)
                    with pe.If(bad == 0):
                        def first_layer(g, v, k, h):
                            pe.wait_ge(e8_in[v], 16 * (k + 1))
                            since(pe, hid_ready, 2 * g + h)
                            pe.matmul(hid_ps[:, :], fc0_s[:, :], e8_s[v][:, h, :], start=True, stop=True).then_inc(hid_done, 1)

                        def second_layer(g, v, q):
                            if q == 0:
                                pe.wait_ge(hid_ready, 2 * g + 2)
                            since(pe, mid_done, 4 * g + q - 1)
                            for h in range(2):
                                last = pe.matmul(w_ps[q % 2][h][:, :, :], hid[v][h][:, q * P:(q + 1) * P], fc1_s[:, :, :], start=True, stop=True)
                            last.then_inc(w_done, 1)

                        def sum_up(g, v, q):
                            pe.wait_ge(mid_done, 4 * g + q + 1)
                            if q == 0:
                                pe.wait_ge(sel_done, g + 1)
                                since(pe, part_done, g - 1)
                            parts = [list(segment(pe, y_ps[v][j * RANKS:(j + 1) * RANKS, :],
                                                  lambda c, t=j * QS + q: sel[v][:, t, c, :], mid[q][:, j, :], q == 0)) for j in range(SUBS)]
                            for c in range(4):
                                for j in range(SUBS):
                                    last = parts[j][c]()
                            last.then_inc(seg_done, 1)

                        def hand_over(g, v):
                            since(pe, part_done, g)
                            since(pe, same_done, g)
                            pe.matmul(y_ps[v][0:RANKS, :], carry[1 - v][:, :], part[1 - v][:, :], start=False, stop=True,
                                      skip_group_check=True).then_inc(y_done, 1)

                        def merge(g, v):
                            pe.wait_ge(part_done, g + 1)
                            pe.wait_ge(same_done, g + 1)
                            since(pe, total_done, 2 * g)
                            pe.matmul(t_ps[:, :], same[v][:, :, :], part[v][:, :], start=True, stop=True).then_inc(t_done, 1)

                        def body(g, v, k, last=False):
                            started = not isinstance(g, int) or g > 0
                            for q in range(QS):
                                second_layer(g, v, q)
                                if q > 0:
                                    sum_up(g, v, q - 1)
                                elif started:
                                    sum_up(g - 1, 1 - v, QS - 1)
                                    hand_over(g - 1, 1 - v)
                                if q == 2 and started:
                                    merge(g - 1, 1 - v)
                                if q % 2 and not last:
                                    first_layer(g + 1, 1 - v, k + v, q // 2)
                        first_layer(0, 0, 0, 0)
                        first_layer(0, 0, 0, 1)
                        pe.wait_ge(zero_done, 1)
                        body(0, 0, 0)
                        body(1, 1, 0)
                        with pe.Fori(1, NG // 2 - 1) as i:
                            body(2 * i, 0, i)
                            body(2 * i + 1, 1, i)
                        body(NG - 2, 0, NG // 2 - 1)
                        body(NG - 1, 1, NG // 2 - 1, last=True)
                        sum_up(NG - 1, 1, QS - 1)
                        hand_over(NG - 1, 1)
                        merge(NG - 1, 1)
                    with pe.Else():
                        with pe.Fori(0, NG * GT) as s:
                            pe.wait_ge(g_in, 16 * (s + 1))
                            pe.matmul(hid_ps[:, 0:P], fc0_s[:, :], e8_s[0][:, 0, 0:P], start=True, stop=True).then_inc(g_hid, 1)
                            pe.wait_ge(g_silu, s + 1)
                            pe.matmul(w_ps[0][0][:, :, :], hid[0][0][:, 0:P], fc1_s[:, :, :], start=True, stop=True).then_inc(g_w, 1)
                            pe.wait_ge(g_sel, 3 * s + 1)
                            pe.transpose(t_ps[:, 0:P], same[0][:, :, :], ident[:, :]).then_inc(g_sum, 1)
                            pe.wait_ge(g_sel, 3 * s + 3)
                            parts = list(segment(pe, y_ps[0][:, :], lambda c: sel[0][:, c, :, :].rearrange("p a r -> p (a r)"), mid[0][:, 0, :], True))
                            for p in parts:
                                last = p()
                            last.then_inc(g_sum, 1)

                @block.vector
                def _(dve):
                    dve.memset(fc0_s[:, :], 0.0).then_inc(fc_zero, 1)
                    dve.memset(fc1_s[:, :, :], 0.0).then_inc(fc_zero, 1)
                    dve.memset(e8_s[0][:, :, :], 0.0).then_inc(fc_zero, 1)
                    dve.memset(e8_s[1][:, :, :], 0.0).then_inc(fc_zero, 1)
                    dve.memset(part[1][:, :], 0.0)
                    dve.memset(carry[0][:, :], 0.0)
                    dve.memset(carry[1][:, :], 0.0).then_inc(zero_done, 1)
                    dve.memset(total[0][:, :], 0.0).then_inc(g_zero, 1)
                    dve.wait_ge(zero_done, 1)
                    bad = dve.value_load(flag[0:1, 0:1], min_val=0, max_val=1)
                    with dve.If(bad == 0):
                        def select(g, v, k):
                            dve.wait_ge(sh_in[v], 16 * (k + 1))
                            since(dve, seg_done, 4 * (g - 1))
                            dve.tensor_tensor(eq[:, :, :], riota[:, 0:1, :].to_broadcast((P, GT, RANKS)),
                                              rank[:, bass.ds(g * GT, GT)][:, :, None].to_broadcast((P, GT, RANKS)), ALU.is_equal).then_inc(eq_done, 1)
                            dve.wait_ge(eq_done, g + 1)
                            dve.tensor_tensor(sel[v][:, :, :, :], eq[:, :, None, :].to_broadcast((P, GT, 4, RANKS)),
                                              sh_s[v][:, :, :, None].to_broadcast((P, GT, 4, RANKS)), ALU.mult).then_inc(sel_done, 1)

                        def share(g, v, last):
                            since(dve, t_done, g - 1)
                            since(dve, y_done, g)
                            if not last:
                                dve.scalar_tensor_tensor(carry[v][:, 0:1], neg_ncol[:, bass.ds(g, 1)], 0.0, neg_base[:, bass.ds(g + 1, 1), 0:1].rearrange("p g j -> p (g j)"),
                                                         ALU.add, ALU.is_equal)
                            dve.scalar_tensor_tensor(same[v][:, :, :], riota[:, :, :], neg_ncol[:, bass.ds(g, 1)],
                                                     neg_base[:, bass.ds(g, 1), :].rearrange("p g j -> p (g j)")[:, :, None].to_broadcast((P, SUBS, RANKS)),
                                                     ALU.add, ALU.is_equal).then_inc(same_done, 1)

                        def messages(g, v, k, q):
                            dve.wait_ge(w_done, 4 * g + q + 1)
                            dve.wait_ge(xs_in[v][q], 16 * SUBS * (k + 1))
                            since(dve, seg_done, 4 * (g - 1) + q + 1)
                            for j in range(SUBS):
                                last = products(dve, w_ps[q % 2][j // 2][:, j % 2, :], xs[v][:, q, j, :], mid[q][:, j, :])
                            last.then_inc(mid_done, 1)

                        def body(g, v, k, last=False):
                            select(g, v, k)
                            for q in range(QS):
                                messages(g, v, k, q)
                                if q == 1:
                                    share(g, v, last)
                        body(0, 0, 0)
                        body(1, 1, 0)
                        with dve.Fori(1, NG // 2 - 1) as i:
                            body(2 * i, 0, i)
                            body(2 * i + 1, 1, i)
                        body(NG - 2, 0, NG // 2 - 1)
                        body(NG - 1, 1, NG // 2 - 1, last=True)
                    with dve.Else():
                        with dve.Fori(0, NG * GT) as s:
                            def step(n, ins):
                                ins.then_inc(g_dve, 1)
                                dve.wait_ge(g_dve, s * 4 + n)
                            dst_col = rank[:, bass.ds(s, 1)]
                            dve.wait_ge(g_src, 32 * (s + 1))
                            step(1, dve.tensor_scalar(dst_col, dst_i[:, bass.ds(s, 1)], 1.0, None, ALU.mult))
                            dve.tensor_scalar(same[0][:, :, :].rearrange("p j r -> p (j r)"), dst_col.to_broadcast((P, P)), 1.0, None, ALU.mult).then_inc(g_sel, 1)
                            dve.tensor_scalar(row_s[0][:, :], dst_col, 1.0, None, ALU.mult).then_inc(g_row, 1)
                            dve.wait_ge(g_sum, 2 * s + 1)
                            eqm = eq[:, 0:4, :].rearrange("p a b -> p (a b)")
                            step(2, dve.tensor_scalar(eqm, t_ps[:, 0:P], dst_col, None, ALU.is_equal))
                            for c in range(4):
                                last = dve.tensor_scalar(sel[0][:, c, :, :], eq[:, 0:4, :], sh_s[0][:, 0, c:c + 1], None, ALU.mult)
                            last.then_inc(g_sel, 1)
                            dve.wait_ge(before_done, 1)
                            step(3, dve.scalar_tensor_tensor(eq[:, 4:8, :].rearrange("p a b -> p (a b)"), eqm, 1.0, before[:, :], ALU.mult, ALU.mult,
                                                             accum_out=first[:, 0:1]))
                            step(4, dve.tensor_scalar(first[:, 1:2], first[:, 0:1], SKIP, dst_col, ALU.mult, ALU.add))
                            dve.tensor_copy(row_s[1][:, :], first[:, 1:2]).then_inc(g_row, 1)
                            dve.wait_ge(g_w, s + 1)
                            dve.wait_ge(g_gather, 16 * (s + 1))
                            products(dve, w_ps[0][0][:, 0, :], xs[0][:, 0, 0, :], mid[0][:, 0, :]).then_inc(g_sel, 1)
                            dve.wait_ge(g_sum, 2 * s + 2)
                            dve.wait_ge(g_old, 16 * (s + 1))
                            dve.tensor_tensor(total[0][:, :], total[1][:, :], y_ps[0][:, :], ALU.add).then_inc(g_new, 1)

        windows.close()

        with ExitStack() as c3:
            def s3(name, shape, dt=F32):
                return sb(name, shape, dt, c3)

            def sem(name):
                return c3.enter_context(nc.semaphore(name))

            wl2 = s3("wl2", [P, 2, MUL])
            router_s = s3("router_s", [P, 2, NE])
            w1_s = s3("w1_s", [P, NE, 2, D])
            w2_s = s3("w2_s", [P, NE, 2, D])
            b1_s = s3("b1_s", [P, NE, 2])
            b2_s = s3("b2_s", [P, D])
            tT = s3("tT", [P, 2, NPAD])
            eighth = s3("eighth", [P, NE])

            x_in = [sem(f"y_in{u}") for u in range(2)]
            wl_in, wl_ready, w_in, b2_zero = sem("wl_in"), sem("wl_ready"), sem("w_in3"), sem("b2_zero")
            tr_done, tr_taken, o_done, o_taken = sem("tr_done"), sem("tr_taken"), sem("o_done"), sem("o_taken")
            var_ready, std_ready, dve_step, pool_ready = sem("var_ready3"), sem("std_ready3"), sem("dve_step3"), sem("pool_ready")
            tn_done, tp_done, tp_taken, kept, logit_done = sem("tn_done"), sem("tp_done"), sem("tp_taken"), sem("kept"), sem("logit_done")
            shifted, powered, comb_done, combT_ps, combT_done, comb_out = (
                sem("shifted"), sem("powered"), sem("comb_done"), sem("combT_ps"), sem("combT_done"), sem("comb_out"))
            with nc.Block() as block, ExitStack() as c:
                yb = [sb(f"yb{u}", [P, Y], F32, c) for u in range(2)]
                yT = [sb(f"yT{u}", [P, Y], F32, c) for u in range(2)]
                tn = [sb(f"tn{u}", [P, D], F32, c) for u in range(2)]
                tnT = [sb(f"tnT{u}", [P, 2, P], F32, c) for u in range(2)]
                st = sb("st3", [P, NT, 6], F32, c)
                tmp = sb("tmp3", [P, NT], F32, c)
                prob, rest, comb = (sb(name, [P, NT, NE], F32, c) for name in ("prob", "rest", "comb"))
                pick = [sb(f"pick{n}", [P, NT, NE], F32, c) for n in range(2)]
                top = [sb(f"top{n}", [P, NT], F32, c) for n in range(3)]
                combT = sb("combT", [P, -(-NT // 16), P], F32, c)
                tps = [c.enter_context(nc.psum_tensor(f"ytp{u}", [P, Y], F32)) for u in range(2)]
                ops = [c.enter_context(nc.psum_tensor(f"yop{u}", [P, 512], F32)) for u in range(2)]
                logit_ps = c.enter_context(nc.psum_tensor("logit_ps", [P, 512], F32))
                ct_ps = c.enter_context(nc.psum_tensor("ct_ps", [P, 512], F32))
                LW = -(-NT // 16)

                @block.sync
                def _(sp):
                    def load(t, u, k):
                        since(sp, tr_done, t - 1)
                        sp.dma_start(yb[u][:, :], y_sums[bass.ds(t * P, P), :]).then_inc(x_in[u], 16)
                    in_pairs(sp, NT, load)
                    for e in range(NE):
                        sp.dma_start(w1_s[:, e, :, :], w1[e].rearrange("(k p) n -> p k n", p=P)).then_inc(w_in, 16)
                        sp.dma_start(w2_s[:, e, :, :], w2[e].rearrange("(k p) n -> p k n", p=P)).then_inc(w_in, 16)
                    sp.dma_start(b1_s[:, :, :], b1).then_inc(w_in, 16)
                    sp.wait_ge(b2_zero, 1)
                    sp.dma_start(b2_s[0:NE, :], b2).then_inc(w_in, 16)
                    sp.wait_ge(combT_done, 1)
                    for b in range(LW):
                        tiles = min(16, NT - 16 * b)
                        sp.dma_start(comb_rows.rearrange("e (t p) -> t e p", p=P)[16 * b:16 * b + tiles, :, :], combT[0:tiles * NE, b, :]).then_inc(comb_out, 16)
                    sp.wait_ge(comb_out, 16 * LW)
                    sp.wait_ge(w_in, 16 * (2 * NE + 2))

                @block.gpsimd
                def _(pool):
                    pool.iota(eighth[:, :], [[-1, NE]], base=NE, channel_multiplier=0, allow_small_or_imprecise_dtypes=True).then_inc(pool_ready, 1)

                    def body(t, u, k):
                        pool.wait_ge(tn_done, t + 1)
                        xt = X[:, bass.ds(t, 1), :].rearrange("p a b -> p (a b)")
                        pool.tensor_tensor(xt, xt, tn[u][:, :], ALU.add)
                        pool.wait_ge(tp_taken, t + 1)
                        pool.tensor_copy(tT[:, :, bass.ds(t * P, P)], tnT[u][:, :, :]).then_inc(kept, 1)
                    in_pairs(pool, NT, body)

                @block.scalar
                def _(act):
                    act.dma_start(wl2[:, 0, :], w_l20).then_inc(wl_in, 16)
                    for h in range(2):
                        act.dma_start(wl2[(1 - h) * MUL:(2 - h) * MUL, 1, :], w_l21[h * MUL:(h + 1) * MUL, :]).then_inc(wl_in, 16)
                    act.dma_start(router_s[:, :, :], router_t.rearrange("(k p) e -> p k e", p=P)).then_inc(wl_in, 16)
                    act.wait_ge(wl_in, 64)
                    act.mul(wl2[0:MUL, 0, :], wl2[0:MUL, 0, :], OUT_SCALE)
                    act.mul(wl2[MUL:P, 0, :], wl2[MUL:P, 0, :], OUT_SCALE * INV_SQRT3)
                    act.mul(wl2[:, 1, :], wl2[:, 1, :], OUT_SCALE).then_inc(wl_ready, 1)

                    def take(t, u, k):
                        act.wait_ge(tr_done, t + 1)
                        since(act, o_done, t - 1)
                        act.copy(yT[u][:, :], tps[u][:, :]).then_inc(tr_taken, 1)
                    in_pairs(act, NT, take)
                    act.wait_ge(var_ready, 1)
                    act.activation(rstd[:, :], tmp[:, :], ACT.Sqrt, bias=eps_col[:, 0:1], scale=1.0 / D).then_inc(std_ready, 1)

                    def keep(t, u, k):
                        act.wait_ge(tp_done, t + 1)
                        since(act, kept, t - 1)
                        since(act, logit_done, t - 1)
                        act.copy(tnT[u][:, :, :], ops[u][:, 0:D].rearrange("p (k n) -> p k n", k=2)).then_inc(tp_taken, 1)
                    in_pairs(act, NT, keep)
                    act.wait_ge(shifted, 1)
                    act.activation(prob[:, :, :], rest[:, :, :], ACT.Exp).then_inc(powered, 1)
                    act.wait_ge(combT_ps, 1)
                    act.copy(combT[:, :, :], ct_ps[:, 0:LW * P].rearrange("p (b n) -> p b n", b=LW)).then_inc(combT_done, 1)

                @block.tensor
                def _(pe):
                    pe.wait_ge(wl_ready, 1)

                    def lin2(t, u):
                        pe.wait_ge(tr_taken, t + 1)
                        since(pe, o_taken, t - 1)
                        pe.matmul(ops[u][:, 0:MUL], yT[u][:, 0:P], wl2[:, 0, :], start=True, stop=True)
                        for c in range(3):
                            last = pe.matmul(ops[u][:, MUL + c:D:3], yT[u][:, (c + 1) * P:(c + 2) * P], wl2[:, 1, :], start=True, stop=True)
                        last.then_inc(o_done, 1)

                    def turn(t, u, k):
                        pe.wait_ge(x_in[u], 16 * (k + 1))
                        since(pe, tr_taken, t - 1)
                        for b in range(4):
                            last = pe.transpose(tps[u][:, b * P:(b + 1) * P], yb[u][:, b * P:(b + 1) * P], ident[:, :])
                        last.then_inc(tr_done, 1)
                        if not isinstance(t, int) or t > 0:
                            lin2(t - 1, 1 - u)
                    in_pairs(pe, NT, turn)
                    lin2(NT - 1, 0)

                    def logits(t, u):
                        pe.wait_ge(tp_taken, t + 1)
                        for k in range(2):
                            last = pe.matmul(logit_ps[:, bass.ds(t * NE, NE)], tnT[u][:, k, :], router_s[:, k, :], start=(k == 0), stop=(k == 1))
                        last.then_inc(logit_done, 1)

                    def turn_back(t, u, k):
                        pe.wait_ge(tn_done, t + 1)
                        if isinstance(t, int) and t < 2:
                            pe.wait_ge(o_taken, NT)
                        since(pe, tp_taken, t - 1)
                        for b in range(2):
                            last = pe.transpose(ops[u][:, b * P:(b + 1) * P], tn[u][:, b * P:(b + 1) * P], ident[:, :])
                        last.then_inc(tp_done, 1)
                        if not isinstance(t, int) or t > 0:
                            logits(t - 1, 1 - u)
                    in_pairs(pe, NT, turn_back)
                    logits(NT - 1, 0)

                    pe.wait_ge(comb_done, 1)
                    for b in range(LW):
                        tiles = min(16, NT - 16 * b)
                        last = pe.transpose(ct_ps[0:tiles * NE, b * P:(b + 1) * P], comb[:, 16 * b:16 * b + tiles, :], ident[:, :])
                    last.then_inc(combT_ps, 1)

                @block.vector
                def _(dve):
                    chain = Chain(dve, dve_step)
                    dve.memset(b2_s[:, :], 0.0).then_inc(b2_zero, 1)
                    dve.memset(ct_ps[:, :], 0.0)

                    def residual(t, u, k):
                        dve.wait_ge(o_done, t + 1)
                        xt = X[:, bass.ds(t, 1), :].rearrange("p a b -> p (a b)")
                        dve.scalar_tensor_tensor(xt, ops[u][:, 0:D], zcol[:, bass.ds(t, 1)], xt, ALU.mult, ALU.add).then_inc(o_taken, 1)
                        if not isinstance(t, int) or t > 0:
                            stats(t - 1)

                    def stats(t):
                        dve.wait_ge(o_taken, t + 1)
                        dve.bn_stats(st[:, bass.ds(t, 1), :].rearrange("p a b -> p (a b)"), X[:, bass.ds(t, 1), :].rearrange("p a b -> p (a b)"))
                    in_pairs(dve, NT, residual)
                    stats(NT - 1)
                    chain.then(dve.memset(rest[:, :, :], 0.0))
                    stats_to_rstd(dve, st, tmp, chain, var_ready, std_ready)

                    def norm(t, u, k):
                        since(dve, tp_done, t - 1)
                        since(dve, kept, t - 1)
                        xt = X[:, bass.ds(t, 1), :].rearrange("p a b -> p (a b)")
                        dve.tensor_scalar(tn[u][:, :], xt, mean[:, bass.ds(t, 1)], rstd[:, bass.ds(t, 1)], ALU.subtract, ALU.mult).then_inc(tn_done, 1)
                    in_pairs(dve, NT, norm)

                    def wide(col):
                        return col[:, :, None].to_broadcast((P, NT, NE))
                    index = eighth[:, None, :].to_broadcast((P, NT, NE))
                    dve.wait_ge(logit_done, NT)
                    logit = logit_ps[:, 0:NT * NE].rearrange("p (t e) -> p t e", e=NE)
                    chain.then(dve.tensor_reduce(top[0][:, :], logit, AX.X, ALU.max))
                    dve.tensor_tensor(rest[:, :, :], logit, wide(top[0]), ALU.subtract).then_inc(shifted, 1)
                    dve.wait_ge(powered, 1)
                    chain.then(dve.tensor_reduce(top[0][:, :], prob[:, :, :], AX.X, ALU.add))
                    chain.then(dve.reciprocal(top[0][:, :], top[0][:, :]))
                    chain.then(dve.tensor_tensor(prob[:, :, :], prob[:, :, :], wide(top[0]), ALU.mult))
                    dve.wait_ge(pool_ready, 1)
                    left = prob
                    for n in range(TOPK):
                        chain.then(dve.tensor_reduce(top[n][:, :], left[:, :, :], AX.X, ALU.max))
                        chain.then(dve.tensor_tensor(pick[n][:, :, :], left[:, :, :], wide(top[n]), ALU.is_equal))
                        chain.then(dve.tensor_tensor(pick[n][:, :, :], pick[n][:, :, :], index, ALU.mult))
                        chain.then(dve.tensor_reduce(top[2][:, :], pick[n][:, :, :], AX.X, ALU.max))
                        chain.then(dve.tensor_tensor(pick[n][:, :, :], index, wide(top[2]), ALU.is_equal))
                        if n == 0:
                            chain.then(dve.scalar_tensor_tensor(rest[:, :, :].rearrange("p t e -> p (t e)"), pick[0][:, :, :].rearrange("p t e -> p (t e)"), -2.0,
                                                                prob[:, :, :].rearrange("p t e -> p (t e)"), ALU.mult, ALU.add))
                            left = rest
                    chain.then(dve.tensor_tensor(top[2][:, :], top[0][:, :], top[1][:, :], ALU.add))
                    chain.then(dve.tensor_scalar(top[2][:, :], top[2][:, :], 1e-12, None, ALU.max))
                    chain.then(dve.reciprocal(top[2][:, :], top[2][:, :]))
                    chain.then(dve.tensor_tensor(pick[0][:, :, :], pick[0][:, :, :], pick[1][:, :, :], ALU.add))
                    chain.then(dve.tensor_tensor(pick[0][:, :, :], pick[0][:, :, :], prob[:, :, :], ALU.mult))
                    dve.tensor_tensor(comb[:, :, :], pick[0][:, :, :], wide(top[2]), ALU.mult).then_inc(comb_done, 1)

            with nc.Block() as block, ExitStack() as c:
                cbc = [sb(f"cbc{u}", [P, NE, CH], F32, c) for u in range(2)]
                crow = [sb(f"crow{u}", [P, CH], F32, c) for u in range(2)]
                g_s = [sb(f"g_s{m}", [P, CH], F32, c) for m in range(4)]
                gs = [sb(f"gs{m}", [P, CH], F32, c) for m in range(4)]
                oT = sb("oT", [P, 2, CH], F32, c)
                hps = [c.enter_context(nc.psum_tensor(f"hps{m}", [P, CH], F32)) for m in range(4)]
                acc = [c.enter_context(nc.psum_tensor(f"acc{d}", [P, CH], F32)) for d in range(2)]
                fps = [c.enter_context(nc.psum_tensor(f"fps{n}", [P, 2, D], F32)) for n in range(2)]

                def esem(name):
                    return c.enter_context(nc.semaphore(name))
                c_in = [esem(f"c_in{u}") for u in range(2)]
                crow_zero, h_done, g_done, gs_done, e_done = esem("crow_zero"), esem("h_done"), esem("g_done"), esem("gs_done"), esem("e_done")
                oT_done, f_done, x_done = esem("oT_done"), esem("f_done"), esem("x_done3")
                out_in = esem("out_in")
                FULL = NPAD // CH
                LASTW = NPAD - FULL * CH
                U = 2 * NE

                def chunks(eng, body):
                    in_pairs(eng, FULL, lambda n, u, k: body(n, u, k, CH))
                    body(FULL, FULL % 2, FULL // 2, LASTW)

                @block.sync
                def _(sp):
                    sp.wait_ge(crow_zero, 1)

                    def load(n, u, k, w):
                        since(sp, e_done, U * (n - 1))
                        sp.dma_start(crow[u][0:NE, 0:w], comb_rows[:, bass.ds(n * CH, w)]).then_inc(c_in[u], 16)
                        sp.dma_start(cbc[u][:, :, 0:w], comb_rows[:, bass.ds(n * CH, w)][None, :, :].to_broadcast((P, NE, w))).then_inc(c_in[u], 16)
                    chunks(sp, load)

                @block.gpsimd
                def _(pool):
                    def store(n, u, k, w):
                        pool.wait_ge(x_done, n + 1)
                        pool.dma_start(out.rearrange("(t p) d -> p t d", p=P)[:, bass.ds(n * (CH // P), w // P), :],
                                       X[:, bass.ds(n * (CH // P), w // P), :]).then_inc(out_in, 16)
                    chunks(pool, store)
                    pool.wait_ge(out_in, 16 * (FULL + 1))

                @block.scalar
                def _(act):
                    def body(n, u, k, w):
                        for e in range(NE):
                            for m in range(2):
                                i = U * n + 2 * e + m
                                s = (2 * e + m) % 4
                                act.wait_ge(h_done, i + 1)
                                since(act, gs_done, i - 3)
                                act.activation(g_s[s][:, 0:w], hps[s][:, 0:w], ACT.Gelu, bias=b1_s[:, e, m:m + 1]).then_inc(g_done, 1)
                            if e == 1 and (not isinstance(n, int) or n > 0):
                                take(n - 1, CH)

                    def take(n, w):
                        act.wait_ge(e_done, U * (n + 1))
                        since(act, f_done, n)
                        for d in range(2):
                            last = act.copy(oT[:, d, 0:w], acc[d][:, 0:w])
                        last.then_inc(oT_done, 1)
                    chunks(act, body)
                    take(FULL, LASTW)

                @block.tensor
                def _(pe):
                    def up(n, u, k, w, e):
                        for m in range(2):
                            i = U * n + 2 * e + m
                            s = (2 * e + m) % 4
                            since(pe, g_done, i - 3)
                            for kk in range(2):
                                last = pe.matmul(hps[s][:, 0:w], w1_s[:, e, kk, m * P:(m + 1) * P], tT[:, kk, bass.ds(n * CH, w)],
                                                 start=(kk == 0), stop=(kk == 1))
                            last.then_inc(h_done, 1)

                    def down(n, u, k, w, e):
                        if e == 0:
                            pe.wait_ge(c_in[u], 32 * (k + 1))
                            since(pe, oT_done, n)
                            for d in range(2):
                                pe.matmul(acc[d][:, 0:w], b2_s[:, d * P:(d + 1) * P], crow[u][:, 0:w], start=True, stop=False)
                        for m in range(2):
                            i = U * n + 2 * e + m
                            pe.wait_ge(gs_done, i + 1)
                            for d in range(2):
                                last = pe.matmul(acc[d][:, 0:w], w2_s[:, e, m, d * P:(d + 1) * P], gs[(2 * e + m) % 4][:, 0:w],
                                                 start=False, stop=(e == NE - 1 and m == 1))
                            last.then_inc(e_done, 1)

                    def finish(n, w):
                        pe.wait_ge(oT_done, n + 1)
                        since(pe, x_done, n)
                        for t in range(w // P):
                            for d in range(2):
                                last = pe.transpose(fps[t // 2][:, t % 2, d * P:(d + 1) * P], oT[:, d, t * P:(t + 1) * P], ident[:, :])
                        last.then_inc(f_done, 1)

                    def body(n, u, k, w):
                        started = not isinstance(n, int) or n > 0
                        for e in range(NE):
                            up(n, u, k, w, e)
                            if e >= 2:
                                down(n, u, k, w, e - 2)
                            if e == 4 and started:
                                finish(n - 1, CH)
                        for e in (NE - 2, NE - 1):
                            down(n, u, k, w, e)
                    chunks(pe, body)
                    finish(FULL, LASTW)

                @block.vector
                def _(dve):
                    for u in range(2):
                        last = dve.memset(crow[u][:, :], 0.0)
                    last.then_inc(crow_zero, 1)

                    def body(n, u, k, w):
                        dve.wait_ge(c_in[u], 32 * (k + 1))
                        for e in range(NE):
                            for m in range(2):
                                i = U * n + 2 * e + m
                                s = (2 * e + m) % 4
                                dve.wait_ge(g_done, i + 1)
                                since(dve, e_done, i - 3)
                                dve.tensor_tensor(gs[s][:, 0:w], g_s[s][:, 0:w], cbc[u][:, e, 0:w], ALU.mult).then_inc(gs_done, 1)
                            if e == 4 and (not isinstance(n, int) or n > 0):
                                add(n - 1, CH)

                    def add(n, w):
                        dve.wait_ge(f_done, n + 1)
                        for h in range(-(-w // (2 * P))):
                            tiles = min(2, w // P - 2 * h)
                            xt = X[:, bass.ds(n * (CH // P) + 2 * h, tiles), :]
                            last = dve.tensor_tensor(xt, fps[h][:, 0:tiles, :], xt, ALU.add)
                        last.then_inc(x_done, 1)
                    chunks(dve, body)
                    add(FULL, LASTW)


def kernel(x, src, dst, edge_attr_4, edge_attr_8, node_vec1, L0_gnn_W_sc0, L0_gnn_W_sc1, L0_gnn_W_lin1_0,
           L0_gnn_W_lin1_1, L0_gnn_fc_w0, L0_gnn_fc_w1, L0_gnn_W_lin2_0, L0_gnn_W_lin2_1, L0_ffn_router_w,
           L0_ffn_w1, L0_ffn_b1, L0_ffn_w2, L0_ffn_b2):
    import concourse.bacc as bacc
    from concourse.bass_utils import run_bass_kernel_spmd

    def padded(a, rows, value=0):
        a = np.asarray(a)
        out = np.full((rows,) + a.shape[1:], value, a.dtype)
        out[:a.shape[0]] = a
        return out

    def by_tile(a):
        a = a.reshape((NG, SUBS, P, QS) + a.shape[1:])
        return np.moveaxis(a, 2, 1)

    dst_pad = padded(dst, EPAD, N - 1)
    dst_nat = padded(dst_pad, EPAD + GROUP, NPAD)
    starts = dst_nat[:EPAD + WIN:WIN]
    e8 = padded(edge_attr_8, EPAD).reshape(NG, 2, 2, P, QS, NB)
    arrays = {
        "x": padded(x, NPAD),
        "z": np.ascontiguousarray(padded(node_vec1, NPAD).reshape(NT, P).T),
        "src": np.ascontiguousarray(by_tile(padded(src, EPAD)).reshape(NG, P, GT)),
        "dst": np.ascontiguousarray(np.moveaxis(by_tile(dst_pad), 0, 1).reshape(P, NG * GT)),
        "dst_nat": dst_nat,
        "firsts": np.stack([starts[:-1].reshape(NG, SUBS), starts[1:].reshape(NG, SUBS)], axis=1),
        "sh": np.ascontiguousarray(by_tile(padded(edge_attr_4, EPAD)).reshape(NG, P, GT * 4)),
        "e8": np.ascontiguousarray(e8.transpose(0, 1, 2, 5, 4, 3).reshape(NG, 2, 2 * NB, WIN)),
        "w_sc0": L0_gnn_W_sc0, "w_sc1": L0_gnn_W_sc1, "w_l10": L0_gnn_W_lin1_0, "w_l11": L0_gnn_W_lin1_1,
        "fc0": L0_gnn_fc_w0, "fc1": L0_gnn_fc_w1, "w_l20": L0_gnn_W_lin2_0, "w_l21": L0_gnn_W_lin2_1,
        "router_t": np.ascontiguousarray(np.asarray(L0_ffn_router_w).T),
        "w1": L0_ffn_w1, "b1": np.asarray(L0_ffn_b1).reshape(NE, 2, P).transpose(2, 0, 1), "w2": L0_ffn_w2, "b2": L0_ffn_b2,
    }
    arrays = {k: np.ascontiguousarray(v) for k, v in arrays.items()}
    nc = bacc.Bacc("TRN2", target_bir_lowering=False, num_devices=1)
    aps = {k: nc.dram_tensor(f"in_{k}", a.shape, mybir.dt.from_np(a.dtype), kind="ExternalInput").ap() for k, a in arrays.items()}
    out = nc.dram_tensor("out_0", (NPAD, D), F32, kind="ExternalOutput").ap()
    gnn_moe(nc, **aps, out=out)
    r = run_bass_kernel_spmd(nc, [{f"in_{k}": a for k, a in arrays.items()}], core_ids=[0])
    return r.results[0]["out_0"][:N]
```

```python
from contextlib import ExitStack

import numpy as np

import concourse.bass as bass
from concourse import mybir

F32 = mybir.dt.float32
F32R = mybir.dt.float32r
I32 = mybir.dt.int32
U32 = mybir.dt.uint32
ALU = mybir.AluOpType
ACT = mybir.ActivationFunctionType
AX = mybir.AxisListType

P = 128
N, E = 6250, 200000
MUL, NB, RN = 64, 8, 64
D = 4 * MUL
Y = 2 * D
NT = -(-N // P)
NPAD = NT * P
SUBS, QS = 4, 4
WIN = QS * P
GROUP = SUBS * WIN
GT = SUBS * QS
NG = -(-E // GROUP)
EPAD = NG * GROUP
RANKS = P // SUBS
NE, TOPK = 8, 2
CH = 512
EPS = 1e-5
HIGH = -(1 << 12)
SKIP = 1.0e6

C_S = float(np.float32(np.sin(np.pi / 8.0)))
C_X = float(np.float32(np.cos(np.pi / 8.0)))
INV_M = 1.0 / np.sqrt(MUL)
OUT_SCALE = float(C_X / np.sqrt(2 * MUL) / np.sqrt(16.0) / np.sqrt(RN))
INV_SQRT3 = float(1.0 / np.sqrt(3.0))


def since(eng, sem, value):
    if not isinstance(value, int) or value > 0:
        eng.wait_ge(sem, value)


def in_pairs(eng, count, body):
    body(0, 0, 0)
    body(1, 1, 0)
    with eng.Fori(1, count // 2) as i:
        body(2 * i, 0, i)
        body(2 * i + 1, 1, i)
    if count % 2:
        body(count - 1, 0, count // 2)


class Chain:

    def __init__(self, eng, sem):
        self.eng, self.sem, self.count = eng, sem, 0

    def then(self, ins):
        self.count += 1
        ins.then_inc(self.sem, 1)
        self.eng.wait_ge(self.sem, self.count)


def gnn_moe(nc, x, z, src, dst, dst_nat, firsts, sh, e8, w_sc0, w_sc1, w_l10, w_l11, fc0, fc1, w_l20, w_l21,
            router_t, w1, b1, w2, b2, out):
    h_table = nc.dram_tensor("h_table", (NPAD, D), F32, kind="Internal").ap()
    y_sums = nc.dram_tensor("y_sums", (NPAD + RANKS, Y), F32, kind="Internal").ap()
    t_cols = nc.dram_tensor("t_cols", (2, P, NPAD), F32, kind="Internal").ap()
    comb_rows = nc.dram_tensor("comb_rows", (NE, NPAD), F32, kind="Internal").ap()

    with ExitStack() as whole:
        def sb(name, shape, dt=F32, ctx=whole):
            return ctx.enter_context(nc.sbuf_tensor(name, shape, dt))

        windows = ExitStack()
        X = sb("X", [P, NT, D])
        zcol = sb("zcol", [P, NT])
        ident = sb("ident", [P, P])
        ones = sb("ones", [P, P])
        mean = sb("mean", [P, NT])
        rstd = sb("rstd", [P, NT])
        eps_col = sb("eps_col", [P, 1])
        riota = sb("riota", [P, SUBS, RANKS], ctx=windows)
        neg_base = sb("neg_base", [P, NG, SUBS], ctx=windows)
        neg_ncol = sb("neg_ncol", [P, NG], ctx=windows)
        rank = sb("rank", [P, NG * GT], ctx=windows)
        dst_i = sb("dst_i", [P, NG * GT], I32, ctx=windows)
        bases = sb("bases", [1, NG, SUBS], I32, windows)
        flag = sb("flag", [1, 1], I32, windows)

        def stats_to_rstd(dve, st, tmp, chain, sqrt_in, sqrt_out):
            m1, q1, m2, q2 = st[:, :, 1], st[:, :, 2], st[:, :, 4], st[:, :, 5]
            chain.then(dve.tensor_tensor(mean[:, :], m1, m2, ALU.add))
            chain.then(dve.tensor_tensor(tmp[:, :], m1, m2, ALU.subtract))
            chain.then(dve.tensor_scalar(mean[:, :], mean[:, :], 0.5, None, ALU.mult))
            chain.then(dve.scalar_tensor_tensor(tmp[:, :], tmp[:, :], D / 4.0, tmp[:, :], ALU.mult, ALU.mult))
            chain.then(dve.tensor_tensor(tmp[:, :], tmp[:, :], q1, ALU.add))
            dve.tensor_tensor(tmp[:, :], tmp[:, :], q2, ALU.add).then_inc(sqrt_in, 1)
            dve.wait_ge(sqrt_out, 1)
            chain.then(dve.reciprocal(rstd[:, :], rstd[:, :]))

        with ExitStack() as c1:
            def s1(name, shape, dt=F32):
                return sb(name, shape, dt, c1)

            def sem(name):
                return c1.enter_context(nc.semaphore(name))

            CHUNKS, PER = 7, NT // 7
            st = s1("st", [P, NT, 6])
            tmp = s1("tmp", [P, NT])
            wlin = s1("wlin", [P, 2, 2 * P])
            xn = [s1(f"xn{u}", [P, 4, MUL]) for u in range(2)]
            xnT = [s1(f"xnT{u}", [P, 2 * P]) for u in range(2)]
            hrow = [s1(f"hrow{u}", [P, 2, P]) for u in range(2)]
            z_h = s1("z_h", [P, NT])
            z_s = s1("z_s", [P, NT])
            dst_a = s1("dst_a", [NG, GROUP + 1], I32)
            diff = s1("diff", [NG, GROUP])
            base_i = s1("base_i", [P, 2, SUBS], I32)
            base_f = s1("base_f", [P, 2, SUBS])
            bad = s1("bad", [P, 4])
            diag = s1("diag", [P, NG, SUBS])
            spread = s1("spread", [P, SUBS, RANKS])
            rcol = s1("rcol", [P, 1])
            bad_f = s1("bad_f", [1, 1])

            tps = [c1.enter_context(nc.psum_tensor(f"tps{u}", [P, 512], F32)) for u in range(2)]
            lin_ps, sc_ps = ([c1.enter_context(nc.psum_tensor(f"{name}{u}", [P, 512], F32)) for u in range(2)] for name in ("lin_ps", "sc_ps"))
            base_ps = c1.enter_context(nc.psum_tensor("base_ps", [P, 512], F32))
            col_ps = c1.enter_context(nc.psum_tensor("col_ps", [P, 512], F32))

            x_in = [sem(f"x_in{c}") for c in range(CHUNKS)]
            w_in, z_in, dst_in = sem("w_in"), sem("z_in"), sem("dst_in")
            w_zero, pool_const = sem("w_zero"), sem("pool_const")
            pool_step = sem("pool_step")
            dve_step, var_ready, std_ready = sem("dve_step"), sem("var_ready"), sem("std_ready")
            const_ready, z_ready = sem("const_ready"), sem("z_ready")
            xn_ready, tr_ready, xnT_ready, lin_ready = sem("xn_ready"), sem("tr_ready"), sem("xnT_ready"), sem("lin_ready")
            h_ready, x_done = sem("h_ready"), sem("x_done")
            h_out = [sem(f"h_out{u}") for u in range(2)]
            spread_ready, spread_ps, bad_ready = sem("spread_ready"), sem("spread_ps"), sem("bad_ready")

            with nc.Block() as block:
                @block.sync
                def _(sp):
                    sp.dma_start(dst_a[:, :], bass.AP(dst_nat.tensor, 0, [[GROUP, NG], [1, GROUP + 1]])).then_inc(dst_in, 16)
                    sp.dma_start(dst_i[:, :], dst).then_inc(dst_in, 16)
                    sp.dma_start(base_i[0:NG, :, :], firsts).then_inc(dst_in, 16)
                    sp.dma_start(bases[:, :, :], firsts[:, 0, :][None, :, :]).then_inc(dst_in, 16)

                    xt = x.rearrange("(t p) d -> p t d", p=P)
                    for c in range(CHUNKS):
                        sp.dma_start(X[:, c * PER:(c + 1) * PER, :], xt[:, c * PER:(c + 1) * PER, :]).then_inc(x_in[c], 16)
                    def store(t, u, _k):
                        sp.wait_ge(h_ready, t + 1)
                        sp.dma_start(h_table[bass.ds(t * P, P), :], hrow[u][:, :, :].rearrange("p a b -> p (a b)")).then_inc(h_out[u], 16)
                    in_pairs(sp, NT, store)
                    sp.wait_ge(h_out[0], 16 * (NT - NT // 2))
                    sp.wait_ge(h_out[1], 16 * (NT // 2))

                @block.gpsimd
                def _(pool):
                    chain = Chain(pool, pool_step)
                    pool.memset(wlin[:, :, :], 0.0).then_inc(w_zero, 1)
                    chain.then(pool.memset(ident[:, :], 0.0))
                    pool.memset(ones[:, :], 1.0)
                    chain.then(pool.affine_select(out=ident[:, :], in_=ident[:, :], compare_op=ALU.not_equal, fill=1.0,
                                                  base=0, pattern=[[-1, P]], channel_multiplier=1))
                    chain.then(pool.iota(riota[:, :, :], [[0, SUBS], [1, RANKS]], base=0, channel_multiplier=0,
                                         allow_small_or_imprecise_dtypes=True))
                    for j in range(SUBS):
                        chain.then(pool.iota(rcol[j * RANKS:(j + 1) * RANKS, :], [[1, 1]], base=0, channel_multiplier=1,
                                             allow_small_or_imprecise_dtypes=True))
                    pool.sem_inc(pool_const, 1)

                @block.scalar
                def _(act):
                    act.dma_start(zcol[:, :], z).then_inc(z_in, 16)
                    act.wait_ge(w_zero, 1)
                    for b, (top, bottom) in enumerate((((w_l10, w_sc0), (w_l11, w_sc1)), ((w_l11, w_sc1), (w_l11, w_sc1)))):
                        for half, ws in enumerate((top, bottom)):
                            for k, w in enumerate(ws):
                                lo = k * P + half * MUL
                                act.dma_start(wlin[half * MUL:(half + 1) * MUL, b, lo:lo + MUL], w).then_inc(w_in, 16)
                    act.wait_ge(const_ready, 1)
                    act.wait_ge(var_ready, 1)
                    act.activation(rstd[:, :], tmp[:, :], ACT.Sqrt, bias=eps_col[:, 0:1], scale=1.0 / D).then_inc(std_ready, 1)

                    def h_of(t, u, k):
                        act.wait_ge(lin_ready, t + 1)
                        since(act, h_out[u], 16 * k)
                        act.activation(hrow[u][:, :, :], lin_ps[u][:, 0:2 * P].rearrange("p (a b) -> p a b", a=2), ACT.Copy,
                                       scale=z_h[:, bass.ds(t, 1)]).then_inc(h_ready, 1)

                    def body(t, u, k):
                        act.wait_ge(tr_ready, t + 1)
                        since(act, lin_ready, t - 1)
                        act.copy(xnT[u][:, :], tps[u][:, 0:2 * P]).then_inc(xnT_ready, 1)
                        if not isinstance(t, int) or t > 1:
                            h_of(t - 2, u, k - 1)
                    act.wait_ge(z_ready, 2)
                    in_pairs(act, NT, body)
                    h_of(NT - 2, 1, NT // 2 - 1)
                    h_of(NT - 1, 0, NT // 2)

                @block.tensor
                def _(pe):
                    pe.wait_ge(pool_const, 1)
                    pe.wait_ge(spread_ready, 1)
                    pe.matmul(base_ps[:, 0:NG * SUBS], ones[:, :], diag[:, :, :], start=True, stop=True)
                    pe.matmul(col_ps[:, 0:NG], spread[:, :, :], ident[:, 0:NG], start=True, stop=True)
                    pe.wait_ge(bad_ready, 1)
                    pe.matmul(base_ps[0:1, 511:512], bad[:, 2:3], ones[:, 0:1], start=True, stop=True).then_inc(spread_ps, 1)

                    pe.wait_ge(w_in, 16 * 8)

                    def lin(t, u):
                        pe.wait_ge(xnT_ready, t + 1)
                        since(pe, h_ready, t - 1)
                        since(pe, x_done, t - 1)
                        for k, to in enumerate((lin_ps, sc_ps)):
                            for b in range(2):
                                last = pe.matmul(to[u][:, b * P:(b + 1) * P], xnT[u][:, b * P:(b + 1) * P], wlin[:, b, k * P:(k + 1) * P],
                                                 start=True, stop=True)
                        last.then_inc(lin_ready, 1)

                    def body(t, u, k):
                        pe.wait_ge(xn_ready, t + 1)
                        since(pe, xnT_ready, t - 1)
                        for b in range(2):
                            last = pe.transpose(tps[u][:, b * P:(b + 1) * P], xn[u][:, 2 * b:2 * b + 2, :], ident[:, :])
                        last.then_inc(tr_ready, 1)
                        if not isinstance(t, int) or t > 0:
                            lin(t - 1, 1 - u)
                    in_pairs(pe, NT, body)
                    lin(NT - 1, 0)

                @block.vector
                def _(dve):
                    chain = Chain(dve, dve_step)
                    dve.memset(eps_col[:, :], EPS).then_inc(const_ready, 1)
                    dve.wait_ge(z_in, 16)
                    dve.tensor_scalar(z_h[:, :], zcol[:, :], INV_M, None, ALU.mult).then_inc(z_ready, 1)
                    dve.tensor_scalar(z_s[:, :], zcol[:, :], INV_M * C_S, None, ALU.mult).then_inc(z_ready, 1)
                    chain.then(dve.memset(bad[:, :], 0.0))
                    dve.wait_ge(dst_in, 16 * 4)
                    chain.then(dve.memset(base_f[:, :, :], 0.0))
                    chain.then(dve.tensor_copy(base_f[0:NG, :, :], base_i[0:NG, :, :]))
                    chain.then(dve.memset(base_f[0:1, 0, 0:1], 0.0))
                    chain.then(dve.tensor_tensor(diff[:, :], dst_a[:, 1:GROUP + 1], dst_a[:, 0:GROUP], ALU.subtract))
                    chain.then(dve.tensor_reduce(bad[0:NG, 0:1], diff[:, :], AX.X, ALU.min))
                    chain.then(dve.tensor_tensor(diff[:, 0:SUBS], base_f[0:NG, 1, :], base_f[0:NG, 0, :], ALU.subtract))
                    chain.then(dve.tensor_reduce(bad[0:NG, 1:2], diff[:, 0:SUBS], AX.X, ALU.max))
                    chain.then(dve.tensor_scalar(bad[:, 0:1], bad[:, 0:1], 0.0, None, ALU.is_lt))
                    chain.then(dve.tensor_scalar(bad[:, 1:2], bad[:, 1:2], float(RANKS - 1), None, ALU.is_gt))
                    dve.tensor_tensor(bad[:, 2:3], bad[:, 0:1], bad[:, 1:2], ALU.add).then_inc(bad_ready, 1)
                    dve.wait_ge(pool_const, 1)
                    dve.tensor_tensor(diag[:, :, :], ident[:, 0:NG, None].to_broadcast((P, NG, SUBS)),
                                      base_f[:, 0:1, :].to_broadcast((P, NG, SUBS)), ALU.mult)
                    dve.tensor_copy(spread[:, :, :], base_f[:, 0, :, None].to_broadcast((P, SUBS, RANKS))).then_inc(spread_ready, 1)
                    dve.wait_ge(spread_ps, 1)
                    chain.then(dve.tensor_scalar(neg_base[:, :, :].rearrange("p g j -> p (g j)"), base_ps[:, 0:NG * SUBS], -1.0, None, ALU.mult))
                    chain.then(dve.tensor_scalar(neg_ncol[:, :], col_ps[:, 0:NG], rcol[:, 0:1], -1.0, ALU.add, ALU.mult))
                    chain.then(dve.tensor_tensor(rank[:, :].rearrange("p (w q) -> p w q", q=QS), dst_i[:, :].rearrange("p (w q) -> p w q", q=QS),
                                                 neg_base[:, :, :].rearrange("p g j -> p (g j)")[:, :, None].to_broadcast((P, NG * SUBS, QS)), ALU.add))
                    chain.then(dve.tensor_scalar(flag[:, :], base_ps[0:1, 511:512], 0.0, None, ALU.is_gt))

                    for c in range(CHUNKS):
                        dve.wait_ge(x_in[c], 16)
                        for t in range(c * PER, (c + 1) * PER):
                            last = dve.bn_stats(st[:, t, :], X[:, t, :])
                    chain.then(last)
                    stats_to_rstd(dve, st, tmp, chain, var_ready, std_ready)

                    def residual(t, u):
                        dve.wait_ge(lin_ready, t + 1)
                        xt = X[:, bass.ds(t, 1), :].rearrange("p a b -> p (a b)")
                        x0, x1 = xt[:, 0:MUL], xt[:, MUL:D].rearrange("p (v c) -> p c v", c=3)
                        s = sc_ps[u][:, 0:D].rearrange("p (c v) -> p c v", c=4)
                        dve.scalar_tensor_tensor(x0, s[:, 0, :], z_s[:, bass.ds(t, 1)], x0, ALU.mult, ALU.add)
                        dve.scalar_tensor_tensor(x1, s[:, 1:4, :], z_s[:, bass.ds(t, 1)], x1,
                                                 ALU.mult, ALU.add).then_inc(x_done, 1)

                    def body(t, u, k):
                        since(dve, tr_ready, t - 1)
                        xt = X[:, bass.ds(t, 1), :].rearrange("p a b -> p (a b)")
                        m, r = mean[:, bass.ds(t, 1)], rstd[:, bass.ds(t, 1)]
                        dve.tensor_scalar(xn[u][:, 0, :], xt[:, 0:MUL], m, r, ALU.subtract, ALU.mult)
                        dve.tensor_scalar(xn[u][:, 1:4, :], xt[:, MUL:D].rearrange("p (v c) -> p c v", c=3), m, r,
                                          ALU.subtract, ALU.mult).then_inc(xn_ready, 1)
                        if not isinstance(t, int) or t > 1:
                            residual(t - 2, u)
                    in_pairs(dve, NT, body)
                    residual(NT - 2, 1)
                    residual(NT - 1, 0)

        with ExitStack() as c2:
            def s2(name, shape, dt=F32):
                return sb(name, shape, dt, c2)

            def sem(name):
                return c2.enter_context(nc.semaphore(name))

            fc0_s = s2("fc0_s", [P, P])
            fc1_s = s2("fc1_s", [P, 2, D])
            e8_s = [s2(f"e8_s{v}", [P, 2, WIN]) for v in range(2)]
            src_s = [s2(f"src_s{v}", [P, GT], I32) for v in range(2)]
            sh_s = [s2(f"sh_s{v}", [P, GT, 4]) for v in range(2)]
            hid = [[s2(f"hid{v}{h}", [P, WIN]) for h in range(2)] for v in range(2)]
            xs = [s2(f"xs{v}", [P, QS, SUBS, D]) for v in range(2)]
            mid = [s2(f"mid{k}", [P, SUBS, Y]) for k in range(4)]
            eq = s2("eq", [P, GT, RANKS])
            sel = [s2(f"sel{v}", [P, GT, 4, RANKS]) for v in range(2)]
            same = [s2(f"same{v}", [P, SUBS, RANKS]) for v in range(2)]
            carry = [s2(f"carry{v}", [P, RANKS]) for v in range(2)]
            part = [s2(f"part{v}", [P, Y]) for v in range(2)]
            total = [s2(f"total{v}", [P, Y]) for v in range(2)]
            row_s = [s2(f"row_s{v}", [P, 1], U32) for v in range(2)]
            before = s2("before", [P, P])
            first = s2("first", [P, 2])

            w_ps = [[c2.enter_context(nc.psum_tensor(f"w_ps{k}{h}", [P, 2, D], F32)) for h in range(2)] for k in range(2)]
            y_ps = [c2.enter_context(nc.psum_tensor(f"y_ps{v}", [P, Y], F32)) for v in range(2)]
            hid_ps = c2.enter_context(nc.psum_tensor("hid_ps", [P, WIN], F32))
            t_ps = c2.enter_context(nc.psum_tensor("t_ps", [P, Y], F32))

            pool_went_on, g_went_on = sem("pool_went_on"), sem("g_went_on")
            zero_done, fc_in, fc_zero, before_done = sem("zero_done"), sem("fc_in"), sem("fc_zero"), sem("before_done")
            e8_in = [sem(f"e8_in{v}") for v in range(2)]
            src_in = [sem(f"src_in{v}") for v in range(2)]
            sh_in = [sem(f"sh_in{v}") for v in range(2)]
            xs_in = [[sem(f"xs_in{v}{q}") for q in range(QS)] for v in range(2)]
            hid_done, hid_ready, w_done = sem("hid_done"), sem("hid_ready"), sem("w_done")
            eq_done, sel_done, mid_done, seg_done = sem("eq_done"), sem("sel_done"), sem("mid_done"), sem("seg_done")
            same_done, y_done, part_done, t_done, total_done = sem("same_done"), sem("y_done"), sem("part_done"), sem("t_done"), sem("total_done")
            y_out = sem("y_out")
            g_cleared, g_in, g_src, g_gather, g_old, g_put = sem("g_cleared"), sem("g_in"), sem("g_src"), sem("g_gather"), sem("g_old"), sem("g_put")
            g_hid, g_silu, g_w, g_sel, g_row, g_sum, g_new, g_dve, g_zero = (
                sem("g_hid"), sem("g_silu"), sem("g_w"), sem("g_sel"), sem("g_row"), sem("g_sum"), sem("g_new"), sem("g_dve"), sem("g_zero"))

            def products(dve, w, x_row, m):
                wk = w.rearrange("p (f k u) -> p f k u", f=2, k=2)
                mk = m.rearrange("p (b u) -> p b u", u=MUL)
                dve.tensor_tensor(mk[:, 0:8:7, :], wk[:, 0, :, :], x_row[:, None, 0:MUL].to_broadcast((P, 2, MUL)), ALU.mult)
                return dve.tensor_tensor(mk[:, 1:7, :].rearrange("p (k c) u -> p k c u", k=2), wk[:, 1, :, None, :].to_broadcast((P, 2, 3, MUL)),
                                         x_row[:, MUL:D].rearrange("p (c u) -> p c u", c=3)[:, None, :, :].to_broadcast((P, 2, 3, MUL)), ALU.mult)

            def segment(pe, acc, lhs, m, first):
                to = acc.rearrange("p (b u) -> p b u", u=MUL)
                yield lambda: pe.matmul(to[:, 0:8:2, :], lhs(0), m[:, 0:D], start=first, stop=False, skip_group_check=True)
                for c in range(1, 4):
                    moving = m[:, D:Y].rearrange("p (b u) -> p b u", u=MUL)[:, c - 1:4:4 - c, :]
                    yield lambda c=c, moving=moving: pe.matmul(to[:, 1:2 * c + 2:2 * c, :], lhs(c), moving, start=False, stop=False, skip_group_check=True)

            with nc.Block() as block:
                @block.sync
                def _(sp):
                    sp.wait_ge(fc_zero, 4)
                    for h in range(2):
                        sp.dma_start(fc0_s[h * NB:(h + 1) * NB, h * RN:(h + 1) * RN], fc0).then_inc(fc_in, 16)
                        sp.dma_start(fc1_s[h * RN:(h + 1) * RN, h, :], fc1).then_inc(fc_in, 16)
                    bad = sp.value_load(flag[0:1, 0:1], min_val=0, max_val=1)
                    with sp.If(bad == 0):
                        def load(g, v, k):
                            if k is not None:
                                sp.wait_ge(hid_done, 2 * (g - 1))
                            sp.dma_start(e8_s[v][0:2 * NB, :, :], e8[bass.ds(g, 1), :, :, :].rearrange("g h f e -> f (g h) e")).then_inc(e8_in[v], 16)
                            if k is not None:
                                for q in range(QS):
                                    sp.wait_ge(xs_in[v][q], 16 * SUBS * k)
                            sp.dma_start(src_s[v][:, :], src[bass.ds(g, 1), :, :].rearrange("g p t -> (g p) t")).then_inc(src_in[v], 16)
                            if k is not None:
                                sp.wait_ge(sel_done, g - 1)
                            sp.dma_start(sh_s[v][:, :, :].rearrange("p t c -> p (t c)"), sh[bass.ds(g, 1), :, :].rearrange("g p t -> (g p) t")).then_inc(sh_in[v], 16)

                        def store(g, v):
                            sp.wait_ge(total_done, g + 1)
                            for j in range(SUBS):
                                if isinstance(g, int) and g == 0 and j == 0:
                                    node = 0
                                else:
                                    node = sp.value_load(bases[0:1, bass.ds(g, 1), j:j + 1].rearrange("a g j -> a (g j)"), min_val=0, max_val=N - 1)
                                    sp.wait_ge(y_out, 16 * (SUBS * g + j))
                                sp.dma_start(y_sums[bass.ds(node, RANKS), :], total[v][j * RANKS:(j + 1) * RANKS, :]).then_inc(y_out, 16)
                        load(0, 0, None)
                        load(1, 1, None)
                        load(2, 0, 1)
                        load(3, 1, 1)
                        store(0, 0)
                        with sp.Fori(2, NG // 2) as i:
                            load(2 * i, 0, i)
                            store(2 * i - 3, 1)
                            load(2 * i + 1, 1, i)
                            store(2 * i - 2, 0)
                        for g in range(NG - 3, NG):
                            store(g, g % 2)
                        sp.wait_ge(y_out, 16 * SUBS * NG)
                    with sp.Else():
                        sp.wait_ge(g_zero, 1)
                        with sp.Fori(0, NT) as t:
                            sp.dma_start(y_sums[bass.ds(t * P, P), :], total[0][:, :]).then_inc(g_cleared, 16)
                        sp.dma_start(y_sums[NPAD:NPAD + RANKS, :], total[0][0:RANKS, :]).then_inc(g_cleared, 16)
                        sp.wait_ge(g_cleared, 16 * (NT + 1))
                        with sp.Fori(0, NG) as g:
                            for j in range(SUBS):
                                for q in range(QS):
                                    s = g * GT + j * QS + q
                                    sp.dma_start(e8_s[0][0:NB, 0, 0:P], e8[bass.ds(g, 1), j // 2, (j % 2) * NB:(j % 2 + 1) * NB, q * P:(q + 1) * P].rearrange("g f e -> (g f) e")).then_inc(g_in, 16)
                                    with nc.allow_non_contiguous_dma(reason="one index a partition"):
                                        sp.dma_start(src_s[0][:, 0:1], src[bass.ds(g, 1), :, j * QS + q:j * QS + q + 1].rearrange("g p t -> (g p) t")).then_inc(g_src, 16)
                                    sp.dma_start(sh_s[0][:, 0, :], sh[bass.ds(g, 1), :, (j * QS + q) * 4:(j * QS + q) * 4 + 4].rearrange("g p t -> (g p) t")).then_inc(g_src, 16)
                                    sp.wait_ge(g_put, 16 * (s + 1))
                                    sp.sem_inc(g_went_on, 1)

                @block.gpsimd
                def _(pool):
                    pool.affine_select(out=before[:, :], in_=ones[:, :], compare_op=ALU.is_gt, fill=0.0,
                                       base=0, pattern=[[-1, P]], channel_multiplier=1).then_inc(before_done, 1)
                    def hold(sem, value):
                        pool.wait_ge(sem, value)
                        pool.sem_inc(pool_went_on, 1)

                    bad = pool.value_load(flag[0:1, 0:1], min_val=0, max_val=1)
                    with pool.If(bad == 0):
                        def gather(g, v, k):
                            hold(src_in[v], 16 * (k + 1))
                            for q in range(QS):
                                if not isinstance(g, int) or g >= 2:
                                    hold(mid_done, 4 * (g - 2) + q + 1)
                                for j in range(SUBS):
                                    t = j * QS + q
                                    pool.indirect_dma_start(xs[v][:, q, j, :], None, h_table,
                                                            bass.IndirectOffsetOnAxis(ap=src_s[v][:, t:t + 1], axis=0)).then_inc(xs_in[v][q], 16)
                        gather(0, 0, 0)
                        gather(1, 1, 0)
                        with pool.Fori(1, NG // 2) as i:
                            gather(2 * i, 0, i)
                            gather(2 * i + 1, 1, i)
                    with pool.Else():
                        with pool.Fori(0, NG * GT) as s:
                            hold(g_src, 32 * (s + 1))
                            pool.indirect_dma_start(xs[0][:, 0, 0, :], None, h_table,
                                                    bass.IndirectOffsetOnAxis(ap=src_s[0][:, 0:1], axis=0)).then_inc(g_gather, 16)
                            hold(g_row, 2 * (s + 1))
                            hold(g_gather, 16 * (s + 1))
                            pool.indirect_dma_start(total[1][:, :], None, y_sums,
                                                    bass.IndirectOffsetOnAxis(ap=row_s[0][:, 0:1], axis=0)).then_inc(g_old, 16)
                            hold(g_new, s + 1)
                            pool.indirect_dma_start(y_sums, bass.IndirectOffsetOnAxis(ap=row_s[1][:, 0:1], axis=0), total[0][:, :], None,
                                                    bounds_check=NPAD - 1, oob_is_err=False).then_inc(g_put, 16)
                        pool.wait_ge(g_put, 16 * NG * GT)

                @block.scalar
                def _(act):
                    bad = act.value_load(flag[0:1, 0:1], min_val=0, max_val=1)
                    with act.If(bad == 0):
                        def silu(g, v, h):
                            act.wait_ge(hid_done, 2 * g + h + 1)
                            since(act, w_done, 4 * (g - 1))
                            act.activation(hid[v][h][:, :], hid_ps[:, :], ACT.Silu, scale=float(1.0 / np.sqrt(NB))).then_inc(hid_ready, 1)

                        def take_part(g, v):
                            act.wait_ge(y_done, g + 1)
                            since(act, t_done, g - 1)
                            act.copy(part[v][:, :], y_ps[v][:, :]).then_inc(part_done, 1)

                        def take_total(g, v):
                            act.wait_ge(t_done, g + 1)
                            since(act, y_out, 16 * SUBS * (g - 1))
                            act.copy(total[v][:, :], t_ps[:, :]).then_inc(total_done, 1)

                        def body(g, v, k, last=False):
                            started = not isinstance(g, int) or g > 0
                            if started:
                                take_part(g - 1, 1 - v)
                            if not last:
                                silu(g + 1, 1 - v, 0)
                            if started:
                                take_total(g - 1, 1 - v)
                            if not last:
                                silu(g + 1, 1 - v, 1)
                        silu(0, 0, 0)
                        silu(0, 0, 1)
                        body(0, 0, 0)
                        body(1, 1, 0)
                        with act.Fori(1, NG // 2 - 1) as i:
                            body(2 * i, 0, i)
                            body(2 * i + 1, 1, i)
                        body(NG - 2, 0, NG // 2 - 1)
                        body(NG - 1, 1, NG // 2 - 1, last=True)
                        take_part(NG - 1, 1)
                        take_total(NG - 1, 1)
                    with act.Else():
                        with act.Fori(0, NG * GT) as s:
                            act.wait_ge(g_hid, s + 1)
                            act.activation(hid[0][0][:, 0:P], hid_ps[:, 0:P], ACT.Silu, scale=float(1.0 / np.sqrt(NB))).then_inc(g_silu, 1)

                @block.tensor
                def _(pe):
                    pe.wait_ge(fc_in, 16 * 4)
                    bad = pe.value_load(flag[0:1, 0:1], min_val=0, max_val=1)
                    with pe.If(bad == 0):
                        def first_layer(g, v, k, h):
                            pe.wait_ge(e8_in[v], 16 * (k + 1))
                            since(pe, hid_ready, 2 * g + h)
                            pe.matmul(hid_ps[:, :], fc0_s[:, :], e8_s[v][:, h, :], start=True, stop=True).then_inc(hid_done, 1)

                        def second_layer(g, v, q):
                            if q == 0:
                                pe.wait_ge(hid_ready, 2 * g + 2)
                            since(pe, mid_done, 4 * g + q - 1)
                            for h in range(2):
                                last = pe.matmul(w_ps[q % 2][h][:, :, :], hid[v][h][:, q * P:(q + 1) * P], fc1_s[:, :, :], start=True, stop=True)
                            last.then_inc(w_done, 1)

                        def sum_up(g, v, q):
                            pe.wait_ge(mid_done, 4 * g + q + 1)
                            if q == 0:
                                pe.wait_ge(sel_done, g + 1)
                                since(pe, part_done, g - 1)
                            parts = [list(segment(pe, y_ps[v][j * RANKS:(j + 1) * RANKS, :],
                                                  lambda c, t=j * QS + q: sel[v][:, t, c, :], mid[q][:, j, :], q == 0)) for j in range(SUBS)]
                            for c in range(4):
                                for j in range(SUBS):
                                    last = parts[j][c]()
                            last.then_inc(seg_done, 1)

                        def hand_over(g, v):
                            since(pe, part_done, g)
                            since(pe, same_done, g)
                            pe.matmul(y_ps[v][0:RANKS, :], carry[1 - v][:, :], part[1 - v][:, :], start=False, stop=True,
                                      skip_group_check=True).then_inc(y_done, 1)

                        def merge(g, v):
                            pe.wait_ge(part_done, g + 1)
                            pe.wait_ge(same_done, g + 1)
                            since(pe, total_done, g)
                            pe.matmul(t_ps[:, :], same[v][:, :, :], part[v][:, :], start=True, stop=True).then_inc(t_done, 1)

                        def body(g, v, k, last=False):
                            started = not isinstance(g, int) or g > 0
                            for q in range(QS):
                                second_layer(g, v, q)
                                if q > 0:
                                    sum_up(g, v, q - 1)
                                elif started:
                                    sum_up(g - 1, 1 - v, QS - 1)
                                    hand_over(g - 1, 1 - v)
                                if q == 2 and started:
                                    merge(g - 1, 1 - v)
                                if q % 2 and not last:
                                    first_layer(g + 1, 1 - v, k + v, q // 2)
                        first_layer(0, 0, 0, 0)
                        first_layer(0, 0, 0, 1)
                        pe.wait_ge(zero_done, 1)
                        body(0, 0, 0)
                        body(1, 1, 0)
                        with pe.Fori(1, NG // 2 - 1) as i:
                            body(2 * i, 0, i)
                            body(2 * i + 1, 1, i)
                        body(NG - 2, 0, NG // 2 - 1)
                        body(NG - 1, 1, NG // 2 - 1, last=True)
                        sum_up(NG - 1, 1, QS - 1)
                        hand_over(NG - 1, 1)
                        merge(NG - 1, 1)
                    with pe.Else():
                        with pe.Fori(0, NG * GT) as s:
                            pe.wait_ge(g_in, 16 * (s + 1))
                            pe.matmul(hid_ps[:, 0:P], fc0_s[:, :], e8_s[0][:, 0, 0:P], start=True, stop=True).then_inc(g_hid, 1)
                            pe.wait_ge(g_silu, s + 1)
                            pe.matmul(w_ps[0][0][:, :, :], hid[0][0][:, 0:P], fc1_s[:, :, :], start=True, stop=True).then_inc(g_w, 1)
                            pe.wait_ge(g_sel, 3 * s + 1)
                            pe.transpose(t_ps[:, 0:P], same[0][:, :, :], ident[:, :]).then_inc(g_sum, 1)
                            pe.wait_ge(g_sel, 3 * s + 3)
                            parts = list(segment(pe, y_ps[0][:, :], lambda c: sel[0][:, c, :, :].rearrange("p a r -> p (a r)"), mid[0][:, 0, :], True))
                            for p in parts:
                                last = p()
                            last.then_inc(g_sum, 1)

                @block.vector
                def _(dve):
                    dve.memset(fc0_s[:, :], 0.0).then_inc(fc_zero, 1)
                    dve.memset(fc1_s[:, :, :], 0.0).then_inc(fc_zero, 1)
                    dve.memset(e8_s[0][:, :, :], 0.0).then_inc(fc_zero, 1)
                    dve.memset(e8_s[1][:, :, :], 0.0).then_inc(fc_zero, 1)
                    dve.memset(part[1][:, :], 0.0)
                    dve.memset(carry[0][:, :], 0.0)
                    dve.memset(carry[1][:, :], 0.0).then_inc(zero_done, 1)
                    dve.memset(total[0][:, :], 0.0).then_inc(g_zero, 1)
                    dve.wait_ge(zero_done, 1)
                    bad = dve.value_load(flag[0:1, 0:1], min_val=0, max_val=1)
                    with dve.If(bad == 0):
                        def select(g, v, k):
                            dve.wait_ge(sh_in[v], 16 * (k + 1))
                            since(dve, seg_done, 4 * (g - 1))
                            dve.tensor_tensor(eq[:, :, :], riota[:, 0:1, :].to_broadcast((P, GT, RANKS)),
                                              rank[:, bass.ds(g * GT, GT)][:, :, None].to_broadcast((P, GT, RANKS)), ALU.is_equal).then_inc(eq_done, 1)
                            dve.wait_ge(eq_done, g + 1)
                            dve.tensor_tensor(sel[v][:, :, :, :], eq[:, :, None, :].to_broadcast((P, GT, 4, RANKS)),
                                              sh_s[v][:, :, :, None].to_broadcast((P, GT, 4, RANKS)), ALU.mult).then_inc(sel_done, 1)

                        def share(g, v, last):
                            since(dve, t_done, g - 1)
                            since(dve, y_done, g)
                            if not last:
                                dve.scalar_tensor_tensor(carry[v][:, 0:1], neg_ncol[:, bass.ds(g, 1)], 0.0, neg_base[:, bass.ds(g + 1, 1), 0:1].rearrange("p g j -> p (g j)"),
                                                         ALU.add, ALU.is_equal)
                            dve.scalar_tensor_tensor(same[v][:, :, :], riota[:, :, :], neg_ncol[:, bass.ds(g, 1)],
                                                     neg_base[:, bass.ds(g, 1), :].rearrange("p g j -> p (g j)")[:, :, None].to_broadcast((P, SUBS, RANKS)),
                                                     ALU.add, ALU.is_equal).then_inc(same_done, 1)

                        def messages(g, v, k, q):
                            dve.wait_ge(w_done, 4 * g + q + 1)
                            dve.wait_ge(xs_in[v][q], 16 * SUBS * (k + 1))
                            since(dve, seg_done, 4 * (g - 1) + q + 1)
                            for j in range(SUBS):
                                last = products(dve, w_ps[q % 2][j // 2][:, j % 2, :], xs[v][:, q, j, :], mid[q][:, j, :])
                            last.then_inc(mid_done, 1)

                        def body(g, v, k, last=False):
                            select(g, v, k)
                            for q in range(QS):
                                messages(g, v, k, q)
                                if q == 1:
                                    share(g, v, last)
                        body(0, 0, 0)
                        body(1, 1, 0)
                        with dve.Fori(1, NG // 2 - 1) as i:
                            body(2 * i, 0, i)
                            body(2 * i + 1, 1, i)
                        body(NG - 2, 0, NG // 2 - 1)
                        body(NG - 1, 1, NG // 2 - 1, last=True)
                    with dve.Else():
                        with dve.Fori(0, NG * GT) as s:
                            def step(n, ins):
                                ins.then_inc(g_dve, 1)
                                dve.wait_ge(g_dve, s * 4 + n)
                            dst_col = rank[:, bass.ds(s, 1)]
                            dve.wait_ge(g_src, 32 * (s + 1))
                            step(1, dve.tensor_scalar(dst_col, dst_i[:, bass.ds(s, 1)], 1.0, None, ALU.mult))
                            dve.tensor_scalar(same[0][:, :, :].rearrange("p j r -> p (j r)"), dst_col.to_broadcast((P, P)), 1.0, None, ALU.mult).then_inc(g_sel, 1)
                            dve.tensor_scalar(row_s[0][:, :], dst_col, 1.0, None, ALU.mult).then_inc(g_row, 1)
                            dve.wait_ge(g_sum, 2 * s + 1)
                            eqm = eq[:, 0:4, :].rearrange("p a b -> p (a b)")
                            step(2, dve.tensor_scalar(eqm, t_ps[:, 0:P], dst_col, None, ALU.is_equal))
                            for c in range(4):
                                last = dve.tensor_scalar(sel[0][:, c, :, :], eq[:, 0:4, :], sh_s[0][:, 0, c:c + 1], None, ALU.mult)
                            last.then_inc(g_sel, 1)
                            dve.wait_ge(before_done, 1)
                            step(3, dve.scalar_tensor_tensor(eq[:, 4:8, :].rearrange("p a b -> p (a b)"), eqm, 1.0, before[:, :], ALU.mult, ALU.mult,
                                                             accum_out=first[:, 0:1]))
                            step(4, dve.tensor_scalar(first[:, 1:2], first[:, 0:1], SKIP, dst_col, ALU.mult, ALU.add))
                            dve.tensor_copy(row_s[1][:, :], first[:, 1:2]).then_inc(g_row, 1)
                            dve.wait_ge(g_w, s + 1)
                            dve.wait_ge(g_gather, 16 * (s + 1))
                            products(dve, w_ps[0][0][:, 0, :], xs[0][:, 0, 0, :], mid[0][:, 0, :]).then_inc(g_sel, 1)
                            dve.wait_ge(g_sum, 2 * s + 2)
                            dve.wait_ge(g_old, 16 * (s + 1))
                            dve.tensor_tensor(total[0][:, :], total[1][:, :], y_ps[0][:, :], ALU.add).then_inc(g_new, 1)

        windows.close()

        with ExitStack() as c3:
            def s3(name, shape, dt=F32):
                return sb(name, shape, dt, c3)

            def sem(name):
                return c3.enter_context(nc.semaphore(name))

            wl2 = s3("wl2", [P, 2, MUL])
            router_s = s3("router_s", [P, 2, NE])
            w_hi = s3("w_hi", [P, NE, 2, 2, D], F32R)
            w_lo = s3("w_lo", [P, NE, 2, 2, D], F32R)
            b1_s = s3("b1_s", [P, NE, 2])
            b2_s = s3("b2_s", [P, D])
            eighth = s3("eighth", [P, NE])

            x_in = [sem(f"y_in{u}") for u in range(2)]
            stage_in = [sem(f"stage_in{u}") for u in range(2)]
            t_out = [sem(f"t_out{u}") for u in range(2)]
            split_step = sem("split_step")
            wl_in, wl_ready, w_in, b2_zero = sem("wl_in"), sem("wl_ready"), sem("w_in3"), sem("b2_zero")
            tr_done, tr_taken, o_done, o_taken = sem("tr_done"), sem("tr_taken"), sem("o_done"), sem("o_taken")
            var_ready, std_ready, dve_step, pool_ready = sem("var_ready3"), sem("std_ready3"), sem("dve_step3"), sem("pool_ready")
            tn_done, tp_done, tp_taken, kept, logit_done = sem("tn_done"), sem("tp_done"), sem("tp_taken"), sem("kept"), sem("logit_done")
            shifted, powered, comb_done, combT_ps, combT_done, comb_out = (
                sem("shifted"), sem("powered"), sem("comb_done"), sem("combT_ps"), sem("combT_done"), sem("comb_out"))
            with nc.Block() as block, ExitStack() as c:
                yb = [sb(f"yb{u}", [P, Y], F32, c) for u in range(2)]
                yT = [sb(f"yT{u}", [P, Y], F32, c) for u in range(2)]
                tn = [sb(f"tn{u}", [P, D], F32, c) for u in range(2)]
                tnT = [sb(f"tnT{u}", [P, 2, P], F32, c) for u in range(2)]
                st = sb("st3", [P, NT, 6], F32, c)
                tmp = sb("tmp3", [P, NT], F32, c)
                prob, rest, comb = (sb(name, [P, NT, NE], F32, c) for name in ("prob", "rest", "comb"))
                pick = [sb(f"pick{n}", [P, NT, NE], F32, c) for n in range(2)]
                top = [sb(f"top{n}", [P, NT], F32, c) for n in range(3)]
                stage = [sb(f"stage{u}", [P, 2, 2, D], F32, c) for u in range(2)]
                scaled, scaled_less = (sb(name, [P, 2, 2, D], F32, c) for name in ("scaled", "scaled_less"))
                combT = sb("combT", [P, -(-NT // 16), P], F32, c)
                tps = [c.enter_context(nc.psum_tensor(f"ytp{u}", [P, Y], F32)) for u in range(2)]
                ops = [c.enter_context(nc.psum_tensor(f"yop{u}", [P, 512], F32)) for u in range(2)]
                logit_ps = c.enter_context(nc.psum_tensor("logit_ps", [P, 512], F32))
                ct_ps = c.enter_context(nc.psum_tensor("ct_ps", [P, 512], F32))
                LW = -(-NT // 16)

                @block.sync
                def _(sp):
                    def load(t, u, k):
                        since(sp, tr_done, t - 1)
                        sp.dma_start(yb[u][:, :], y_sums[bass.ds(t * P, P), :]).then_inc(x_in[u], 16)
                    in_pairs(sp, NT, load)
                    sp.dma_start(b1_s[:, :, :], b1).then_inc(w_in, 16)
                    sp.wait_ge(b2_zero, 1)
                    sp.dma_start(b2_s[0:NE, :], b2).then_inc(w_in, 16)
                    def keep(t, u, k):
                        sp.wait_ge(tp_taken, t + 1)
                        sp.dma_start(t_cols.rearrange("k p n -> p k n")[:, :, bass.ds(t * P, P)], tnT[u][:, :, :]).then_inc(t_out[u], 16)
                    in_pairs(sp, NT, keep)
                    sp.wait_ge(combT_done, 1)
                    for b in range(LW):
                        tiles = min(16, NT - 16 * b)
                        sp.dma_start(comb_rows.rearrange("e (t p) -> t e p", p=P)[16 * b:16 * b + tiles, :, :], combT[0:tiles * NE, b, :]).then_inc(comb_out, 16)
                    sp.wait_ge(comb_out, 16 * LW)
                    sp.wait_ge(w_in, 32)
                    sp.wait_ge(t_out[0], 16 * (NT - NT // 2))
                    sp.wait_ge(t_out[1], 16 * (NT // 2))

                @block.gpsimd
                def _(pool):
                    pool.iota(eighth[:, :], [[-1, NE]], base=NE, channel_multiplier=0, allow_small_or_imprecise_dtypes=True).then_inc(pool_ready, 1)

                    chain = Chain(pool, split_step)

                    def load(e):
                        for which, w in enumerate((w1, w2)):
                            pool.dma_start(stage[e % 2][:, which, :, :], w[e].rearrange("(k p) n -> p k n", p=P)).then_inc(stage_in[e % 2], 16)
                    load(0)
                    load(1)
                    for e in range(NE):
                        pool.wait_ge(stage_in[e % 2], 32 * (e // 2 + 1))
                        whole_w = stage[e % 2][:, :, :, :].rearrange("p w k n -> p (w k n)")
                        times = scaled[:, :, :, :].rearrange("p w k n -> p (w k n)")
                        less = scaled_less[:, :, :, :].rearrange("p w k n -> p (w k n)")
                        hi = w_hi[:, e, :, :, :].rearrange("p w k n -> p (w k n)")
                        chain.then(pool.tensor_scalar(times, whole_w, float(1 - HIGH), None, ALU.mult))
                        chain.then(pool.tensor_tensor(less, times, whole_w, ALU.subtract))
                        chain.then(pool.tensor_tensor(hi, times, less, ALU.subtract))
                        chain.then(pool.tensor_tensor(w_lo[:, e, :, :, :].rearrange("p w k n -> p (w k n)"), whole_w, hi.bitcast(F32), ALU.subtract))
                        if e + 2 < NE:
                            load(e + 2)

                    def body(t, u, k):
                        pool.wait_ge(tn_done, t + 1)
                        xt = X[:, bass.ds(t, 1), :].rearrange("p a b -> p (a b)")
                        pool.tensor_tensor(xt, xt, tn[u][:, :], ALU.add).then_inc(kept, 1)
                    in_pairs(pool, NT, body)

                @block.scalar
                def _(act):
                    act.dma_start(wl2[:, 0, :], w_l20).then_inc(wl_in, 16)
                    for h in range(2):
                        act.dma_start(wl2[(1 - h) * MUL:(2 - h) * MUL, 1, :], w_l21[h * MUL:(h + 1) * MUL, :]).then_inc(wl_in, 16)
                    act.dma_start(router_s[:, :, :], router_t.rearrange("(k p) e -> p k e", p=P)).then_inc(wl_in, 16)
                    act.wait_ge(wl_in, 64)
                    act.mul(wl2[0:MUL, 0, :], wl2[0:MUL, 0, :], OUT_SCALE)
                    act.mul(wl2[MUL:P, 0, :], wl2[MUL:P, 0, :], OUT_SCALE * INV_SQRT3)
                    act.mul(wl2[:, 1, :], wl2[:, 1, :], OUT_SCALE).then_inc(wl_ready, 1)

                    def take(t, u, k):
                        act.wait_ge(tr_done, t + 1)
                        since(act, o_done, t - 1)
                        act.copy(yT[u][:, :], tps[u][:, :]).then_inc(tr_taken, 1)
                    in_pairs(act, NT, take)
                    act.wait_ge(var_ready, 1)
                    act.activation(rstd[:, :], tmp[:, :], ACT.Sqrt, bias=eps_col[:, 0:1], scale=1.0 / D).then_inc(std_ready, 1)

                    def keep(t, u, k):
                        act.wait_ge(tp_done, t + 1)
                        since(act, t_out[u], 16 * k)
                        since(act, logit_done, t - 1)
                        act.copy(tnT[u][:, :, :], ops[u][:, 0:D].rearrange("p (k n) -> p k n", k=2)).then_inc(tp_taken, 1)
                    in_pairs(act, NT, keep)
                    act.wait_ge(shifted, 1)
                    act.activation(prob[:, :, :], rest[:, :, :], ACT.Exp).then_inc(powered, 1)
                    act.wait_ge(combT_ps, 1)
                    act.copy(combT[:, :, :], ct_ps[:, 0:LW * P].rearrange("p (b n) -> p b n", b=LW)).then_inc(combT_done, 1)

                @block.tensor
                def _(pe):
                    pe.wait_ge(wl_ready, 1)

                    def lin2(t, u):
                        pe.wait_ge(tr_taken, t + 1)
                        since(pe, o_taken, t - 1)
                        pe.matmul(ops[u][:, 0:MUL], yT[u][:, 0:P], wl2[:, 0, :], start=True, stop=True)
                        for c in range(3):
                            last = pe.matmul(ops[u][:, MUL + c:D:3], yT[u][:, (c + 1) * P:(c + 2) * P], wl2[:, 1, :], start=True, stop=True)
                        last.then_inc(o_done, 1)

                    def turn(t, u, k):
                        pe.wait_ge(x_in[u], 16 * (k + 1))
                        since(pe, tr_taken, t - 1)
                        for b in range(4):
                            last = pe.transpose(tps[u][:, b * P:(b + 1) * P], yb[u][:, b * P:(b + 1) * P], ident[:, :])
                        last.then_inc(tr_done, 1)
                        if not isinstance(t, int) or t > 0:
                            lin2(t - 1, 1 - u)
                    in_pairs(pe, NT, turn)
                    lin2(NT - 1, 0)

                    def logits(t, u):
                        pe.wait_ge(tp_taken, t + 1)
                        for k in range(2):
                            last = pe.matmul(logit_ps[:, bass.ds(t * NE, NE)], tnT[u][:, k, :], router_s[:, k, :], start=(k == 0), stop=(k == 1))
                        last.then_inc(logit_done, 1)

                    def turn_back(t, u, k):
                        pe.wait_ge(tn_done, t + 1)
                        if isinstance(t, int) and t < 2:
                            pe.wait_ge(o_taken, NT)
                        since(pe, tp_taken, t - 1)
                        for b in range(2):
                            last = pe.transpose(ops[u][:, b * P:(b + 1) * P], tn[u][:, b * P:(b + 1) * P], ident[:, :])
                        last.then_inc(tp_done, 1)
                        if not isinstance(t, int) or t > 0:
                            logits(t - 1, 1 - u)
                    in_pairs(pe, NT, turn_back)
                    logits(NT - 1, 0)

                    pe.wait_ge(comb_done, 1)
                    for b in range(LW):
                        tiles = min(16, NT - 16 * b)
                        last = pe.transpose(ct_ps[0:tiles * NE, b * P:(b + 1) * P], comb[:, 16 * b:16 * b + tiles, :], ident[:, :])
                    last.then_inc(combT_ps, 1)

                @block.vector
                def _(dve):
                    chain = Chain(dve, dve_step)
                    dve.memset(b2_s[:, :], 0.0).then_inc(b2_zero, 1)
                    dve.memset(ct_ps[:, :], 0.0)

                    def residual(t, u, k):
                        dve.wait_ge(o_done, t + 1)
                        xt = X[:, bass.ds(t, 1), :].rearrange("p a b -> p (a b)")
                        dve.scalar_tensor_tensor(xt, ops[u][:, 0:D], zcol[:, bass.ds(t, 1)], xt, ALU.mult, ALU.add).then_inc(o_taken, 1)
                        if not isinstance(t, int) or t > 0:
                            stats(t - 1)

                    def stats(t):
                        dve.wait_ge(o_taken, t + 1)
                        dve.bn_stats(st[:, bass.ds(t, 1), :].rearrange("p a b -> p (a b)"), X[:, bass.ds(t, 1), :].rearrange("p a b -> p (a b)"))
                    in_pairs(dve, NT, residual)
                    stats(NT - 1)
                    chain.then(dve.memset(rest[:, :, :], 0.0))
                    stats_to_rstd(dve, st, tmp, chain, var_ready, std_ready)

                    def norm(t, u, k):
                        since(dve, tp_done, t - 1)
                        since(dve, kept, t - 1)
                        xt = X[:, bass.ds(t, 1), :].rearrange("p a b -> p (a b)")
                        dve.tensor_scalar(tn[u][:, :], xt, mean[:, bass.ds(t, 1)], rstd[:, bass.ds(t, 1)], ALU.subtract, ALU.mult).then_inc(tn_done, 1)
                    in_pairs(dve, NT, norm)

                    def wide(col):
                        return col[:, :, None].to_broadcast((P, NT, NE))
                    index = eighth[:, None, :].to_broadcast((P, NT, NE))
                    dve.wait_ge(logit_done, NT)
                    logit = logit_ps[:, 0:NT * NE].rearrange("p (t e) -> p t e", e=NE)
                    chain.then(dve.tensor_reduce(top[0][:, :], logit, AX.X, ALU.max))
                    dve.tensor_tensor(rest[:, :, :], logit, wide(top[0]), ALU.subtract).then_inc(shifted, 1)
                    dve.wait_ge(powered, 1)
                    chain.then(dve.tensor_reduce(top[0][:, :], prob[:, :, :], AX.X, ALU.add))
                    chain.then(dve.reciprocal(top[0][:, :], top[0][:, :]))
                    chain.then(dve.tensor_tensor(prob[:, :, :], prob[:, :, :], wide(top[0]), ALU.mult))
                    dve.wait_ge(pool_ready, 1)
                    left = prob
                    for n in range(TOPK):
                        chain.then(dve.tensor_reduce(top[n][:, :], left[:, :, :], AX.X, ALU.max))
                        chain.then(dve.tensor_tensor(pick[n][:, :, :], left[:, :, :], wide(top[n]), ALU.is_equal))
                        chain.then(dve.tensor_tensor(pick[n][:, :, :], pick[n][:, :, :], index, ALU.mult))
                        chain.then(dve.tensor_reduce(top[2][:, :], pick[n][:, :, :], AX.X, ALU.max))
                        chain.then(dve.tensor_tensor(pick[n][:, :, :], index, wide(top[2]), ALU.is_equal))
                        if n == 0:
                            chain.then(dve.scalar_tensor_tensor(rest[:, :, :].rearrange("p t e -> p (t e)"), pick[0][:, :, :].rearrange("p t e -> p (t e)"), -2.0,
                                                                prob[:, :, :].rearrange("p t e -> p (t e)"), ALU.mult, ALU.add))
                            left = rest
                    chain.then(dve.tensor_tensor(top[2][:, :], top[0][:, :], top[1][:, :], ALU.add))
                    chain.then(dve.tensor_scalar(top[2][:, :], top[2][:, :], 1e-12, None, ALU.max))
                    chain.then(dve.reciprocal(top[2][:, :], top[2][:, :]))
                    chain.then(dve.tensor_tensor(pick[0][:, :, :], pick[0][:, :, :], pick[1][:, :, :], ALU.add))
                    chain.then(dve.tensor_tensor(pick[0][:, :, :], pick[0][:, :, :], prob[:, :, :], ALU.mult))
                    dve.tensor_tensor(comb[:, :, :], pick[0][:, :, :], wide(top[2]), ALU.mult).then_inc(comb_done, 1)

            with nc.Block() as block, ExitStack() as c:
                HE = NE // 2
                cbc = [sb(f"cbc{h}", [P, HE, CH], F32, c) for h in range(2)]
                crow = [sb(f"crow{u}", [P, CH], F32, c) for u in range(2)]
                t_f = [sb(f"t_f{u}", [P, 2, CH], F32, c) for u in range(2)]
                t_up = sb("t_up", [P, 2, CH], F32, c)
                t_hi = [sb(f"t_hi{u}", [P, 2, CH], F32R, c) for u in range(2)]
                t_lo = [sb(f"t_lo{u}", [P, 2, CH], F32R, c) for u in range(2)]
                g_s = [sb(f"g_s{m}", [P, CH], F32, c) for m in range(4)]
                g_c = [sb(f"g_c{m}", [P, CH], F32, c) for m in range(2)]
                g_up = [sb(f"g_up{m}", [P, CH], F32, c) for m in range(2)]
                g_hi = [sb(f"g_hi{m}", [P, CH], F32R, c) for m in range(4)]
                g_lo = [sb(f"g_lo{m}", [P, CH], F32R, c) for m in range(4)]
                oT = sb("oT", [P, 2, CH], F32, c)
                hps = [c.enter_context(nc.psum_tensor(f"hps{m}", [P, CH], F32)) for m in range(4)]
                acc = [c.enter_context(nc.psum_tensor(f"acc{d}", [P, CH], F32)) for d in range(2)]
                fps = [c.enter_context(nc.psum_tensor(f"fps{n}", [P, 2, D], F32)) for n in range(2)]

                def esem(name):
                    return c.enter_context(nc.semaphore(name))
                t_in = [esem(f"t_in{u}") for u in range(2)]
                crow_in = [esem(f"crow_in{u}") for u in range(2)]
                c_in = [esem(f"c_in{h}") for h in range(2)]
                t_up_done, t_hi_done, t_lo_done = esem("t_up_done"), esem("t_hi_done"), esem("t_lo_done")
                crow_zero, h_done, g_done, e_done = esem("crow_zero"), esem("h_done"), esem("g_done"), esem("e_done")
                g_c_done, g_up_done, g_hi_done, g_lo_done = esem("g_c_done"), esem("g_up_done"), esem("g_hi_done"), esem("g_lo_done")
                oT_done, f_done, x_done = esem("oT_done"), esem("f_done"), esem("x_done3")
                out_in = esem("out_in")
                FULL = NPAD // CH
                LASTW = NPAD - FULL * CH
                U = 2 * NE

                def chunks(eng, body):
                    def full(n, u, k, after=CH):
                        body(n, u, k, CH, after)
                    full(0, 0, 0)
                    full(1, 1, 0)
                    with eng.Fori(1, FULL // 2 - 1) as i:
                        full(2 * i, 0, i)
                        full(2 * i + 1, 1, i)
                    full(FULL - 2, 0, FULL // 2 - 1)
                    full(FULL - 1, 1, FULL // 2 - 1, LASTW)
                    body(FULL, 0, FULL // 2, LASTW, 0)

                @block.sync
                def _(sp):
                    sp.wait_ge(crow_zero, 1)

                    def load(n, u, k, w, _after):
                        since(sp, t_lo_done, n - 1)
                        sp.dma_start(t_f[u][:, :, 0:w], t_cols.rearrange("k p n -> p k n")[:, :, bass.ds(n * CH, w)]).then_inc(t_in[u], 16)
                        since(sp, e_done, U * (n - 1))
                        sp.dma_start(crow[u][0:NE, 0:w], comb_rows[:, bass.ds(n * CH, w)]).then_inc(crow_in[u], 16)
                        for h in range(2):
                            since(sp, g_c_done, U * (n - 1) + (h + 1) * 2 * HE)
                            sp.dma_start(cbc[h][:, :, 0:w], comb_rows[h * HE:(h + 1) * HE, bass.ds(n * CH, w)][None, :, :].to_broadcast((P, HE, w))).then_inc(c_in[h], 16)
                    chunks(sp, load)

                @block.gpsimd
                def _(pool):
                    def store(n, u, k, w, _after):
                        pool.wait_ge(x_done, n + 1)
                        pool.dma_start(out.rearrange("(t p) d -> p t d", p=P)[:, bass.ds(n * (CH // P), w // P), :],
                                       X[:, bass.ds(n * (CH // P), w // P), :]).then_inc(out_in, 16)
                    chunks(pool, store)
                    pool.wait_ge(out_in, 16 * (FULL + 1))

                @block.scalar
                def _(act):
                    def upper_t(n, u, w):
                        act.wait_ge(t_up_done, n + 1)
                        since(act, h_done, U * (n - 1))
                        act.copy(t_hi[u][:, :, 0:w], t_up[:, :, 0:w]).then_inc(t_hi_done, 1)

                    def upper_g(i, s, w):
                        act.wait_ge(g_up_done, i + 1)
                        since(act, e_done, i - 3)
                        act.copy(g_hi[s][:, 0:w], g_up[s % 2][:, 0:w]).then_inc(g_hi_done, 1)

                    def body(n, u, k, w, after):
                        for b in range(U):
                            i, s = U * n + b, b % 4
                            act.wait_ge(h_done, i + 1)
                            since(act, g_c_done, i - 3)
                            act.activation(g_s[s][:, 0:w], hps[s][:, 0:w], ACT.Gelu, bias=b1_s[:, b // 2, b % 2:b % 2 + 1]).then_inc(g_done, 1)
                            if b >= 2:
                                upper_g(i - 2, (b - 2) % 4, w)
                            elif not isinstance(n, int) or n > 0:
                                upper_g(i - 2, (b - 2) % 4, CH)
                            if b == 5 and (not isinstance(n, int) or n > 0):
                                take(n - 1, CH)
                            if b == 9 and after:
                                upper_t(n + 1, 1 - u, after)

                    def take(n, w):
                        act.wait_ge(e_done, U * (n + 1))
                        since(act, f_done, n)
                        for d in range(2):
                            last = act.copy(oT[:, d, 0:w], acc[d][:, 0:w])
                        last.then_inc(oT_done, 1)
                    upper_t(0, 0, CH)
                    chunks(act, body)
                    for b in (U - 2, U - 1):
                        upper_g(U * FULL + b, b % 4, LASTW)
                    take(FULL, LASTW)

                @block.tensor
                def _(pe):
                    def split_product(to, w_part, hi, lo, first, last):
                        pe.matmul(to, w_part(w_hi), hi, start=first, stop=False)
                        pe.matmul(to, w_part(w_hi), lo, start=False, stop=False)
                        return pe.matmul(to, w_part(w_lo), hi, start=False, stop=last)

                    def up(n, u, w, e):
                        if e == 0:
                            pe.wait_ge(t_hi_done, n + 1)
                            pe.wait_ge(t_lo_done, n + 1)
                        for m in range(2):
                            i = U * n + 2 * e + m
                            s = (2 * e + m) % 4
                            since(pe, g_done, i - 3)
                            for kk in range(2):
                                last = split_product(hps[s][:, 0:w], lambda part, kk=kk, m=m: part[:, e, 0, kk, m * P:(m + 1) * P],
                                                     t_hi[u][:, kk, 0:w], t_lo[u][:, kk, 0:w], kk == 0, kk == 1)
                            last.then_inc(h_done, 1)

                    def down(n, u, k, w, e):
                        if e == 0:
                            pe.wait_ge(crow_in[u], 16 * (k + 1))
                            since(pe, oT_done, n)
                            for d in range(2):
                                pe.matmul(acc[d][:, 0:w], b2_s[:, d * P:(d + 1) * P], crow[u][:, 0:w], start=True, stop=False)
                        for m in range(2):
                            i = U * n + 2 * e + m
                            s = (2 * e + m) % 4
                            pe.wait_ge(g_lo_done, i + 1)
                            pe.wait_ge(g_hi_done, i + 1)
                            for d in range(2):
                                last = split_product(acc[d][:, 0:w], lambda part, d=d, m=m: part[:, e, 1, m, d * P:(d + 1) * P],
                                                     g_hi[s][:, 0:w], g_lo[s][:, 0:w], False, e == NE - 1 and m == 1)
                            last.then_inc(e_done, 1)

                    def finish(n, w):
                        pe.wait_ge(oT_done, n + 1)
                        since(pe, x_done, n)
                        for t in range(w // P):
                            for d in range(2):
                                last = pe.transpose(fps[t // 2][:, t % 2, d * P:(d + 1) * P], oT[:, d, t * P:(t + 1) * P], ident[:, :])
                        last.then_inc(f_done, 1)

                    def body(n, u, k, w, _after):
                        started = not isinstance(n, int) or n > 0
                        for e in range(NE):
                            up(n, u, w, e)
                            if e >= 2:
                                down(n, u, k, w, e - 2)
                            elif started:
                                down(n - 1, 1 - u, k - 1 + u, CH, NE - 2 + e)
                            if e == 5 and started:
                                finish(n - 1, CH)
                    chunks(pe, body)
                    for e in (NE - 2, NE - 1):
                        down(FULL, 0, FULL // 2, LASTW, e)
                    finish(FULL, LASTW)

                @block.vector
                def _(dve):
                    for u in range(2):
                        last = dve.memset(crow[u][:, :], 0.0)
                    last.then_inc(crow_zero, 1)

                    def split_t(n, u, k, w):
                        dve.wait_ge(t_in[u], 16 * (k + 1))
                        since(dve, t_hi_done, n)
                        dve.tensor_scalar(t_up[:, :, 0:w].bitcast(I32), t_f[u][:, :, 0:w].bitcast(I32), HIGH, None, ALU.bitwise_and).then_inc(t_up_done, 1)
                        since(dve, h_done, U * (n - 1))
                        dve.wait_ge(t_up_done, n + 1)
                        dve.tensor_tensor(t_lo[u][:, :, 0:w], t_f[u][:, :, 0:w], t_up[:, :, 0:w], ALU.subtract).then_inc(t_lo_done, 1)

                    def body(n, u, k, w, after):
                        for b in range(U):
                            i, s = U * n + b, b % 4
                            if b % (2 * HE) == 0:
                                dve.wait_ge(c_in[b // (2 * HE)], 16 * (n + 1))
                            dve.wait_ge(g_done, i + 1)
                            dve.tensor_tensor(g_c[s % 2][:, 0:w], g_s[s][:, 0:w], cbc[b // (2 * HE)][:, b // 2 % HE, 0:w], ALU.mult).then_inc(g_c_done, 1)
                            dve.wait_ge(g_c_done, i + 1)
                            since(dve, g_hi_done, i - 1)
                            dve.tensor_scalar(g_up[s % 2][:, 0:w].bitcast(I32), g_c[s % 2][:, 0:w].bitcast(I32), HIGH, None, ALU.bitwise_and).then_inc(g_up_done, 1)
                            dve.wait_ge(g_up_done, i + 1)
                            since(dve, e_done, i - 3)
                            dve.tensor_tensor(g_lo[s][:, 0:w], g_c[s % 2][:, 0:w], g_up[s % 2][:, 0:w], ALU.subtract).then_inc(g_lo_done, 1)
                            if b == 8 and after:
                                split_t(n + 1, 1 - u, k + u, after)
                            if b == 12 and (not isinstance(n, int) or n > 0):
                                add(n - 1, CH)

                    def add(n, w):
                        dve.wait_ge(f_done, n + 1)
                        for h in range(-(-w // (2 * P))):
                            tiles = min(2, w // P - 2 * h)
                            xt = X[:, bass.ds(n * (CH // P) + 2 * h, tiles), :]
                            last = dve.tensor_tensor(xt, fps[h][:, 0:tiles, :], xt, ALU.add)
                        last.then_inc(x_done, 1)
                    split_t(0, 0, 0, CH)
                    chunks(dve, body)
                    add(FULL, LASTW)


def kernel(x, src, dst, edge_attr_4, edge_attr_8, node_vec1, L0_gnn_W_sc0, L0_gnn_W_sc1, L0_gnn_W_lin1_0,
           L0_gnn_W_lin1_1, L0_gnn_fc_w0, L0_gnn_fc_w1, L0_gnn_W_lin2_0, L0_gnn_W_lin2_1, L0_ffn_router_w,
           L0_ffn_w1, L0_ffn_b1, L0_ffn_w2, L0_ffn_b2):
    import concourse.bacc as bacc
    from concourse.bass_utils import run_bass_kernel_spmd

    def padded(a, rows, value=0):
        a = np.asarray(a)
        out = np.full((rows,) + a.shape[1:], value, a.dtype)
        out[:a.shape[0]] = a
        return out

    def by_tile(a):
        a = a.reshape((NG, SUBS, P, QS) + a.shape[1:])
        return np.moveaxis(a, 2, 1)

    dst_pad = padded(dst, EPAD, N - 1)
    dst_nat = padded(dst_pad, EPAD + GROUP, NPAD)
    starts = dst_nat[:EPAD + WIN:WIN]
    e8 = padded(edge_attr_8, EPAD).reshape(NG, 2, 2, P, QS, NB)
    arrays = {
        "x": padded(x, NPAD),
        "z": np.ascontiguousarray(padded(node_vec1, NPAD).reshape(NT, P).T),
        "src": np.ascontiguousarray(by_tile(padded(src, EPAD)).reshape(NG, P, GT)),
        "dst": np.ascontiguousarray(np.moveaxis(by_tile(dst_pad), 0, 1).reshape(P, NG * GT)),
        "dst_nat": dst_nat,
        "firsts": np.stack([starts[:-1].reshape(NG, SUBS), starts[1:].reshape(NG, SUBS)], axis=1),
        "sh": np.ascontiguousarray(by_tile(padded(edge_attr_4, EPAD)).reshape(NG, P, GT * 4)),
        "e8": np.ascontiguousarray(e8.transpose(0, 1, 2, 5, 4, 3).reshape(NG, 2, 2 * NB, WIN)),
        "w_sc0": L0_gnn_W_sc0, "w_sc1": L0_gnn_W_sc1, "w_l10": L0_gnn_W_lin1_0, "w_l11": L0_gnn_W_lin1_1,
        "fc0": L0_gnn_fc_w0, "fc1": L0_gnn_fc_w1, "w_l20": L0_gnn_W_lin2_0, "w_l21": L0_gnn_W_lin2_1,
        "router_t": np.ascontiguousarray(np.asarray(L0_ffn_router_w).T),
        "w1": L0_ffn_w1, "b1": np.asarray(L0_ffn_b1).reshape(NE, 2, P).transpose(2, 0, 1), "w2": L0_ffn_w2, "b2": L0_ffn_b2,
    }
    arrays = {k: np.ascontiguousarray(v) for k, v in arrays.items()}
    nc = bacc.Bacc("TRN2", target_bir_lowering=False, num_devices=1)
    aps = {k: nc.dram_tensor(f"in_{k}", a.shape, mybir.dt.from_np(a.dtype), kind="ExternalInput").ap() for k, a in arrays.items()}
    out = nc.dram_tensor("out_0", (NPAD, D), F32, kind="ExternalOutput").ap()
    gnn_moe(nc, **aps, out=out)
    r = run_bass_kernel_spmd(nc, [{f"in_{k}": a for k, a in arrays.items()}], core_ids=[0])
    return r.results[0]["out_0"][:N]
```

```python
from contextlib import ExitStack

import numpy as np

import concourse.bass as bass
from concourse import mybir

F32 = mybir.dt.float32
F32R = mybir.dt.float32r
I32 = mybir.dt.int32
U32 = mybir.dt.uint32
ALU = mybir.AluOpType
ACT = mybir.ActivationFunctionType
AX = mybir.AxisListType

P = 128
N, E = 6250, 200000
MUL, NB, RN = 64, 8, 64
D = 4 * MUL
Y = 2 * D
NT = -(-N // P)
NPAD = NT * P
SUBS, QS = 4, 4
WIN = QS * P
GROUP = SUBS * WIN
GT = SUBS * QS
NG = -(-E // GROUP)
EPAD = NG * GROUP
RANKS = P // SUBS
NE, TOPK = 8, 2
CH = 512
EPS = 1e-5
HIGH = -(1 << 12)
SKIP = 1.0e6

C_S = float(np.float32(np.sin(np.pi / 8.0)))
C_X = float(np.float32(np.cos(np.pi / 8.0)))
INV_M = 1.0 / np.sqrt(MUL)
OUT_SCALE = float(C_X / np.sqrt(2 * MUL) / np.sqrt(16.0) / np.sqrt(RN))
INV_SQRT3 = float(1.0 / np.sqrt(3.0))


def since(eng, sem, value):
    if not isinstance(value, int) or value > 0:
        eng.wait_ge(sem, value)


def in_turns(eng, count, slots, body, peeled=1):
    for t in range(peeled * slots):
        body(t, t % slots, t // slots)
    with eng.Fori(peeled, count // slots) as i:
        for slot in range(slots):
            body(slots * i + slot, slot, i)
    for t in range(count - count % slots, count):
        body(t, t % slots, count // slots)


class Chain:

    def __init__(self, eng, sem):
        self.eng, self.sem, self.count = eng, sem, 0

    def then(self, ins):
        self.count += 1
        ins.then_inc(self.sem, 1)
        self.eng.wait_ge(self.sem, self.count)


def gnn_moe(nc, x, z, src, dst, dst_nat, firsts, sh, e8, w_sc0, w_sc1, w_l10, w_l11, fc0, fc1, w_l20, w_l21,
            router_t, w1, b1, w2, b2, out):
    h_table = nc.dram_tensor("h_table", (NPAD, D), F32, kind="Internal").ap()
    y_sums = nc.dram_tensor("y_sums", (NPAD + RANKS, Y), F32, kind="Internal").ap()
    t_cols = nc.dram_tensor("t_cols", (2, P, NPAD), F32, kind="Internal").ap()
    comb_rows = nc.dram_tensor("comb_rows", (NE, NPAD), F32, kind="Internal").ap()

    with ExitStack() as whole:
        def sb(name, shape, dt=F32, ctx=whole):
            return ctx.enter_context(nc.sbuf_tensor(name, shape, dt))

        windows = ExitStack()
        X = sb("X", [P, NT, D])
        zcol = sb("zcol", [P, NT])
        ident = sb("ident", [P, P])
        ones = sb("ones", [P, P])
        mean = sb("mean", [P, NT])
        rstd = sb("rstd", [P, NT])
        eps_col = sb("eps_col", [P, 1])
        wl2 = sb("wl2", [P, 2, MUL])
        router_s = sb("router_s", [P, 2, NE])
        riota = sb("riota", [P, SUBS, RANKS], ctx=windows)
        neg_base = sb("neg_base", [P, NG, SUBS], ctx=windows)
        neg_ncol = sb("neg_ncol", [P, NG], ctx=windows)
        rank = sb("rank", [P, NG * GT], ctx=windows)
        dst_i = sb("dst_i", [P, NG * GT], I32, ctx=windows)
        bases = sb("bases", [1, NG, SUBS], I32, windows)
        flag = sb("flag", [1, 1], I32, windows)

        def stats_to_rstd(dve, st, tmp, chain, sqrt_in, sqrt_out):
            m1, q1, m2, q2 = st[:, :, 1], st[:, :, 2], st[:, :, 4], st[:, :, 5]
            chain.then(dve.tensor_tensor(mean[:, :], m1, m2, ALU.add))
            chain.then(dve.tensor_tensor(tmp[:, :], m1, m2, ALU.subtract))
            chain.then(dve.tensor_scalar(mean[:, :], mean[:, :], 0.5, None, ALU.mult))
            chain.then(dve.scalar_tensor_tensor(tmp[:, :], tmp[:, :], D / 4.0, tmp[:, :], ALU.mult, ALU.mult))
            chain.then(dve.tensor_tensor(tmp[:, :], tmp[:, :], q1, ALU.add))
            dve.tensor_tensor(tmp[:, :], tmp[:, :], q2, ALU.add).then_inc(sqrt_in, 1)
            dve.wait_ge(sqrt_out, 1)
            chain.then(dve.reciprocal(rstd[:, :], rstd[:, :]))

        with ExitStack() as c1:
            def s1(name, shape, dt=F32):
                return sb(name, shape, dt, c1)

            def sem(name):
                return c1.enter_context(nc.semaphore(name))

            CHUNKS, PER = 7, NT // 7
            st = s1("st", [P, NT, 6])
            tmp = s1("tmp", [P, NT])
            wlin = s1("wlin", [P, 2, 2 * P])
            xn = [s1(f"xn{u}", [P, 4, MUL]) for u in range(4)]
            xnT = [s1(f"xnT{u}", [P, 2 * P]) for u in range(4)]
            hrow = [s1(f"hrow{u}", [P, 2, P]) for u in range(4)]
            z_h = s1("z_h", [P, NT])
            z_s = s1("z_s", [P, NT])
            dst_a = s1("dst_a", [NG, GROUP + 1], I32)
            diff = s1("diff", [NG, GROUP])
            base_i = s1("base_i", [P, 2, SUBS], I32)
            base_f = s1("base_f", [P, 2, SUBS])
            bad = s1("bad", [P, 4])
            diag = s1("diag", [P, NG, SUBS])
            spread = s1("spread", [P, SUBS, RANKS])
            rcol = s1("rcol", [P, 1])
            bad_f = s1("bad_f", [1, 1])

            tps = [c1.enter_context(nc.psum_tensor(f"tps{u}", [P, 512], F32)) for u in range(2)]
            lin_ps, sc_ps = ([c1.enter_context(nc.psum_tensor(f"{name}{u}", [P, 512], F32)) for u in range(2)] for name in ("lin_ps", "sc_ps"))
            base_ps = c1.enter_context(nc.psum_tensor("base_ps", [P, 512], F32))
            col_ps = c1.enter_context(nc.psum_tensor("col_ps", [P, 512], F32))

            x_in = [sem(f"x_in{c}") for c in range(CHUNKS)]
            w_in, wl_in, z_in, dst_in = sem("w_in"), sem("wl_in"), sem("z_in"), sem("dst_in")
            w_zero, pool_const = sem("w_zero"), sem("pool_const")
            pool_step = sem("pool_step")
            dve_step, var_ready, std_ready = sem("dve_step"), sem("var_ready"), sem("std_ready")
            const_ready, z_ready = sem("const_ready"), sem("z_ready")
            xn_ready, tr_ready, xnT_ready, lin_ready = sem("xn_ready"), sem("tr_ready"), sem("xnT_ready"), sem("lin_ready")
            h_ready, x_done = sem("h_ready"), sem("x_done")
            h_out = [sem(f"h_out{u}") for u in range(4)]
            spread_ready, spread_ps, bad_ready = sem("spread_ready"), sem("spread_ps"), sem("bad_ready")

            with nc.Block() as block:
                @block.sync
                def _(sp):
                    sp.dma_start(dst_a[:, :], bass.AP(dst_nat.tensor, 0, [[GROUP, NG], [1, GROUP + 1]])).then_inc(dst_in, 16)
                    sp.dma_start(dst_i[:, :], dst).then_inc(dst_in, 16)
                    sp.dma_start(base_i[0:NG, :, :], firsts).then_inc(dst_in, 16)
                    sp.dma_start(bases[:, :, :], firsts[:, 0, :][None, :, :]).then_inc(dst_in, 16)

                    xt = x.rearrange("(t p) d -> p t d", p=P)
                    for c in range(CHUNKS):
                        sp.dma_start(X[:, c * PER:(c + 1) * PER, :], xt[:, c * PER:(c + 1) * PER, :]).then_inc(x_in[c], 16)
                    def store(t, u, _k):
                        sp.wait_ge(h_ready, t + 1)
                        sp.dma_start(h_table[bass.ds(t * P, P), :], hrow[u][:, :, :].rearrange("p a b -> p (a b)")).then_inc(h_out[u], 16)
                    in_turns(sp, NT, 4, store)
                    for u in range(4):
                        sp.wait_ge(h_out[u], 16 * len(range(u, NT, 4)))

                @block.gpsimd
                def _(pool):
                    chain = Chain(pool, pool_step)
                    pool.memset(wlin[:, :, :], 0.0).then_inc(w_zero, 1)
                    chain.then(pool.memset(ident[:, :], 0.0))
                    pool.memset(ones[:, :], 1.0)
                    chain.then(pool.affine_select(out=ident[:, :], in_=ident[:, :], compare_op=ALU.not_equal, fill=1.0,
                                                  base=0, pattern=[[-1, P]], channel_multiplier=1))
                    chain.then(pool.iota(riota[:, :, :], [[0, SUBS], [1, RANKS]], base=0, channel_multiplier=0,
                                         allow_small_or_imprecise_dtypes=True))
                    for j in range(SUBS):
                        chain.then(pool.iota(rcol[j * RANKS:(j + 1) * RANKS, :], [[1, 1]], base=0, channel_multiplier=1,
                                             allow_small_or_imprecise_dtypes=True))
                    pool.sem_inc(pool_const, 1)

                @block.scalar
                def _(act):
                    act.dma_start(zcol[:, :], z).then_inc(z_in, 16)
                    act.wait_ge(w_zero, 1)
                    for b, (top, bottom) in enumerate((((w_l10, w_sc0), (w_l11, w_sc1)), ((w_l11, w_sc1), (w_l11, w_sc1)))):
                        for half, ws in enumerate((top, bottom)):
                            for k, w in enumerate(ws):
                                lo = k * P + half * MUL
                                act.dma_start(wlin[half * MUL:(half + 1) * MUL, b, lo:lo + MUL], w).then_inc(w_in, 16)
                    act.dma_start(wl2[:, 0, :], w_l20).then_inc(wl_in, 16)
                    for h in range(2):
                        act.dma_start(wl2[(1 - h) * MUL:(2 - h) * MUL, 1, :], w_l21[h * MUL:(h + 1) * MUL, :]).then_inc(wl_in, 16)
                    act.dma_start(router_s[:, :, :], router_t.rearrange("(k p) e -> p k e", p=P)).then_inc(wl_in, 16)
                    act.wait_ge(wl_in, 64)
                    act.mul(wl2[0:MUL, 0, :], wl2[0:MUL, 0, :], OUT_SCALE)
                    act.mul(wl2[MUL:P, 0, :], wl2[MUL:P, 0, :], OUT_SCALE * INV_SQRT3)
                    act.mul(wl2[:, 1, :], wl2[:, 1, :], OUT_SCALE)
                    act.wait_ge(const_ready, 1)
                    act.wait_ge(var_ready, 1)
                    act.activation(rstd[:, :], tmp[:, :], ACT.Sqrt, bias=eps_col[:, 0:1], scale=1.0 / D).then_inc(std_ready, 1)

                    def h_of(t, u, k):
                        act.wait_ge(lin_ready, t + 1)
                        since(act, h_out[u], 16 * k)
                        act.activation(hrow[u][:, :, :], lin_ps[u % 2][:, 0:2 * P].rearrange("p (a b) -> p a b", a=2), ACT.Copy,
                                       scale=z_h[:, bass.ds(t, 1)]).then_inc(h_ready, 1)

                    def body(t, u, k):
                        act.wait_ge(tr_ready, t + 1)
                        since(act, lin_ready, t - 3)
                        act.copy(xnT[u][:, :], tps[u % 2][:, 0:2 * P]).then_inc(xnT_ready, 1)
                        if not isinstance(t, int) or t > 1:
                            h_of(t - 2, (u - 2) % 4, k - 1 if u < 2 else k)
                    act.wait_ge(z_ready, 2)
                    in_turns(act, NT, 4, body)
                    for t in (NT - 2, NT - 1):
                        h_of(t, t % 4, t // 4)

                @block.tensor
                def _(pe):
                    pe.wait_ge(pool_const, 1)
                    pe.wait_ge(spread_ready, 1)
                    pe.matmul(base_ps[:, 0:NG * SUBS], ones[:, :], diag[:, :, :], start=True, stop=True)
                    pe.matmul(col_ps[:, 0:NG], spread[:, :, :], ident[:, 0:NG], start=True, stop=True)
                    pe.wait_ge(bad_ready, 1)
                    pe.matmul(base_ps[0:1, 511:512], bad[:, 2:3], ones[:, 0:1], start=True, stop=True).then_inc(spread_ps, 1)

                    pe.wait_ge(w_in, 16 * 8)

                    def lin(t, u):
                        pe.wait_ge(xnT_ready, t + 1)
                        since(pe, h_ready, t - 1)
                        since(pe, x_done, t - 1)
                        for k, to in enumerate((lin_ps, sc_ps)):
                            for b in range(2):
                                last = pe.matmul(to[u % 2][:, b * P:(b + 1) * P], xnT[u][:, b * P:(b + 1) * P], wlin[:, b, k * P:(k + 1) * P],
                                                 start=True, stop=True)
                        last.then_inc(lin_ready, 1)

                    def body(t, u, k):
                        pe.wait_ge(xn_ready, t + 1)
                        since(pe, xnT_ready, t - 1)
                        for b in range(2):
                            last = pe.transpose(tps[u % 2][:, b * P:(b + 1) * P], xn[u][:, 2 * b:2 * b + 2, :], ident[:, :])
                        last.then_inc(tr_ready, 1)
                        if not isinstance(t, int) or t > 0:
                            lin(t - 1, (u - 1) % 4)
                    in_turns(pe, NT, 4, body)
                    lin(NT - 1, (NT - 1) % 4)

                @block.vector
                def _(dve):
                    chain = Chain(dve, dve_step)
                    dve.memset(eps_col[:, :], EPS).then_inc(const_ready, 1)
                    dve.wait_ge(z_in, 16)
                    dve.tensor_scalar(z_h[:, :], zcol[:, :], INV_M, None, ALU.mult).then_inc(z_ready, 1)
                    dve.tensor_scalar(z_s[:, :], zcol[:, :], INV_M * C_S, None, ALU.mult).then_inc(z_ready, 1)
                    chain.then(dve.memset(bad[:, :], 0.0))
                    dve.wait_ge(dst_in, 16 * 4)
                    chain.then(dve.memset(base_f[:, :, :], 0.0))
                    chain.then(dve.tensor_copy(base_f[0:NG, :, :], base_i[0:NG, :, :]))
                    chain.then(dve.memset(base_f[0:1, 0, 0:1], 0.0))
                    chain.then(dve.tensor_tensor(diff[:, :], dst_a[:, 1:GROUP + 1], dst_a[:, 0:GROUP], ALU.subtract))
                    chain.then(dve.tensor_reduce(bad[0:NG, 0:1], diff[:, :], AX.X, ALU.min))
                    chain.then(dve.tensor_tensor(diff[:, 0:SUBS], base_f[0:NG, 1, :], base_f[0:NG, 0, :], ALU.subtract))
                    chain.then(dve.tensor_reduce(bad[0:NG, 1:2], diff[:, 0:SUBS], AX.X, ALU.max))
                    chain.then(dve.tensor_scalar(bad[:, 0:1], bad[:, 0:1], 0.0, None, ALU.is_lt))
                    chain.then(dve.tensor_scalar(bad[:, 1:2], bad[:, 1:2], float(RANKS - 1), None, ALU.is_gt))
                    dve.tensor_tensor(bad[:, 2:3], bad[:, 0:1], bad[:, 1:2], ALU.add).then_inc(bad_ready, 1)
                    dve.wait_ge(pool_const, 1)
                    dve.tensor_tensor(diag[:, :, :], ident[:, 0:NG, None].to_broadcast((P, NG, SUBS)),
                                      base_f[:, 0:1, :].to_broadcast((P, NG, SUBS)), ALU.mult)
                    dve.tensor_copy(spread[:, :, :], base_f[:, 0, :, None].to_broadcast((P, SUBS, RANKS))).then_inc(spread_ready, 1)
                    dve.wait_ge(spread_ps, 1)
                    chain.then(dve.tensor_scalar(neg_base[:, :, :].rearrange("p g j -> p (g j)"), base_ps[:, 0:NG * SUBS], -1.0, None, ALU.mult))
                    chain.then(dve.tensor_scalar(neg_ncol[:, :], col_ps[:, 0:NG], rcol[:, 0:1], -1.0, ALU.add, ALU.mult))
                    chain.then(dve.tensor_tensor(rank[:, :].rearrange("p (w q) -> p w q", q=QS), dst_i[:, :].rearrange("p (w q) -> p w q", q=QS),
                                                 neg_base[:, :, :].rearrange("p g j -> p (g j)")[:, :, None].to_broadcast((P, NG * SUBS, QS)), ALU.add))
                    chain.then(dve.tensor_scalar(flag[:, :], base_ps[0:1, 511:512], 0.0, None, ALU.is_gt))

                    for c in range(CHUNKS):
                        dve.wait_ge(x_in[c], 16)
                        for t in range(c * PER, (c + 1) * PER):
                            last = dve.bn_stats(st[:, t, :], X[:, t, :])
                    chain.then(last)
                    stats_to_rstd(dve, st, tmp, chain, var_ready, std_ready)

                    def residual(t, u):
                        dve.wait_ge(lin_ready, t + 1)
                        xt = X[:, bass.ds(t, 1), :].rearrange("p a b -> p (a b)")
                        x0, x1 = xt[:, 0:MUL], xt[:, MUL:D].rearrange("p (v c) -> p c v", c=3)
                        s = sc_ps[u % 2][:, 0:D].rearrange("p (c v) -> p c v", c=4)
                        dve.scalar_tensor_tensor(x0, s[:, 0, :], z_s[:, bass.ds(t, 1)], x0, ALU.mult, ALU.add)
                        dve.scalar_tensor_tensor(x1, s[:, 1:4, :], z_s[:, bass.ds(t, 1)], x1,
                                                 ALU.mult, ALU.add).then_inc(x_done, 1)

                    def body(t, u, k):
                        since(dve, tr_ready, t - 3)
                        xt = X[:, bass.ds(t, 1), :].rearrange("p a b -> p (a b)")
                        m, r = mean[:, bass.ds(t, 1)], rstd[:, bass.ds(t, 1)]
                        dve.tensor_scalar(xn[u][:, 0, :], xt[:, 0:MUL], m, r, ALU.subtract, ALU.mult)
                        dve.tensor_scalar(xn[u][:, 1:4, :], xt[:, MUL:D].rearrange("p (v c) -> p c v", c=3), m, r,
                                          ALU.subtract, ALU.mult).then_inc(xn_ready, 1)
                        if not isinstance(t, int) or t > 2:
                            residual(t - 3, (u - 3) % 4)
                    in_turns(dve, NT, 4, body)
                    for t in (NT - 3, NT - 2, NT - 1):
                        residual(t, t % 4)

        with ExitStack() as c2:
            def s2(name, shape, dt=F32):
                return sb(name, shape, dt, c2)

            def sem(name):
                return c2.enter_context(nc.semaphore(name))

            fc0_s = s2("fc0_s", [P, P])
            fc1_s = s2("fc1_s", [P, 2, D])
            e8_s = [s2(f"e8_s{v}", [P, 2, WIN]) for v in range(2)]
            src_s = [s2(f"src_s{v}", [P, GT], I32) for v in range(2)]
            sh_s = [s2(f"sh_s{v}", [P, GT, 4]) for v in range(2)]
            hid = [[s2(f"hid{v}{h}", [P, WIN]) for h in range(2)] for v in range(2)]
            xs = [s2(f"xs{v}", [P, QS, SUBS, D]) for v in range(2)]
            mid = [s2(f"mid{k}", [P, SUBS, Y]) for k in range(4)]
            eq = s2("eq", [P, GT, RANKS])
            sel = [s2(f"sel{v}", [P, GT, 4, RANKS]) for v in range(2)]
            same = [s2(f"same{v}", [P, SUBS, RANKS]) for v in range(2)]
            carry = [s2(f"carry{v}", [P, RANKS]) for v in range(2)]
            part = [s2(f"part{v}", [P, Y]) for v in range(2)]
            total = [s2(f"total{v}", [P, Y]) for v in range(2)]
            row_s = [s2(f"row_s{v}", [P, 1], U32) for v in range(2)]
            before = s2("before", [P, P])
            first = s2("first", [P, 2])

            w_ps = [[c2.enter_context(nc.psum_tensor(f"w_ps{k}{h}", [P, 2, D], F32)) for h in range(2)] for k in range(2)]
            y_ps = [c2.enter_context(nc.psum_tensor(f"y_ps{v}", [P, Y], F32)) for v in range(2)]
            hid_ps = c2.enter_context(nc.psum_tensor("hid_ps", [P, WIN], F32))
            t_ps = c2.enter_context(nc.psum_tensor("t_ps", [P, Y], F32))

            pool_went_on, g_went_on = sem("pool_went_on"), sem("g_went_on")
            zero_done, fc_in, fc_zero, before_done = sem("zero_done"), sem("fc_in"), sem("fc_zero"), sem("before_done")
            e8_in = [sem(f"e8_in{v}") for v in range(2)]
            src_in = [sem(f"src_in{v}") for v in range(2)]
            sh_in = [sem(f"sh_in{v}") for v in range(2)]
            xs_in = [[sem(f"xs_in{v}{q}") for q in range(QS)] for v in range(2)]
            hid_done, hid_ready, w_done = sem("hid_done"), sem("hid_ready"), sem("w_done")
            eq_done, sel_done, mid_done, seg_done = sem("eq_done"), sem("sel_done"), sem("mid_done"), sem("seg_done")
            same_done, y_done, part_done, t_done, total_done = sem("same_done"), sem("y_done"), sem("part_done"), sem("t_done"), sem("total_done")
            y_out = sem("y_out")
            g_cleared, g_in, g_src, g_gather, g_old, g_put = sem("g_cleared"), sem("g_in"), sem("g_src"), sem("g_gather"), sem("g_old"), sem("g_put")
            g_hid, g_silu, g_w, g_sel, g_row, g_sum, g_new, g_dve, g_zero = (
                sem("g_hid"), sem("g_silu"), sem("g_w"), sem("g_sel"), sem("g_row"), sem("g_sum"), sem("g_new"), sem("g_dve"), sem("g_zero"))

            def products(dve, w, x_row, m):
                wk = w.rearrange("p (f k u) -> p f k u", f=2, k=2)
                mk = m.rearrange("p (b u) -> p b u", u=MUL)
                dve.tensor_tensor(mk[:, 0:8:7, :], wk[:, 0, :, :], x_row[:, None, 0:MUL].to_broadcast((P, 2, MUL)), ALU.mult)
                return dve.tensor_tensor(mk[:, 1:7, :].rearrange("p (k c) u -> p k c u", k=2), wk[:, 1, :, None, :].to_broadcast((P, 2, 3, MUL)),
                                         x_row[:, MUL:D].rearrange("p (c u) -> p c u", c=3)[:, None, :, :].to_broadcast((P, 2, 3, MUL)), ALU.mult)

            def segment(pe, acc, lhs, m, first):
                to = acc.rearrange("p (b u) -> p b u", u=MUL)
                yield lambda: pe.matmul(to[:, 0:8:2, :], lhs(0), m[:, 0:D], start=first, stop=False, skip_group_check=True)
                for c in range(1, 4):
                    moving = m[:, D:Y].rearrange("p (b u) -> p b u", u=MUL)[:, c - 1:4:4 - c, :]
                    yield lambda c=c, moving=moving: pe.matmul(to[:, 1:2 * c + 2:2 * c, :], lhs(c), moving, start=False, stop=False, skip_group_check=True)

            with nc.Block() as block:
                @block.sync
                def _(sp):
                    bad = sp.value_load(flag[0:1, 0:1], min_val=0, max_val=1)
                    with sp.If(bad == 0):
                        def load(g, v, k):
                            if k is not None:
                                for q in range(QS):
                                    sp.wait_ge(xs_in[v][q], 16 * SUBS * k)
                            sp.dma_start(src_s[v][:, :], src[bass.ds(g, 1), :, :].rearrange("g p t -> (g p) t")).then_inc(src_in[v], 16)
                            if k is None:
                                sp.wait_ge(fc_zero, 2 + v + 1)
                            else:
                                sp.wait_ge(hid_done, 2 * (g - 1))
                            sp.dma_start(e8_s[v][0:2 * NB, :, :], e8[bass.ds(g, 1), :, :, :].rearrange("g h f e -> f (g h) e")).then_inc(e8_in[v], 16)
                            if k is not None:
                                sp.wait_ge(sel_done, 4 * (g - 1))
                            sp.dma_start(sh_s[v][:, :, :].rearrange("p t c -> p (t c)"), sh[bass.ds(g, 1), :, :].rearrange("g p t -> (g p) t")).then_inc(sh_in[v], 16)

                        def store(g, v):
                            sp.wait_ge(total_done, g + 1)
                            for j in range(SUBS):
                                if isinstance(g, int) and g == 0 and j == 0:
                                    node = 0
                                else:
                                    node = sp.value_load(bases[0:1, bass.ds(g, 1), j:j + 1].rearrange("a g j -> a (g j)"), min_val=0, max_val=N - 1)
                                    sp.wait_ge(y_out, 16 * (SUBS * g + j))
                                sp.dma_start(y_sums[bass.ds(node, RANKS), :], total[v][j * RANKS:(j + 1) * RANKS, :]).then_inc(y_out, 16)
                        load(0, 0, None)
                        load(1, 1, None)
                        load(2, 0, 1)
                        load(3, 1, 1)
                        store(0, 0)
                        with sp.Fori(2, NG // 2) as i:
                            load(2 * i, 0, i)
                            store(2 * i - 3, 1)
                            load(2 * i + 1, 1, i)
                            store(2 * i - 2, 0)
                        for g in range(NG - 3, NG):
                            store(g, g % 2)
                        sp.wait_ge(y_out, 16 * SUBS * NG)
                    with sp.Else():
                        sp.wait_ge(g_zero, 1)
                        with sp.Fori(0, NT) as t:
                            sp.dma_start(y_sums[bass.ds(t * P, P), :], total[0][:, :]).then_inc(g_cleared, 16)
                        sp.dma_start(y_sums[NPAD:NPAD + RANKS, :], total[0][0:RANKS, :]).then_inc(g_cleared, 16)
                        sp.wait_ge(g_cleared, 16 * (NT + 1))
                        with sp.Fori(0, NG) as g:
                            for j in range(SUBS):
                                for q in range(QS):
                                    s = g * GT + j * QS + q
                                    sp.dma_start(e8_s[0][0:NB, 0, 0:P], e8[bass.ds(g, 1), j // 2, (j % 2) * NB:(j % 2 + 1) * NB, q * P:(q + 1) * P].rearrange("g f e -> (g f) e")).then_inc(g_in, 16)
                                    with nc.allow_non_contiguous_dma(reason="one index a partition"):
                                        sp.dma_start(src_s[0][:, 0:1], src[bass.ds(g, 1), :, j * QS + q:j * QS + q + 1].rearrange("g p t -> (g p) t")).then_inc(g_src, 16)
                                    sp.dma_start(sh_s[0][:, 0, :], sh[bass.ds(g, 1), :, (j * QS + q) * 4:(j * QS + q) * 4 + 4].rearrange("g p t -> (g p) t")).then_inc(g_src, 16)
                                    sp.wait_ge(g_put, 16 * (s + 1))
                                    sp.sem_inc(g_went_on, 1)

                @block.gpsimd
                def _(pool):
                    pool.affine_select(out=before[:, :], in_=ones[:, :], compare_op=ALU.is_gt, fill=0.0,
                                       base=0, pattern=[[-1, P]], channel_multiplier=1).then_inc(before_done, 1)
                    def hold(sem, value):
                        pool.wait_ge(sem, value)
                        pool.sem_inc(pool_went_on, 1)

                    bad = pool.value_load(flag[0:1, 0:1], min_val=0, max_val=1)
                    with pool.If(bad == 0):
                        def gather(g, v, k):
                            hold(src_in[v], 16 * (k + 1))
                            for q in range(QS):
                                if not isinstance(g, int) or g >= 2:
                                    hold(mid_done, 4 * (g - 2) + q + 1)
                                for j in range(SUBS):
                                    t = j * QS + q
                                    pool.indirect_dma_start(xs[v][:, q, j, :], None, h_table,
                                                            bass.IndirectOffsetOnAxis(ap=src_s[v][:, t:t + 1], axis=0)).then_inc(xs_in[v][q], 16)
                        gather(0, 0, 0)
                        gather(1, 1, 0)
                        with pool.Fori(1, NG // 2) as i:
                            gather(2 * i, 0, i)
                            gather(2 * i + 1, 1, i)
                    with pool.Else():
                        with pool.Fori(0, NG * GT) as s:
                            hold(g_src, 32 * (s + 1))
                            pool.indirect_dma_start(xs[0][:, 0, 0, :], None, h_table,
                                                    bass.IndirectOffsetOnAxis(ap=src_s[0][:, 0:1], axis=0)).then_inc(g_gather, 16)
                            hold(g_row, 2 * (s + 1))
                            hold(g_gather, 16 * (s + 1))
                            pool.indirect_dma_start(total[1][:, :], None, y_sums,
                                                    bass.IndirectOffsetOnAxis(ap=row_s[0][:, 0:1], axis=0)).then_inc(g_old, 16)
                            hold(g_new, s + 1)
                            pool.indirect_dma_start(y_sums, bass.IndirectOffsetOnAxis(ap=row_s[1][:, 0:1], axis=0), total[0][:, :], None,
                                                    bounds_check=NPAD - 1, oob_is_err=False).then_inc(g_put, 16)
                        pool.wait_ge(g_put, 16 * NG * GT)

                @block.scalar
                def _(act):
                    act.wait_ge(fc_zero, 2)
                    for h in range(2):
                        act.dma_start(fc0_s[h * NB:(h + 1) * NB, h * RN:(h + 1) * RN], fc0).then_inc(fc_in, 16)
                        act.dma_start(fc1_s[h * RN:(h + 1) * RN, h, :], fc1).then_inc(fc_in, 16)
                    bad = act.value_load(flag[0:1, 0:1], min_val=0, max_val=1)
                    with act.If(bad == 0):
                        def silu(g, v, h):
                            act.wait_ge(hid_done, 2 * g + h + 1)
                            since(act, w_done, 4 * (g - 1))
                            act.activation(hid[v][h][:, :], hid_ps[:, :], ACT.Silu, scale=float(1.0 / np.sqrt(NB))).then_inc(hid_ready, 1)

                        def take_part(g, v):
                            act.wait_ge(y_done, g + 1)
                            since(act, t_done, g - 1)
                            act.copy(part[v][:, :], y_ps[v][:, :]).then_inc(part_done, 1)

                        def take_total(g, v):
                            act.wait_ge(t_done, g + 1)
                            since(act, y_out, 16 * SUBS * (g - 1))
                            act.copy(total[v][:, :], t_ps[:, :]).then_inc(total_done, 1)

                        def body(g, v, k, last=False):
                            started = not isinstance(g, int) or g > 0
                            if started:
                                take_part(g - 1, 1 - v)
                            if not last:
                                silu(g + 1, 1 - v, 0)
                            if started:
                                take_total(g - 1, 1 - v)
                            if not last:
                                silu(g + 1, 1 - v, 1)
                        silu(0, 0, 0)
                        silu(0, 0, 1)
                        body(0, 0, 0)
                        body(1, 1, 0)
                        with act.Fori(1, NG // 2 - 1) as i:
                            body(2 * i, 0, i)
                            body(2 * i + 1, 1, i)
                        body(NG - 2, 0, NG // 2 - 1)
                        body(NG - 1, 1, NG // 2 - 1, last=True)
                        take_part(NG - 1, 1)
                        take_total(NG - 1, 1)
                    with act.Else():
                        with act.Fori(0, NG * GT) as s:
                            act.wait_ge(g_hid, s + 1)
                            act.activation(hid[0][0][:, 0:P], hid_ps[:, 0:P], ACT.Silu, scale=float(1.0 / np.sqrt(NB))).then_inc(g_silu, 1)

                @block.tensor
                def _(pe):
                    pe.wait_ge(fc_in, 16 * 4)
                    bad = pe.value_load(flag[0:1, 0:1], min_val=0, max_val=1)
                    with pe.If(bad == 0):
                        def first_layer(g, v, k, h):
                            pe.wait_ge(e8_in[v], 16 * (k + 1))
                            since(pe, hid_ready, 2 * g + h)
                            pe.matmul(hid_ps[:, :], fc0_s[:, :], e8_s[v][:, h, :], start=True, stop=True).then_inc(hid_done, 1)

                        def second_layer(g, v, q):
                            if q == 0:
                                pe.wait_ge(hid_ready, 2 * g + 2)
                            since(pe, mid_done, 4 * g + q - 1)
                            for h in range(2):
                                last = pe.matmul(w_ps[q % 2][h][:, :, :], hid[v][h][:, q * P:(q + 1) * P], fc1_s[:, :, :], start=True, stop=True)
                            last.then_inc(w_done, 1)

                        def sum_up(g, v, q):
                            pe.wait_ge(mid_done, 4 * g + q + 1)
                            pe.wait_ge(sel_done, 4 * g + q + 1)
                            if q == 0:
                                since(pe, part_done, g - 1)
                            parts = [list(segment(pe, y_ps[v][j * RANKS:(j + 1) * RANKS, :],
                                                  lambda c, t=j * QS + q: sel[v][:, t, c, :], mid[q][:, j, :], q == 0)) for j in range(SUBS)]
                            for c in range(4):
                                for j in range(SUBS):
                                    last = parts[j][c]()
                            last.then_inc(seg_done, 1)

                        def hand_over(g, v):
                            since(pe, part_done, g)
                            since(pe, same_done, g)
                            pe.matmul(y_ps[v][0:RANKS, :], carry[1 - v][:, :], part[1 - v][:, :], start=False, stop=True,
                                      skip_group_check=True).then_inc(y_done, 1)

                        def merge(g, v):
                            pe.wait_ge(part_done, g + 1)
                            pe.wait_ge(same_done, g + 1)
                            since(pe, total_done, g)
                            pe.matmul(t_ps[:, :], same[v][:, :, :], part[v][:, :], start=True, stop=True).then_inc(t_done, 1)

                        def body(g, v, k, last=False):
                            started = not isinstance(g, int) or g > 0
                            for q in range(QS):
                                second_layer(g, v, q)
                                if q > 0:
                                    sum_up(g, v, q - 1)
                                elif started:
                                    sum_up(g - 1, 1 - v, QS - 1)
                                    hand_over(g - 1, 1 - v)
                                if q == 2 and started:
                                    merge(g - 1, 1 - v)
                                if q in (1, 2) and not last:
                                    first_layer(g + 1, 1 - v, k + v, q - 1)
                        first_layer(0, 0, 0, 0)
                        first_layer(0, 0, 0, 1)
                        pe.wait_ge(zero_done, 1)
                        body(0, 0, 0)
                        body(1, 1, 0)
                        with pe.Fori(1, NG // 2 - 1) as i:
                            body(2 * i, 0, i)
                            body(2 * i + 1, 1, i)
                        body(NG - 2, 0, NG // 2 - 1)
                        body(NG - 1, 1, NG // 2 - 1, last=True)
                        sum_up(NG - 1, 1, QS - 1)
                        hand_over(NG - 1, 1)
                        merge(NG - 1, 1)
                    with pe.Else():
                        with pe.Fori(0, NG * GT) as s:
                            pe.wait_ge(g_in, 16 * (s + 1))
                            pe.matmul(hid_ps[:, 0:P], fc0_s[:, :], e8_s[0][:, 0, 0:P], start=True, stop=True).then_inc(g_hid, 1)
                            pe.wait_ge(g_silu, s + 1)
                            pe.matmul(w_ps[0][0][:, :, :], hid[0][0][:, 0:P], fc1_s[:, :, :], start=True, stop=True).then_inc(g_w, 1)
                            pe.wait_ge(g_sel, 3 * s + 1)
                            pe.transpose(t_ps[:, 0:P], same[0][:, :, :], ident[:, :]).then_inc(g_sum, 1)
                            pe.wait_ge(g_sel, 3 * s + 3)
                            parts = list(segment(pe, y_ps[0][:, :], lambda c: sel[0][:, c, :, :].rearrange("p a r -> p (a r)"), mid[0][:, 0, :], True))
                            for p in parts:
                                last = p()
                            last.then_inc(g_sum, 1)

                @block.vector
                def _(dve):
                    dve.memset(fc0_s[:, :], 0.0).then_inc(fc_zero, 1)
                    dve.memset(fc1_s[:, :, :], 0.0).then_inc(fc_zero, 1)
                    dve.memset(e8_s[0][:, :, :], 0.0).then_inc(fc_zero, 1)
                    dve.memset(e8_s[1][:, :, :], 0.0).then_inc(fc_zero, 1)
                    dve.memset(part[1][:, :], 0.0)
                    dve.memset(carry[0][:, :], 0.0)
                    dve.memset(carry[1][:, :], 0.0).then_inc(zero_done, 1)
                    dve.memset(total[0][:, :], 0.0).then_inc(g_zero, 1)
                    dve.wait_ge(zero_done, 1)
                    bad = dve.value_load(flag[0:1, 0:1], min_val=0, max_val=1)
                    with dve.If(bad == 0):
                        def compare(g):
                            since(dve, sel_done, 4 * g)
                            dve.tensor_tensor(eq[:, :, :], riota[:, 0:1, :].to_broadcast((P, GT, RANKS)),
                                              rank[:, bass.ds(g * GT, GT)][:, :, None].to_broadcast((P, GT, RANKS)), ALU.is_equal).then_inc(eq_done, 1)

                        def select(g, v, k, q):
                            if q == 0:
                                dve.wait_ge(sh_in[v], 16 * (k + 1))
                                dve.wait_ge(eq_done, g + 1)
                            since(dve, seg_done, 4 * (g - 2) + q + 1)
                            dve.tensor_tensor(sel[v][:, q::QS, :, :], eq[:, q::QS, None, :].to_broadcast((P, SUBS, 4, RANKS)),
                                              sh_s[v][:, q::QS, :, None].to_broadcast((P, SUBS, 4, RANKS)), ALU.mult).then_inc(sel_done, 1)

                        def share(g, v, last):
                            since(dve, t_done, g - 1)
                            since(dve, y_done, g)
                            if not last:
                                dve.scalar_tensor_tensor(carry[v][:, 0:1], neg_ncol[:, bass.ds(g, 1)], 0.0, neg_base[:, bass.ds(g + 1, 1), 0:1].rearrange("p g j -> p (g j)"),
                                                         ALU.add, ALU.is_equal)
                            dve.scalar_tensor_tensor(same[v][:, :, :], riota[:, :, :], neg_ncol[:, bass.ds(g, 1)],
                                                     neg_base[:, bass.ds(g, 1), :].rearrange("p g j -> p (g j)")[:, :, None].to_broadcast((P, SUBS, RANKS)),
                                                     ALU.add, ALU.is_equal).then_inc(same_done, 1)

                        def messages(g, v, k, q):
                            dve.wait_ge(w_done, 4 * g + q + 1)
                            dve.wait_ge(xs_in[v][q], 16 * SUBS * (k + 1))
                            since(dve, seg_done, 4 * (g - 1) + q + 1)
                            for j in range(SUBS):
                                last = products(dve, w_ps[q % 2][j // 2][:, j % 2, :], xs[v][:, q, j, :], mid[q][:, j, :])
                            last.then_inc(mid_done, 1)

                        def body(g, v, k, last=False):
                            compare(g)
                            for q in range(QS):
                                select(g, v, k, q)
                                messages(g, v, k, q)
                                if q == 1:
                                    share(g, v, last)
                        body(0, 0, 0)
                        body(1, 1, 0)
                        with dve.Fori(1, NG // 2 - 1) as i:
                            body(2 * i, 0, i)
                            body(2 * i + 1, 1, i)
                        body(NG - 2, 0, NG // 2 - 1)
                        body(NG - 1, 1, NG // 2 - 1, last=True)
                    with dve.Else():
                        with dve.Fori(0, NG * GT) as s:
                            def step(n, ins):
                                ins.then_inc(g_dve, 1)
                                dve.wait_ge(g_dve, s * 4 + n)
                            dst_col = rank[:, bass.ds(s, 1)]
                            dve.wait_ge(g_src, 32 * (s + 1))
                            step(1, dve.tensor_scalar(dst_col, dst_i[:, bass.ds(s, 1)], 1.0, None, ALU.mult))
                            dve.tensor_scalar(same[0][:, :, :].rearrange("p j r -> p (j r)"), dst_col.to_broadcast((P, P)), 1.0, None, ALU.mult).then_inc(g_sel, 1)
                            dve.tensor_scalar(row_s[0][:, :], dst_col, 1.0, None, ALU.mult).then_inc(g_row, 1)
                            dve.wait_ge(g_sum, 2 * s + 1)
                            eqm = eq[:, 0:4, :].rearrange("p a b -> p (a b)")
                            step(2, dve.tensor_scalar(eqm, t_ps[:, 0:P], dst_col, None, ALU.is_equal))
                            for c in range(4):
                                last = dve.tensor_scalar(sel[0][:, c, :, :], eq[:, 0:4, :], sh_s[0][:, 0, c:c + 1], None, ALU.mult)
                            last.then_inc(g_sel, 1)
                            dve.wait_ge(before_done, 1)
                            step(3, dve.scalar_tensor_tensor(eq[:, 4:8, :].rearrange("p a b -> p (a b)"), eqm, 1.0, before[:, :], ALU.mult, ALU.mult,
                                                             accum_out=first[:, 0:1]))
                            step(4, dve.tensor_scalar(first[:, 1:2], first[:, 0:1], SKIP, dst_col, ALU.mult, ALU.add))
                            dve.tensor_copy(row_s[1][:, :], first[:, 1:2]).then_inc(g_row, 1)
                            dve.wait_ge(g_w, s + 1)
                            dve.wait_ge(g_gather, 16 * (s + 1))
                            products(dve, w_ps[0][0][:, 0, :], xs[0][:, 0, 0, :], mid[0][:, 0, :]).then_inc(g_sel, 1)
                            dve.wait_ge(g_sum, 2 * s + 2)
                            dve.wait_ge(g_old, 16 * (s + 1))
                            dve.tensor_tensor(total[0][:, :], total[1][:, :], y_ps[0][:, :], ALU.add).then_inc(g_new, 1)

        windows.close()

        with ExitStack() as c3:
            def s3(name, shape, dt=F32):
                return sb(name, shape, dt, c3)

            def sem(name):
                return c3.enter_context(nc.semaphore(name))

            w_hi = s3("w_hi", [P, NE, 2, 2, D], F32R)
            w_lo = s3("w_lo", [P, NE, 2, 2, D], F32R)
            b1_s = s3("b1_s", [P, NE, 2])
            b2_s = s3("b2_s", [P, D])
            b2_r = s3("b2_r", [P, D], F32R)
            eighth = s3("eighth", [P, NE])

            t_f = [s3(f"t_f{u}", [P, 2, CH]) for u in range(2)]
            t_up = s3("t_up", [P, 2, CH])
            t_hi = [s3(f"t_hi{u}", [P, 2, CH], F32R) for u in range(2)]
            t_lo = [s3(f"t_lo{u}", [P, 2, CH], F32R) for u in range(2)]

            t_in = [sem(f"t_in{u}") for u in range(2)]
            t_up_done, t_hi_done, t_lo_done = sem("t_up_done"), sem("t_hi_done"), sem("t_lo_done")
            y_in = [sem(f"y_in{u}") for u in range(4)]
            stage_in = [sem(f"stage_in{u}") for u in range(2)]
            t_out = [sem(f"t_out{u}") for u in range(4)]
            split_step, b2_in = sem("split_step"), sem("b2_in")
            w_in, b2_zero = sem("w_in3"), sem("b2_zero")
            tr_done, tr_taken, o_done, o_taken = sem("tr_done"), sem("tr_taken"), sem("o_done"), sem("o_taken")
            bn_done = sem("bn_done")
            var_ready, std_ready, dve_step, pool_ready = sem("var_ready3"), sem("std_ready3"), sem("dve_step3"), sem("pool_ready")
            tn_done, tp_done, tp_taken, logit_done = sem("tn_done"), sem("tp_done"), sem("tp_taken"), sem("logit_done")
            shifted, powered, comb_done, combT_ps, combT_done, comb_out = (
                sem("shifted"), sem("powered"), sem("comb_done"), sem("combT_ps"), sem("combT_done"), sem("comb_out"))
            U = 2 * NE

            def split_t(dve, n, u, k, w, h_done):
                dve.wait_ge(t_in[u], 16 * (k + 1))
                since(dve, t_hi_done, n)
                dve.tensor_scalar(t_up[:, :, 0:w].bitcast(I32), t_f[u][:, :, 0:w].bitcast(I32), HIGH, None, ALU.bitwise_and).then_inc(t_up_done, 1)
                since(dve, h_done, U * (n - 1))
                dve.wait_ge(t_up_done, n + 1)
                dve.tensor_tensor(t_lo[u][:, :, 0:w], t_f[u][:, :, 0:w], t_up[:, :, 0:w], ALU.subtract).then_inc(t_lo_done, 1)

            def upper_t(act, n, u, w, h_done):
                act.wait_ge(t_up_done, n + 1)
                since(act, h_done, U * (n - 1))
                act.copy(t_hi[u][:, :, 0:w], t_up[:, :, 0:w]).then_inc(t_hi_done, 1)

            with nc.Block() as block, ExitStack() as c:
                yb = [sb(f"yb{u}", [P, Y], F32, c) for u in range(4)]
                yT = [sb(f"yT{u}", [P, Y], F32, c) for u in range(4)]
                tn = [sb(f"tn{u}", [P, D], F32, c) for u in range(4)]
                tnT = [sb(f"tnT{u}", [P, 2, P], F32, c) for u in range(4)]
                st = sb("st3", [P, 4, 6], F32, c)
                mean2, gap, var4, std4, mean4, rstd4 = (sb(name, [P, 4], F32, c) for name in ("mean2", "gap", "var4", "std4", "mean4", "rstd4"))
                prob, rest, comb = (sb(name, [P, NT, NE], F32, c) for name in ("prob", "rest", "comb"))
                pick = [sb(f"pick{n}", [P, NT, NE], F32, c) for n in range(2)]
                top = [sb(f"top{n}", [P, NT], F32, c) for n in range(3)]
                stage = [sb(f"stage{u}", [P, 2, 2, D], F32, c) for u in range(2)]
                scaled, scaled_less = (sb(name, [P, 2, 2, D], F32, c) for name in ("scaled", "scaled_less"))
                combT = sb("combT", [P, -(-NT // 16), P], F32, c)
                tps = [c.enter_context(nc.psum_tensor(f"ytp{u}", [P, Y], F32)) for u in range(2)]
                ops = [c.enter_context(nc.psum_tensor(f"yop{u}", [P, 512], F32)) for u in range(2)]
                nps = [c.enter_context(nc.psum_tensor(f"ntp{u}", [P, 512], F32)) for u in range(2)]
                logit_ps = c.enter_context(nc.psum_tensor("logit_ps", [P, 512], F32))
                ct_ps = c.enter_context(nc.psum_tensor("ct_ps", [P, 512], F32))
                LW = -(-NT // 16)
                TURNS = -(-NT // 4)
                NORM, TURN = 6, 10
                PEELED = 4

                def known(t, lag):
                    return not isinstance(t, int) or t >= lag

                @block.sync
                def _(sp):
                    sp.dma_start(b1_s[:, :, :], b1).then_inc(w_in, 16)
                    sp.wait_ge(b2_zero, 1)
                    for part in range(3):
                        sp.dma_start(b2_s[32 * part:32 * part + NE, :], b2).then_inc(b2_in, 16)

                    def keep(t, u):
                        sp.wait_ge(tp_taken, t + 1)
                        sp.dma_start(t_cols.rearrange("k p n -> p k n")[:, :, bass.ds(t * P, P)], tnT[u][:, :, :]).then_inc(t_out[u], 16)

                    def load(t, u, k):
                        since(sp, tr_done, t - 3)
                        sp.dma_start(yb[u][:, :], y_sums[bass.ds(t * P, P), :]).then_inc(y_in[u], 16)
                        if known(t, TURN + 4):
                            keep(t - TURN - 4, (u - 2) % 4)
                    in_turns(sp, NT, 4, load, PEELED)
                    for t in range(NT - TURN - 4, NT):
                        keep(t, t % 4)
                    for u in range(4):
                        sp.wait_ge(t_out[u], 16 * len(range(u, NT, 4)))
                    sp.dma_start(t_f[0][:, :, :], t_cols.rearrange("k p n -> p k n")[:, :, 0:CH]).then_inc(t_in[0], 16)
                    sp.wait_ge(combT_done, 1)
                    for b in range(LW):
                        tiles = min(16, NT - 16 * b)
                        sp.dma_start(comb_rows.rearrange("e (t p) -> t e p", p=P)[16 * b:16 * b + tiles, :, :], combT[0:tiles * NE, b, :]).then_inc(comb_out, 16)
                    sp.wait_ge(comb_out, 16 * LW)
                    sp.wait_ge(w_in, 16)

                @block.gpsimd
                def _(pool):
                    pool.iota(eighth[:, :], [[-1, NE]], base=NE, channel_multiplier=0, allow_small_or_imprecise_dtypes=True).then_inc(pool_ready, 1)

                    chain = Chain(pool, split_step)

                    def load(e):
                        for which, w in enumerate((w1, w2)):
                            pool.dma_start(stage[e % 2][:, which, :, :], w[e].rearrange("(k p) n -> p k n", p=P)).then_inc(stage_in[e % 2], 16)
                    load(0)
                    load(1)
                    def split(whole, hi, times, less):
                        chain.then(pool.tensor_scalar(times, whole, float(1 - HIGH), None, ALU.mult))
                        chain.then(pool.tensor_tensor(less, times, whole, ALU.subtract))
                        chain.then(pool.tensor_tensor(hi, times, less, ALU.subtract))

                    def flat(a):
                        return a.rearrange("p w k n -> p (w k n)")
                    for e in range(NE):
                        pool.wait_ge(stage_in[e % 2], 32 * (e // 2 + 1))
                        whole, hi = flat(stage[e % 2][:, :, :, :]), flat(w_hi[:, e, :, :, :])
                        split(whole, hi, flat(scaled[:, :, :, :]), flat(scaled_less[:, :, :, :]))
                        chain.then(pool.tensor_tensor(flat(w_lo[:, e, :, :, :]), whole, hi.bitcast(F32), ALU.subtract))
                        if e + 2 < NE:
                            load(e + 2)
                    pool.wait_ge(b2_in, 48)
                    split(b2_s[:, :], b2_r[:, :], scaled[:, 0, 0, :], scaled_less[:, 0, 0, :])
                    chain.then(pool.tensor_tensor(b2_r[64:96, :], b2_s[64:96, :], b2_r[64:96, :].bitcast(F32), ALU.subtract))

                @block.scalar
                def _(act):
                    def keep(t, u, k):
                        act.wait_ge(tp_done, t + 1)
                        since(act, t_out[u], 16 * k)
                        since(act, logit_done, t - 3)
                        act.copy(tnT[u][:, :, :], nps[u % 2][:, 0:D].rearrange("p (k n) -> p k n", k=2)).then_inc(tp_taken, 1)

                    def std(turn):
                        act.wait_ge(var_ready, turn + 1)
                        act.activation(std4[:, :], var4[:, :], ACT.Sqrt, bias=eps_col[:, 0:1], scale=1.0 / D).then_inc(std_ready, 1)

                    def take(t, u, k):
                        act.wait_ge(tr_done, t + 1)
                        since(act, o_done, t - 3)
                        act.copy(yT[u][:, :], tps[u % 2][:, :]).then_inc(tr_taken, 1)
                        if u == 3 and known(t, 4):
                            std(k - 1)
                        if known(t, TURN):
                            keep(t - TURN, (u - 2) % 4, k - 3 if u < 2 else k - 2)
                    in_turns(act, NT, 4, take, PEELED)
                    std(TURNS - 2)
                    for t in range(NT - TURN, NT):
                        keep(t, t % 4, t // 4)
                        if t == NT - TURN + 1:
                            std(TURNS - 1)
                    act.wait_ge(shifted, 1)
                    act.activation(prob[:, :, :], rest[:, :, :], ACT.Exp).then_inc(powered, 1)
                    act.wait_ge(combT_ps, 1)
                    act.copy(combT[:, :, :], ct_ps[:, 0:LW * P].rearrange("p (b n) -> p b n", b=LW)).then_inc(combT_done, 1)
                    upper_t(act, 0, 0, CH, None)

                @block.tensor
                def _(pe):
                    def lin2(t, u):
                        pe.wait_ge(tr_taken, t + 1)
                        since(pe, o_taken, t - 1)
                        pe.matmul(ops[u % 2][:, 0:MUL], yT[u][:, 0:P], wl2[:, 0, :], start=True, stop=True)
                        for c in range(3):
                            last = pe.matmul(ops[u % 2][:, MUL + c:D:3], yT[u][:, (c + 1) * P:(c + 2) * P], wl2[:, 1, :], start=True, stop=True)
                        last.then_inc(o_done, 1)

                    def turn(t, u, k):
                        pe.wait_ge(y_in[u], 16 * (k + 1))
                        since(pe, tr_taken, t - 1)
                        for b in range(4):
                            last = pe.transpose(tps[u % 2][:, b * P:(b + 1) * P], yb[u][:, b * P:(b + 1) * P], ident[:, :])
                        last.then_inc(tr_done, 1)
                        if known(t, 2):
                            lin2(t - 2, (u - 2) % 4)
                        if known(t, TURN):
                            turn_back(t - TURN, (u - 2) % 4)
                        if known(t, TURN + 2):
                            logits(t - TURN - 2, u)

                    def turn_back(t, u):
                        pe.wait_ge(tn_done, t + 1)
                        since(pe, tp_taken, t - 1)
                        for b in range(2):
                            last = pe.transpose(nps[u % 2][:, b * P:(b + 1) * P], tn[u][:, b * P:(b + 1) * P], ident[:, :])
                        last.then_inc(tp_done, 1)

                    def logits(t, u):
                        pe.wait_ge(tp_taken, t + 1)
                        for k in range(2):
                            last = pe.matmul(logit_ps[:, bass.ds(t * NE, NE)], tnT[u][:, k, :], router_s[:, k, :], start=(k == 0), stop=(k == 1))
                        last.then_inc(logit_done, 1)
                    in_turns(pe, NT, 4, turn, PEELED)
                    for t in (NT - 2, NT - 1):
                        lin2(t, t % 4)
                    for t in range(NT - TURN, NT):
                        turn_back(t, t % 4)
                        logits(t - 2, (t - 2) % 4)
                    for t in (NT - 2, NT - 1):
                        logits(t, t % 4)

                    pe.wait_ge(comb_done, 1)
                    for b in range(LW):
                        tiles = min(16, NT - 16 * b)
                        last = pe.transpose(ct_ps[0:tiles * NE, b * P:(b + 1) * P], comb[:, 16 * b:16 * b + tiles, :], ident[:, :])
                    last.then_inc(combT_ps, 1)

                @block.vector
                def _(dve):
                    chain = Chain(dve, dve_step)
                    dve.memset(b2_s[:, :], 0.0).then_inc(b2_zero, 1)
                    dve.memset(ct_ps[:, :], 0.0)

                    dve.memset(st[:, :, :], 0.0)
                    chain.then(dve.memset(rest[:, :, :], 0.0))
                    FIRST, STEPS = chain.count, 6

                    def row(t):
                        return X[:, bass.ds(t, 1), :].rearrange("p a b -> p (a b)")

                    def norm(t, u):
                        since(dve, tp_done, t - 3)
                        dve.tensor_scalar(tn[u][:, :], row(t), mean4[:, u:u + 1], rstd4[:, u:u + 1], ALU.subtract, ALU.mult).then_inc(tn_done, 1)

                    def keep(t, u):
                        dve.wait_ge(tn_done, t + 1)
                        dve.tensor_tensor(row(t), row(t), tn[u][:, :], ALU.add)

                    m1, q1, m2, q2 = st[:, :, 1], st[:, :, 2], st[:, :, 4], st[:, :, 5]

                    def done(turn, n):
                        dve.wait_ge(dve_step, FIRST + STEPS * turn + n)

                    def sums(turn, tiles):
                        dve.wait_ge(bn_done, tiles)
                        dve.tensor_tensor(mean2[:, :], m1, m2, ALU.add).then_inc(dve_step, 1)
                        dve.tensor_tensor(gap[:, :], m1, m2, ALU.subtract).then_inc(dve_step, 1)
                        dve.tensor_tensor(var4[:, :], q1, q2, ALU.add).then_inc(dve_step, 1)

                    def square(turn):
                        done(turn, 3)
                        dve.scalar_tensor_tensor(gap[:, :], gap[:, :], D / 4.0, gap[:, :], ALU.mult, ALU.mult).then_inc(dve_step, 1)

                    def variance(turn):
                        done(turn, 4)
                        dve.tensor_tensor(var4[:, :], var4[:, :], gap[:, :], ALU.add).then_inc(var_ready, 1)

                    def finish(turn):
                        dve.wait_ge(std_ready, turn + 1)
                        dve.reciprocal(rstd4[:, :], std4[:, :]).then_inc(dve_step, 1)
                        dve.tensor_scalar(mean4[:, :], mean2[:, :], 0.5, None, ALU.mult).then_inc(dve_step, 1)

                    def residual(t, u, k):
                        dve.wait_ge(o_done, t + 1)
                        dve.scalar_tensor_tensor(row(t), ops[u % 2][:, 0:D], zcol[:, bass.ds(t, 1)], row(t), ALU.mult, ALU.add).then_inc(o_taken, 1)
                        if u == 0 and known(t, 4):
                            square(k - 1)
                        if u == 2 and known(t, NORM):
                            done(k - 1, 6)
                        if known(t, NORM):
                            norm(t - NORM, (u - 2) % 4)
                        if u == 0 and known(t, 4):
                            variance(k - 1)
                        dve.wait_ge(o_taken, t + 1)
                        if known(t, NORM):
                            keep(t - NORM, (u - 2) % 4)
                        dve.bn_stats(st[:, u, :], row(t)).then_inc(bn_done, 1)
                        if u == 1 and known(t, 4):
                            finish(k - 1)
                        if u == 3:
                            sums(k, t + 1)
                    in_turns(dve, NT, 4, residual, PEELED)
                    norm(NT - NORM, (NT - NORM) % 4)
                    keep(NT - NORM, (NT - NORM) % 4)
                    finish(TURNS - 2)
                    done(TURNS - 2, 6)
                    sums(TURNS - 1, NT)
                    square(TURNS - 1)
                    variance(TURNS - 1)
                    for t in range(NT - NORM + 1, NT - 1):
                        norm(t, t % 4)
                        keep(t, t % 4)
                    finish(TURNS - 1)
                    done(TURNS - 1, 6)
                    norm(NT - 1, (NT - 1) % 4)
                    keep(NT - 1, (NT - 1) % 4)
                    chain.count += STEPS * TURNS

                    def wide(col):
                        return col[:, :, None].to_broadcast((P, NT, NE))
                    index = eighth[:, None, :].to_broadcast((P, NT, NE))
                    dve.wait_ge(logit_done, NT)
                    logit = logit_ps[:, 0:NT * NE].rearrange("p (t e) -> p t e", e=NE)
                    chain.then(dve.tensor_reduce(top[0][:, :], logit, AX.X, ALU.max))
                    dve.tensor_tensor(rest[:, :, :], logit, wide(top[0]), ALU.subtract).then_inc(shifted, 1)
                    dve.wait_ge(powered, 1)
                    chain.then(dve.tensor_reduce(top[0][:, :], prob[:, :, :], AX.X, ALU.add))
                    chain.then(dve.reciprocal(top[0][:, :], top[0][:, :]))
                    chain.then(dve.tensor_tensor(prob[:, :, :], prob[:, :, :], wide(top[0]), ALU.mult))
                    dve.wait_ge(pool_ready, 1)
                    left = prob
                    for n in range(TOPK):
                        chain.then(dve.tensor_reduce(top[n][:, :], left[:, :, :], AX.X, ALU.max))
                        chain.then(dve.tensor_tensor(pick[n][:, :, :], left[:, :, :], wide(top[n]), ALU.is_equal))
                        chain.then(dve.tensor_tensor(pick[n][:, :, :], pick[n][:, :, :], index, ALU.mult))
                        chain.then(dve.tensor_reduce(top[2][:, :], pick[n][:, :, :], AX.X, ALU.max))
                        chain.then(dve.tensor_tensor(pick[n][:, :, :], index, wide(top[2]), ALU.is_equal))
                        if n == 0:
                            chain.then(dve.scalar_tensor_tensor(rest[:, :, :].rearrange("p t e -> p (t e)"), pick[0][:, :, :].rearrange("p t e -> p (t e)"), -2.0,
                                                                prob[:, :, :].rearrange("p t e -> p (t e)"), ALU.mult, ALU.add))
                            left = rest
                    chain.then(dve.tensor_tensor(top[2][:, :], top[0][:, :], top[1][:, :], ALU.add))
                    chain.then(dve.tensor_scalar(top[2][:, :], top[2][:, :], 1e-12, None, ALU.max))
                    chain.then(dve.reciprocal(top[2][:, :], top[2][:, :]))
                    chain.then(dve.tensor_tensor(pick[0][:, :, :], pick[0][:, :, :], pick[1][:, :, :], ALU.add))
                    chain.then(dve.tensor_tensor(pick[0][:, :, :], pick[0][:, :, :], prob[:, :, :], ALU.mult))
                    dve.tensor_tensor(comb[:, :, :], pick[0][:, :, :], wide(top[2]), ALU.mult).then_inc(comb_done, 1)
                    split_t(dve, 0, 0, 0, CH, None)

            with nc.Block() as block, ExitStack() as c:
                HE = NE // 2
                cbc = [sb(f"cbc{h}", [P, HE, CH], F32, c) for h in range(2)]
                crow = [sb(f"crow{u}", [P, CH], F32, c) for u in range(2)]
                crow_up = sb("crow_up", [P, CH], F32, c)
                crow_r = [sb(f"crow_r{u}", [P, CH], F32R, c) for u in range(2)]
                g_s = [sb(f"g_s{m}", [P, CH], F32, c) for m in range(4)]
                g_c = [sb(f"g_c{m}", [P, CH], F32, c) for m in range(2)]
                g_up = [sb(f"g_up{m}", [P, CH], F32, c) for m in range(2)]
                g_hi = [sb(f"g_hi{m}", [P, CH], F32R, c) for m in range(4)]
                g_lo = [sb(f"g_lo{m}", [P, CH], F32R, c) for m in range(4)]
                oT = sb("oT", [P, 2, CH], F32, c)
                hps = [c.enter_context(nc.psum_tensor(f"hps{m}", [P, CH], F32)) for m in range(4)]
                acc = [c.enter_context(nc.psum_tensor(f"acc{d}", [P, CH], F32)) for d in range(2)]
                fps = [c.enter_context(nc.psum_tensor(f"fps{n}", [P, 2, D], F32)) for n in range(2)]

                def esem(name):
                    return c.enter_context(nc.semaphore(name))
                crow_in = [esem(f"crow_in{u}") for u in range(2)]
                c_in = [esem(f"c_in{h}") for h in range(2)]
                crow_up_done, crow_done = esem("crow_up_done"), esem("crow_done")
                crow_zero, h_done, g_done, e_done = esem("crow_zero"), esem("h_done"), esem("g_done"), esem("e_done")
                g_c_done, g_up_done, g_hi_done, g_lo_done = esem("g_c_done"), esem("g_up_done"), esem("g_hi_done"), esem("g_lo_done")
                oT_done, f_done, x_done = esem("oT_done"), esem("f_done"), esem("x_done3")
                out_in = esem("out_in")
                CT = CH // P
                SHORT = -NT % CT
                FULL = (NT - SHORT * (CT - 1)) // CT
                LAST = FULL + SHORT - 1

                def tiles_of(n):
                    return 0 if n > LAST else CT if not isinstance(n, int) or n < FULL else CT - 1

                def first_tile(n):
                    return n * CT if not isinstance(n, int) or n < FULL else FULL * CT + (n - FULL) * (CT - 1)

                def chunks(eng, body):
                    body(0, 0, 0, CT, 0, CT)
                    body(1, 1, 0, CT, CT, CT)
                    with eng.Fori(1, FULL // 2 - 1) as i:
                        body(2 * i, 0, i, CT, CT, CT)
                        body(2 * i + 1, 1, i, CT, CT, CT)
                    for n in range(FULL - 2, FULL + SHORT):
                        body(n, n % 2, n // 2, tiles_of(n), tiles_of(n - 1), tiles_of(n + 1))

                @block.sync
                def _(sp):
                    sp.wait_ge(crow_zero, 1)

                    def load(n, u, k, tiles, _before, _after):
                        at, w = first_tile(n) * P, tiles * P
                        since(sp, t_lo_done, n - 1)
                        if not isinstance(n, int) or n > 0:
                            sp.dma_start(t_f[u][:, :, 0:w], t_cols.rearrange("k p n -> p k n")[:, :, bass.ds(at, w)]).then_inc(t_in[u], 16)
                        since(sp, crow_done, n - 1)
                        for part in range(3):
                            sp.dma_start(crow[u][32 * part:32 * part + NE, 0:w], comb_rows[:, bass.ds(at, w)]).then_inc(crow_in[u], 16)
                        for h in range(2):
                            since(sp, g_c_done, U * (n - 1) + (h + 1) * 2 * HE)
                            sp.dma_start(cbc[h][:, :, 0:w], comb_rows[h * HE:(h + 1) * HE, bass.ds(at, w)][None, :, :].to_broadcast((P, HE, w))).then_inc(c_in[h], 16)
                    chunks(sp, load)

                @block.gpsimd
                def _(pool):
                    def store(n, u, k, tiles, _before, _after):
                        pool.wait_ge(x_done, n + 1)
                        pool.dma_start(out.rearrange("(t p) d -> p t d", p=P)[:, bass.ds(first_tile(n), tiles), :],
                                       X[:, bass.ds(first_tile(n), tiles), :]).then_inc(out_in, 16)
                    chunks(pool, store)
                    pool.wait_ge(out_in, 16 * (LAST + 1))

                @block.scalar
                def _(act):
                    def upper_g(i, s, w):
                        act.wait_ge(g_up_done, i + 1)
                        since(act, e_done, i - 3)
                        act.copy(g_hi[s][:, 0:w], g_up[s % 2][:, 0:w]).then_inc(g_hi_done, 1)

                    def body(n, u, k, tiles, before, after):
                        w = tiles * P
                        for b in range(U):
                            i, s = U * n + b, b % 4
                            act.wait_ge(h_done, i + 1)
                            since(act, g_c_done, i - 3)
                            act.activation(g_s[s][:, 0:w], hps[s][:, 0:w], ACT.Gelu, bias=b1_s[:, b // 2, b % 2:b % 2 + 1]).then_inc(g_done, 1)
                            if b >= 2:
                                upper_g(i - 2, (b - 2) % 4, w)
                            elif before:
                                upper_g(i - 2, (b - 2) % 4, before * P)
                            if b == 3 and before:
                                take(n - 1, before * P)
                            if b == 9 and after:
                                upper_t(act, n + 1, 1 - u, after * P, h_done)

                    def take(n, w):
                        act.wait_ge(e_done, U * (n + 1))
                        since(act, f_done, n)
                        for d in range(2):
                            last = act.copy(oT[:, d, 0:w], acc[d][:, 0:w])
                        last.then_inc(oT_done, 1)
                    chunks(act, body)
                    for b in (U - 2, U - 1):
                        upper_g(U * LAST + b, b % 4, tiles_of(LAST) * P)
                    take(LAST, tiles_of(LAST) * P)

                @block.tensor
                def _(pe):
                    def split_product(to, w_part, hi, lo, first, last):
                        pe.matmul(to, w_part(w_hi), hi, start=first, stop=False)
                        pe.matmul(to, w_part(w_hi), lo, start=False, stop=False)
                        return pe.matmul(to, w_part(w_lo), hi, start=False, stop=last)

                    def up(n, u, w, e):
                        if e == 0:
                            pe.wait_ge(t_hi_done, n + 1)
                            pe.wait_ge(t_lo_done, n + 1)
                        for m in range(2):
                            i = U * n + 2 * e + m
                            s = (2 * e + m) % 4
                            since(pe, g_done, i - 3)
                            for kk in range(2):
                                last = split_product(hps[s][:, 0:w], lambda part, kk=kk, m=m: part[:, e, 0, kk, m * P:(m + 1) * P],
                                                     t_hi[u][:, kk, 0:w], t_lo[u][:, kk, 0:w], kk == 0, kk == 1)
                            last.then_inc(h_done, 1)

                    def down(n, u, w, e):
                        if e == 0:
                            pe.wait_ge(crow_done, n + 1)
                            since(pe, oT_done, n)
                            for d in range(2):
                                pe.matmul(acc[d][:, 0:w], b2_r[:, d * P:(d + 1) * P], crow_r[u][:, 0:w], start=True, stop=False)
                        for m in range(2):
                            i = U * n + 2 * e + m
                            s = (2 * e + m) % 4
                            pe.wait_ge(g_lo_done, i + 1)
                            pe.wait_ge(g_hi_done, i + 1)
                            for d in range(2):
                                last = split_product(acc[d][:, 0:w], lambda part, d=d, m=m: part[:, e, 1, m, d * P:(d + 1) * P],
                                                     g_hi[s][:, 0:w], g_lo[s][:, 0:w], False, e == NE - 1 and m == 1)
                            last.then_inc(e_done, 1)

                    def finish(n, w):
                        pe.wait_ge(oT_done, n + 1)
                        since(pe, x_done, n)
                        for t in range(w // P):
                            for d in range(2):
                                last = pe.transpose(fps[t // 2][:, t % 2, d * P:(d + 1) * P], oT[:, d, t * P:(t + 1) * P], ident[:, :])
                        last.then_inc(f_done, 1)

                    def body(n, u, k, tiles, before, _after):
                        for e in range(NE):
                            up(n, u, tiles * P, e)
                            if e >= 2:
                                down(n, u, tiles * P, e - 2)
                            elif before:
                                down(n - 1, 1 - u, before * P, NE - 2 + e)
                            if e == 5 and before:
                                finish(n - 1, before * P)
                    chunks(pe, body)
                    for e in (NE - 2, NE - 1):
                        down(LAST, LAST % 2, tiles_of(LAST) * P, e)
                    finish(LAST, tiles_of(LAST) * P)

                @block.vector
                def _(dve):
                    for u in range(2):
                        last = dve.memset(crow[u][:, :], 0.0)
                    last.then_inc(crow_zero, 1)

                    def split_crow(n, u, k, w):
                        dve.wait_ge(crow_in[u], 48 * (k + 1))
                        dve.tensor_scalar(crow_up[:, 0:w].bitcast(I32), crow[u][:, 0:w].bitcast(I32), HIGH, None, ALU.bitwise_and).then_inc(crow_up_done, 1)
                        dve.wait_ge(crow_up_done, 2 * n + 1)
                        since(dve, e_done, U * (n - 2) + 1)
                        dve.tensor_copy(crow_r[u][:, 0:w], crow_up[:, 0:w]).then_inc(crow_up_done, 1)
                        dve.wait_ge(crow_up_done, 2 * n + 2)
                        dve.tensor_tensor(crow_r[u][32:64, 0:w], crow[u][32:64, 0:w], crow_up[32:64, 0:w], ALU.subtract).then_inc(crow_done, 1)

                    def body(n, u, k, tiles, before, after):
                        w = tiles * P
                        for b in range(U):
                            i, s = U * n + b, b % 4
                            if b % (2 * HE) == 0:
                                dve.wait_ge(c_in[b // (2 * HE)], 16 * (n + 1))
                            dve.wait_ge(g_done, i + 1)
                            dve.tensor_tensor(g_c[s % 2][:, 0:w], g_s[s][:, 0:w], cbc[b // (2 * HE)][:, b // 2 % HE, 0:w], ALU.mult).then_inc(g_c_done, 1)
                            dve.wait_ge(g_c_done, i + 1)
                            since(dve, g_hi_done, i - 1)
                            dve.tensor_scalar(g_up[s % 2][:, 0:w].bitcast(I32), g_c[s % 2][:, 0:w].bitcast(I32), HIGH, None, ALU.bitwise_and).then_inc(g_up_done, 1)
                            dve.wait_ge(g_up_done, i + 1)
                            since(dve, e_done, i - 3)
                            dve.tensor_tensor(g_lo[s][:, 0:w], g_c[s % 2][:, 0:w], g_up[s % 2][:, 0:w], ALU.subtract).then_inc(g_lo_done, 1)
                            if b == 6 and after:
                                split_crow(n + 1, 1 - u, k + u, after * P)
                            if b == 8 and after:
                                split_t(dve, n + 1, 1 - u, k + u, after * P, h_done)
                            if b == 13 and before:
                                add(n - 1, before)

                    def add(n, tiles):
                        dve.wait_ge(f_done, n + 1)
                        for h in range(-(-tiles // 2)):
                            some = min(2, tiles - 2 * h)
                            xt = X[:, bass.ds(first_tile(n) + 2 * h, some), :]
                            last = dve.tensor_tensor(xt, fps[h][:, 0:some, :], xt, ALU.add)
                        last.then_inc(x_done, 1)
                    split_crow(0, 0, 0, CH)
                    chunks(dve, body)
                    add(LAST, tiles_of(LAST))


def kernel(x, src, dst, edge_attr_4, edge_attr_8, node_vec1, L0_gnn_W_sc0, L0_gnn_W_sc1, L0_gnn_W_lin1_0,
           L0_gnn_W_lin1_1, L0_gnn_fc_w0, L0_gnn_fc_w1, L0_gnn_W_lin2_0, L0_gnn_W_lin2_1, L0_ffn_router_w,
           L0_ffn_w1, L0_ffn_b1, L0_ffn_w2, L0_ffn_b2):
    import concourse.bacc as bacc
    from concourse.bass_utils import run_bass_kernel_spmd

    def padded(a, rows, value=0):
        a = np.asarray(a)
        out = np.full((rows,) + a.shape[1:], value, a.dtype)
        out[:a.shape[0]] = a
        return out

    def by_tile(a):
        a = a.reshape((NG, SUBS, P, QS) + a.shape[1:])
        return np.moveaxis(a, 2, 1)

    dst_pad = padded(dst, EPAD, N - 1)
    dst_nat = padded(dst_pad, EPAD + GROUP, NPAD)
    starts = dst_nat[:EPAD + WIN:WIN]
    e8 = padded(edge_attr_8, EPAD).reshape(NG, 2, 2, P, QS, NB)
    arrays = {
        "x": padded(x, NPAD),
        "z": np.ascontiguousarray(padded(node_vec1, NPAD).reshape(NT, P).T),
        "src": np.ascontiguousarray(by_tile(padded(src, EPAD)).reshape(NG, P, GT)),
        "dst": np.ascontiguousarray(np.moveaxis(by_tile(dst_pad), 0, 1).reshape(P, NG * GT)),
        "dst_nat": dst_nat,
        "firsts": np.stack([starts[:-1].reshape(NG, SUBS), starts[1:].reshape(NG, SUBS)], axis=1),
        "sh": np.ascontiguousarray(by_tile(padded(edge_attr_4, EPAD)).reshape(NG, P, GT * 4)),
        "e8": np.ascontiguousarray(e8.transpose(0, 1, 2, 5, 4, 3).reshape(NG, 2, 2 * NB, WIN)),
        "w_sc0": L0_gnn_W_sc0, "w_sc1": L0_gnn_W_sc1, "w_l10": L0_gnn_W_lin1_0, "w_l11": L0_gnn_W_lin1_1,
        "fc0": L0_gnn_fc_w0, "fc1": L0_gnn_fc_w1, "w_l20": L0_gnn_W_lin2_0, "w_l21": L0_gnn_W_lin2_1,
        "router_t": np.ascontiguousarray(np.asarray(L0_ffn_router_w).T),
        "w1": L0_ffn_w1, "b1": np.asarray(L0_ffn_b1).reshape(NE, 2, P).transpose(2, 0, 1), "w2": L0_ffn_w2, "b2": L0_ffn_b2,
    }
    arrays = {k: np.ascontiguousarray(v) for k, v in arrays.items()}
    nc = bacc.Bacc("TRN2", target_bir_lowering=False, num_devices=1)
    aps = {k: nc.dram_tensor(f"in_{k}", a.shape, mybir.dt.from_np(a.dtype), kind="ExternalInput").ap() for k, a in arrays.items()}
    out = nc.dram_tensor("out_0", (NPAD, D), F32, kind="ExternalOutput").ap()
    gnn_moe(nc, **aps, out=out)
    r = run_bass_kernel_spmd(nc, [{f"in_{k}": a for k, a in arrays.items()}], core_ids=[0])
    return r.results[0]["out_0"][:N]
```
